# Optimizing a Trainium2 kernel written in Bass

```python
import numpy as np
import jax
import jax.numpy as jnp

def _softmax(x, axis=-1):
    return jax.nn.softmax(x, axis=axis)

def _gelu(x):
    return jax.nn.gelu(x, approximate=True)

def _silu(x):
    return jax.nn.silu(x)

def _sigmoid(x):
    return jax.nn.sigmoid(x)

def _layernorm(x, axis=-1, eps=1e-05):
    m = jnp.mean(x, axis=axis, keepdims=True)
    v = jnp.var(x, axis=axis, keepdims=True)
    return (x - m) / jnp.sqrt(v + eps)

def _scatter_add(tgt, idx, src, axis=0):
    return tgt.at[idx].add(src)

def _segment_sum(src, seg, n):
    return jax.ops.segment_sum(src, seg, n)
kernel_name = 'mk_xattn_ffn_d2_seqx_r8_930df3'

def setup_inputs(seed: int=0):
    np.random.seed(seed)
    _w = jnp.asarray

    def _rec_inputs():
        import jax
        import jax.numpy as jnp
        _rk = jax.random.key(seed)
        x = 7.22e-05 + 1 * jax.random.normal(jax.random.fold_in(_rk, 1), (4, 256, 256), jnp.float32)
        _lenS = 256 - jax.random.randint(jax.random.fold_in(_rk, 7), (4,), 0, max(1, 256 // 4) + 1, jnp.int32)
        _lenS2 = 256 - jax.random.randint(jax.random.fold_in(_rk, 8), (4,), 0, max(1, 256 // 4) + 1, jnp.int32)
        _ctx_2048P = jax.random.normal(jax.random.fold_in(_rk, 11), (4, 16, 256), jnp.float32)
        _ctx_2048c = jax.random.dirichlet(jax.random.fold_in(_rk, 511), 0.3 * jnp.ones((16,), jnp.float32), (4, 256))
        _ctx_2048t = jnp.einsum('bsk,bkd->bsd', _ctx_2048c, _ctx_2048P)
        _ctx_2048t = _ctx_2048t * jax.lax.rsqrt(jnp.mean(jnp.square(_ctx_2048t)) + 1e-12) * 0.953939
        ctx_2048 = 4.13588e-05 + 0.999923 * (_ctx_2048t + 0.3 * jax.random.normal(jax.random.fold_in(_rk, 611), (4, 256, 256), jnp.float32))
        return (x, ctx_2048)
    x, ctx_2048 = _rec_inputs()

    def _L0_xattn_setup():
        import math
        import jax, jax.numpy as jnp
        import numpy as np
        HEADS = 16
        MASKED_BIAS = -10000.0

        def _mha(q, k, v):
            B, Sq, D = q.shape
            Sk = k.shape[-2]
            hd = D // HEADS
            qh = q.reshape(B, Sq, HEADS, hd).transpose(0, 2, 1, 3)
            kh = k.reshape(B, Sk, HEADS, hd).transpose(0, 2, 1, 3)
            vh = v.reshape(B, Sk, HEADS, hd).transpose(0, 2, 1, 3)
            scores = jnp.einsum('bhqd,bhkd->bhqk', qh, kh) / math.sqrt(hd)
            qi = jnp.arange(Sq)[:, None] + (Sk - Sq)
            ki = jnp.arange(Sk)[None, :]
            causal = ki <= qi
            scores = jnp.where(causal[None, None], scores, jnp.asarray(MASKED_BIAS, scores.dtype))
            attn = jax.nn.softmax(scores, axis=-1)
            out = jnp.einsum('bhqk,bhkd->bhqd', attn, vh)
            return out.transpose(0, 2, 1, 3).reshape(B, Sq, D)
        key = jax.random.key(seed)
        kq, kk, kv = jax.random.split(key, 3)
        B, S, D = (4, 128, 256)
        q = jax.random.normal(kq, (B, S, D), dtype=jnp.float32)
        k = jax.random.normal(kk, (B, S, D), dtype=jnp.float32)
        v = jax.random.normal(kv, (B, S, D), dtype=jnp.float32)
        return {'q': q, 'k': k, 'v': v}
    _L0_xattn_all = _L0_xattn_setup()
    _L0_xattn_in = {k: v for k, v in _L0_xattn_all.items() if k in ()}
    del _L0_xattn_all

    def _L0_ffn_setup():
        import jax, jax.numpy as jnp
        import numpy as np
        B, S, HID = (2, 256, 256)
        NUM_HEADS = 16
        HEAD_DIM = HID // NUM_HEADS
        NUM_EXPERTS = 8
        TOP_K = 2
        INTER = 512
        EPS = 1e-05

        def _rmsnorm(x, w, eps=EPS):
            return x * jax.lax.rsqrt(jnp.mean(x * x, axis=-1, keepdims=True) + eps) * w

        def _moe(x_flat, Wr, Wg, Wu, Wd):
            T = x_flat.shape[0]
            logits = x_flat @ Wr.T
            top_logits, top_idx = jax.lax.top_k(logits, TOP_K)
            probs = jax.nn.softmax(top_logits, axis=-1)
            cw = jnp.zeros((T, NUM_EXPERTS), x_flat.dtype)
            cw = cw.at[jnp.arange(T)[:, None], top_idx].add(probs)
            hg = jnp.einsum('eih,th->eti', Wg, x_flat)
            hu = jnp.einsum('eih,th->eti', Wu, x_flat)
            y = jnp.einsum('ehi,eti->eth', Wd, jax.nn.silu(hg) * hu)
            return jnp.einsum('eth,te->th', y, cw)
        key = jax.random.key(seed)
        ks = jax.random.split(key, 12)
        sd_h = 1.0 / np.sqrt(HID)
        sd_i = 1.0 / np.sqrt(INTER)
        return {'x': jax.random.normal(ks[0], (B, S, HID), jnp.float32), 'Wq': jax.random.normal(ks[1], (HID, HID), jnp.float32) * sd_h, 'Wk': jax.random.normal(ks[2], (HID, HID), jnp.float32) * sd_h, 'Wv': jax.random.normal(ks[3], (HID, HID), jnp.float32) * sd_h, 'Wo': jax.random.normal(ks[4], (HID, HID), jnp.float32) * sd_h, 'w_ln1': jnp.ones((HID,), jnp.float32), 'w_ln2': jnp.ones((HID,), jnp.float32), 'Wr': jax.random.normal(ks[5], (NUM_EXPERTS, HID), jnp.float32) * sd_h, 'Wg': jax.random.normal(ks[6], (NUM_EXPERTS, INTER, HID), jnp.float32) * sd_h, 'Wu': jax.random.normal(ks[7], (NUM_EXPERTS, INTER, HID), jnp.float32) * sd_h, 'Wd': jax.random.normal(ks[8], (NUM_EXPERTS, HID, INTER), jnp.float32) * sd_i}
    _L0_ffn_all = _L0_ffn_setup()
    _L0_ffn_in = {k: v for k, v in _L0_ffn_all.items() if k in ('Wq', 'Wk', 'Wv', 'Wo', 'w_ln1', 'w_ln2', 'Wr', 'Wg', 'Wu', 'Wd')}
    del _L0_ffn_all

    def _L1_xattn_setup():
        import jax, jax.numpy as jnp
        import numpy as np
        B_DIM, T_DIM, C_DIM = (16, 128, 256)

        def _wkv(w, u, k, v):
            Bn, Tn, Cn = k.shape
            NEG_INF = jnp.float32(-1e+38)

            def step(carry, kv_t):
                p, q, o = carry
                kt, vt = kv_t
                no = jnp.maximum(o, u + kt)
                A = jnp.exp(o - no)
                E = jnp.exp(u + kt - no)
                y = (A * p + E * vt) / (A * q + E)
                no2 = jnp.maximum(w + o, kt)
                A2 = jnp.exp(w + o - no2)
                E2 = jnp.exp(kt - no2)
                return ((A2 * p + E2 * vt, A2 * q + E2, no2), y)
            init = (jnp.zeros((Bn, Cn), k.dtype), jnp.zeros((Bn, Cn), k.dtype), jnp.full((Bn, Cn), NEG_INF, k.dtype))
            kT = jnp.moveaxis(k, 1, 0)
            vT = jnp.moveaxis(v, 1, 0)
            _, yT = jax.lax.scan(step, init, (kT, vT))
            return jnp.moveaxis(yT, 0, 1)
        key = jax.random.key(seed)
        k1, k2, k3, k4 = jax.random.split(key, 4)
        w = -jnp.exp(jax.random.normal(k1, (C_DIM,), jnp.float32))
        u = jax.random.normal(k2, (C_DIM,), jnp.float32)
        k = jax.random.normal(k3, (B_DIM, T_DIM, C_DIM), jnp.float32)
        v = jax.random.normal(k4, (B_DIM, T_DIM, C_DIM), jnp.float32)
        return {'B': B_DIM, 'T': T_DIM, 'C': C_DIM, 'w': w, 'u': u, 'k': k, 'v': v}
    _L1_xattn_all = _L1_xattn_setup()
    _L1_xattn_in = {k: v for k, v in _L1_xattn_all.items() if k in ('w', 'u')}
    del _L1_xattn_all

    def _L1_ffn_setup():
        import jax, jax.numpy as jnp
        import numpy as np
        TOP_K = 2
        NUM_EXPERTS = 8
        ROUTE_SCALE = 1.0
        key = jax.random.key(seed)
        ks = jax.random.split(key, 8)
        bs, slen, dim, hidden, E = (4, 128, 256, 128, NUM_EXPERTS)
        s = 0.02
        return {'x': jax.random.normal(ks[0], (bs, slen, dim), jnp.float32), 'gate_w': jax.random.normal(ks[1], (E, dim), jnp.float32) * s, 'w1': jax.random.normal(ks[2], (E, hidden, dim), jnp.float32) * s, 'w2': jax.random.normal(ks[3], (E, dim, hidden), jnp.float32) * s, 'w3': jax.random.normal(ks[4], (E, hidden, dim), jnp.float32) * s, 'ws1': jax.random.normal(ks[5], (hidden, dim), jnp.float32) * s, 'ws2': jax.random.normal(ks[6], (dim, hidden), jnp.float32) * s, 'ws3': jax.random.normal(ks[7], (hidden, dim), jnp.float32) * s}
    _L1_ffn_all = _L1_ffn_setup()
    _L1_ffn_in = {k: v for k, v in _L1_ffn_all.items() if k in ('gate_w', 'w1', 'w2', 'w3', 'ws1', 'ws2', 'ws3')}
    del _L1_ffn_all
    return {'x': x, 'ctx_2048': ctx_2048, 'L0_ffn_Wq': _L0_ffn_in['Wq'], 'L0_ffn_Wk': _L0_ffn_in['Wk'], 'L0_ffn_Wv': _L0_ffn_in['Wv'], 'L0_ffn_Wo': _L0_ffn_in['Wo'], 'L0_ffn_w_ln1': _L0_ffn_in['w_ln1'], 'L0_ffn_w_ln2': _L0_ffn_in['w_ln2'], 'L0_ffn_Wr': _L0_ffn_in['Wr'], 'L0_ffn_Wg': _L0_ffn_in['Wg'], 'L0_ffn_Wu': _L0_ffn_in['Wu'], 'L0_ffn_Wd': _L0_ffn_in['Wd'], 'L1_xattn_w': _L1_xattn_in['w'], 'L1_xattn_u': _L1_xattn_in['u'], 'L1_ffn_gate_w': _L1_ffn_in['gate_w'], 'L1_ffn_w1': _L1_ffn_in['w1'], 'L1_ffn_w2': _L1_ffn_in['w2'], 'L1_ffn_w3': _L1_ffn_in['w3'], 'L1_ffn_ws1': _L1_ffn_in['ws1'], 'L1_ffn_ws2': _L1_ffn_in['ws2'], 'L1_ffn_ws3': _L1_ffn_in['ws3']}

def reference(x, ctx_2048, L0_ffn_Wq, L0_ffn_Wk, L0_ffn_Wv, L0_ffn_Wo, L0_ffn_w_ln1, L0_ffn_w_ln2, L0_ffn_Wr, L0_ffn_Wg, L0_ffn_Wu, L0_ffn_Wd, L1_xattn_w, L1_xattn_u, L1_ffn_gate_w, L1_ffn_w1, L1_ffn_w2, L1_ffn_w3, L1_ffn_ws1, L1_ffn_ws2, L1_ffn_ws3):
    import jax
    import jax.numpy as jnp

    def _L0_xattn_ref(q, k, v):
        import math
        import jax, jax.numpy as jnp
        import numpy as np
        HEADS = 16
        MASKED_BIAS = -10000.0

        def _mha(q, k, v):
            B, Sq, D = q.shape
            Sk = k.shape[-2]
            hd = D // HEADS
            qh = q.reshape(B, Sq, HEADS, hd).transpose(0, 2, 1, 3)
            kh = k.reshape(B, Sk, HEADS, hd).transpose(0, 2, 1, 3)
            vh = v.reshape(B, Sk, HEADS, hd).transpose(0, 2, 1, 3)
            scores = jnp.einsum('bhqd,bhkd->bhqk', qh, kh) / math.sqrt(hd)
            qi = jnp.arange(Sq)[:, None] + (Sk - Sq)
            ki = jnp.arange(Sk)[None, :]
            causal = ki <= qi
            scores = jnp.where(causal[None, None], scores, jnp.asarray(MASKED_BIAS, scores.dtype))
            attn = jax.nn.softmax(scores, axis=-1)
            out = jnp.einsum('bhqk,bhkd->bhqd', attn, vh)
            return out.transpose(0, 2, 1, 3).reshape(B, Sq, D)
        return _mha(q, k, v)

    def _L0_ffn_ref(x, Wq, Wk, Wv, Wo, w_ln1, w_ln2, Wr, Wg, Wu, Wd):
        import jax, jax.numpy as jnp
        import numpy as np
        B, S, HID = (2, 256, 256)
        NUM_HEADS = 16
        HEAD_DIM = HID // NUM_HEADS
        NUM_EXPERTS = 8
        TOP_K = 2
        INTER = 512
        EPS = 1e-05

        def _rmsnorm(x, w, eps=EPS):
            return x * jax.lax.rsqrt(jnp.mean(x * x, axis=-1, keepdims=True) + eps) * w

        def _moe(x_flat, Wr, Wg, Wu, Wd):
            T = x_flat.shape[0]
            logits = x_flat @ Wr.T
            top_logits, top_idx = jax.lax.top_k(logits, TOP_K)
            probs = jax.nn.softmax(top_logits, axis=-1)
            cw = jnp.zeros((T, NUM_EXPERTS), x_flat.dtype)
            cw = cw.at[jnp.arange(T)[:, None], top_idx].add(probs)
            hg = jnp.einsum('eih,th->eti', Wg, x_flat)
            hu = jnp.einsum('eih,th->eti', Wu, x_flat)
            y = jnp.einsum('ehi,eti->eth', Wd, jax.nn.silu(hg) * hu)
            return jnp.einsum('eth,te->th', y, cw)
        b, s, hid = x.shape
        residual = x
        xn = _rmsnorm(x, w_ln1)
        q = (xn @ Wq.T).reshape(b, s, NUM_HEADS, HEAD_DIM)
        k = (xn @ Wk.T).reshape(b, s, NUM_HEADS, HEAD_DIM)
        v = (xn @ Wv.T).reshape(b, s, NUM_HEADS, HEAD_DIM)
        scale = 1.0 / np.sqrt(HEAD_DIM)
        attn = jnp.einsum('bqhd,bkhd->bhqk', q, k) * scale
        causal = jnp.tril(jnp.ones((s, s), bool))
        attn = jnp.where(causal[None, None], attn, -jnp.inf)
        attn = jax.nn.softmax(attn, axis=-1)
        h = jnp.einsum('bhqk,bkhd->bqhd', attn, v).reshape(b, s, hid)
        x = residual + h @ Wo.T
        residual = x
        xn = _rmsnorm(x, w_ln2)
        moe_out = _moe(xn.reshape(-1, hid), Wr, Wg, Wu, Wd).reshape(b, s, hid)
        return residual + moe_out

    def _L1_xattn_ref(B, T, C, w, u, k, v):
        import jax, jax.numpy as jnp
        import numpy as np
        B_DIM, T_DIM, C_DIM = (16, 128, 256)

        def _wkv(w, u, k, v):
            Bn, Tn, Cn = k.shape
            NEG_INF = jnp.float32(-1e+38)

            def step(carry, kv_t):
                p, q, o = carry
                kt, vt = kv_t
                no = jnp.maximum(o, u + kt)
                A = jnp.exp(o - no)
                E = jnp.exp(u + kt - no)
                y = (A * p + E * vt) / (A * q + E)
                no2 = jnp.maximum(w + o, kt)
                A2 = jnp.exp(w + o - no2)
                E2 = jnp.exp(kt - no2)
                return ((A2 * p + E2 * vt, A2 * q + E2, no2), y)
            init = (jnp.zeros((Bn, Cn), k.dtype), jnp.zeros((Bn, Cn), k.dtype), jnp.full((Bn, Cn), NEG_INF, k.dtype))
            kT = jnp.moveaxis(k, 1, 0)
            vT = jnp.moveaxis(v, 1, 0)
            _, yT = jax.lax.scan(step, init, (kT, vT))
            return jnp.moveaxis(yT, 0, 1)
        return _wkv(w, u, k, v)

    def _L1_ffn_ref(x, gate_w, w1, w2, w3, ws1, ws2, ws3):
        import jax, jax.numpy as jnp
        import numpy as np
        TOP_K = 2
        NUM_EXPERTS = 8
        ROUTE_SCALE = 1.0
        bs, slen, dim = x.shape
        xf = x.reshape(-1, dim)
        logits = (xf @ gate_w.T).astype(jnp.float32)
        scores = jax.nn.sigmoid(logits)
        top_scores, sel_idx = jax.lax.top_k(scores, TOP_K)
        top_scores = top_scores * ROUTE_SCALE
        routed = jnp.zeros_like(xf)
        for k in range(TOP_K):
            xs = xf * top_scores[:, k][:, None]
            h1 = jnp.einsum('td,ehd->teh', xs, w1)
            h3 = jnp.einsum('td,ehd->teh', xs, w3)
            h = jax.nn.silu(h1) * h3
            onehot = jax.nn.one_hot(sel_idx[:, k], NUM_EXPERTS, dtype=h.dtype)
            routed = routed + jnp.einsum('teh,te,edh->td', h, onehot, w2)
        shared = jax.nn.silu(xf @ ws1.T) * (xf @ ws3.T) @ ws2.T
        out = (shared + routed).reshape(bs, slen, dim)
        return out
    x = x + _L0_xattn_ref(_layernorm(x, axis=-1), ctx_2048, ctx_2048)
    x = x + _L0_ffn_ref(_layernorm(x, axis=-1), L0_ffn_Wq, L0_ffn_Wk, L0_ffn_Wv, L0_ffn_Wo, L0_ffn_w_ln1, L0_ffn_w_ln2, L0_ffn_Wr, L0_ffn_Wg, L0_ffn_Wu, L0_ffn_Wd)
    x = x + _L1_xattn_ref(4, 256, 256, L1_xattn_w, L1_xattn_u, _layernorm(x, axis=-1), ctx_2048)
    x = x + _L1_ffn_ref(_layernorm(x, axis=-1), L1_ffn_gate_w, L1_ffn_w1, L1_ffn_w2, L1_ffn_w3, L1_ffn_ws1, L1_ffn_ws2, L1_ffn_ws3)
    return x

_drawn_inputs = setup_inputs


def setup_inputs(seed=0):
    import zlib

    import numpy as np

    out = dict(_drawn_inputs(seed))
    spreads = {'L0_ffn_w_ln1': (1.0, 0.2), 'L0_ffn_w_ln2': (1.0, 0.2)}
    factors = {'L1_ffn_gate_w': 8.0,
     'L1_ffn_w1': 8.0,
     'L1_ffn_w2': 8.0,
     'L1_ffn_w3': 8.0,
     'L1_ffn_ws1': 8.0,
     'L1_ffn_ws2': 8.0,
     'L1_ffn_ws3': 8.0}
    for name, (base, spread) in spreads.items():
        noise = np.random.default_rng([zlib.crc32(name.encode()), seed]).standard_normal(out[name].shape)
        drawn = base * np.exp(spread * noise) if base else spread * noise
        out[name] = jnp.asarray(drawn.astype(out[name].dtype))
    for name, factor in factors.items():
        out[name] = (out[name] * factor).astype(out[name].dtype)
    return out
```

```python
from contextlib import ExitStack

import concourse.bass as bass
from concourse import mybir

F32 = mybir.dt.float32
F16 = mybir.dt.float16
BF16 = mybir.dt.bfloat16
U32 = mybir.dt.uint32
ACT = mybir.ActivationFunctionType
ALU = mybir.AluOpType
X = mybir.AxisListType.X

P = 128
BATCH, TOK, DIM = 4, 256, 256
TT = TOK // P
DC = DIM // P
HEADS, HD = 16, 16
PAIRS = HEADS // 2
STRIP = 32
EXPERTS = 8
INTER = 512
IC = INTER // P
HID1 = 128
NE1 = EXPERTS + 1
CHUNKS1 = [(0, 4), (4, 4), (8, 1)]
EPS = 1e-5

W_UP = 64.0
A_UP = 64.0
QK_UP = 16.0
H_UP = 16.0
SCORE_DOWN = 1.0 / (QK_UP * QK_UP * HD ** 0.5)
PROD_DOWN = 1.0 / (W_UP * A_UP)
QK_SCALE = (QK_UP, QK_UP * PROD_DOWN)
MASK = 2.0 ** 15

E0 = DC * INTER
OFF_QKV = 0
OFF_WO = OFF_QKV + DC * 3 * DIM
OFF_WR = OFF_WO + DC * DIM
OFF_GW = OFF_WR + DC * EXPERTS
OFF_E = OFF_GW + DC * EXPERTS
OFF_W1 = OFF_E + EXPERTS * 3 * E0
OFF_W3 = OFF_W1 + DC * NE1 * HID1
OFF_W2 = OFF_W3 + DC * NE1 * HID1
W_COLS = OFF_W2 + NE1 * DIM
UNIT = 1024
UNITS = [(OFF_QKV, 768), (OFF_QKV + 768, 768), (OFF_WO, OFF_E - OFF_WO)]
UNITS += [(OFF_E + E0 * k, E0) for k in range(3 * EXPERTS)]
UNITS += [(OFF_W1 + 768 * k, 768) for k in range(9)]
STAGES = 4

C_ID, C_TRIQ, C_TRIK, C_COL = 0, P, 2 * P, 3 * P
COL_LN1, COL_LN2, COL_W, COL_U, COL_IOTA, COL_HALF = 2, 4, 6, 8, 10, 18
C_SEL = 3 * P + 22
N_SEL = 16
C_COLS = C_SEL + N_SEL * P


DVE_FIRST, DVE_MID = 27, 65


class Turn:

    def __init__(self, mode, j=None):
        self.mode, self.j = mode, j
        self.front, self.back = mode != "last", mode != "first"


class Signal:

    def __init__(self, sem, front=(), back=(), start=0):
        self.sem, self.start = sem, start
        front, back = list(front), list(back)
        self.order = {"first": front, "mid": front + back, "last": back}

    def before(self, turn):
        first, mid = len(self.order["first"]), len(self.order["mid"])
        if turn.mode == "first":
            return self.start
        return self.start + first + mid * (turn.j if turn.mode == "mid" else BATCH - 1)

    def at(self, turn, name):
        return self.before(turn) + (self.order[turn.mode].index(name) + 1)


class Steps:

    def __init__(self, eng, sem, first, mid):
        self.eng, self.sem, self.first, self.mid = eng, sem, first, mid
        self.n, self.base = 0, 0

    def turn(self, turn):
        self.n = 0
        self.base = 0 if turn.mode == "first" else self.first + self.mid * (turn.j if turn.mode == "mid" else BATCH - 1)

    def done(self, ins):
        self.n += 1
        ins.then_inc(self.sem, 1)

    def wait(self):
        self.eng.wait_ge(self.sem, self.base + self.n)


def att_turns(a):
    return [f"a{a}{s}" for s in ("q", "k", "n0", "n1", "ot0", "ot1")]


def att_acts(a):
    return [f"a{a}k{n}" for n in range(4)] + [f"a{a}p{k}" for k in range(12)]


def att_dves(a):
    return [f"a{a}{s}" for h in range(2) for s in [f"q{2 * h}", f"q{2 * h + 1}"] + [f"s{6 * h + k}" for k in range(6)]]


def kernel_body(nc, x_d, ctx_d, ctxT_d, w_d, c_d, out_d):
    es = ExitStack()
    with es:
        def sb(name, shape, dt=F32):
            return es.enter_context(nc.sbuf_tensor(name, shape, dt))

        def sem(name):
            return es.enter_context(nc.semaphore(name))

        wh = sb("wh", [P, W_COLS], F16)
        wl = sb("wl", [P, W_COLS], F16)
        const = sb("const", [P, C_SEL])
        identb = sb("identb", [P, P], BF16)
        mask_id = sb("mask_id", [P, P], BF16)
        mask_q = sb("mask_q", [P, P], BF16)
        mask_k = sb("mask_k", [P, P], BF16)
        xin = sb("xin", [P, TT, DIM])
        ctx = sb("ctx", [P, TT, DIM])
        vT = sb("vT", [P, DC, TOK])
        sel_rows = sb("sel_rows", [P, N_SEL, P], F16)
        qbd = sb("qbd", [P, PAIRS, 2, TOK], F16)
        kst = sb("kst", [P, PAIRS, TOK], F16)
        vcols = sb("vcols", [P, TT, HEADS * (HD + 1) + STRIP])
        vaug = vcols[:, :, 0:HEADS * (HD + 1)].rearrange("p t (h d) -> p t h d", h=HEADS)
        work = sb("work", [P, 4096])
        probs = work[:, 0:3072].rearrange("p (k n) -> p k n", k=6)
        oT = work[:, 3072:4096].rearrange("p (g n) -> p g n", g=4)
        sg = work[:, 0:1024].rearrange("p (k n) -> p k n", k=2)
        h32 = work[:, 1024:2048].rearrange("p (k n) -> p k n", k=2)
        hT = work[:, 2048:4096].bitcast(F16).rearrange("p (s e i n) -> p s e i n", s=2, e=2, i=IC)
        nmx = sb("nmx", [P, 2, TT, P], BF16)
        nmT = sb("nmT", [P, 2, TOK], BF16)
        att = sb("att", [P, TT, DIM])
        rsum = sb("rsum", [P, TT, HEADS])
        x1 = xin
        z = sb("z", [P, TT, DIM])
        xn = lnq = att
        r2 = z
        xT = sb("xT", [P, 2, DC, TOK], F16)
        kT = sb("kT", [P, 2, DC, TOK], F16)
        x3 = sb("x3", [P, TT, DIM])
        x4 = sb("x4", [P, TT, DIM])
        big = sb("big", [P, 4614])
        stage = [big[:, UNIT * s:UNIT * (s + 1)] for s in range(STAGES)]
        ex = big[:, 0:2048].rearrange("p (k n) -> p k n", k=4)
        ev = big[:, 2048:3072].rearrange("p (k n) -> p k n", k=2)
        omax = big[:, 3072:3586].rearrange("p (c n) -> p c n", c=DC)
        pq = big[:, 3586:4614].rearrange("p (k c n) -> p k c n", k=2, c=DC)
        nd = pq[:, :, :, 0:TOK]
        onew = ev[:, 0, :].rearrange("p (c n) -> p c n", c=DC)
        y = nd[:, 0]
        kx = big[:, 0:512].rearrange("p (t n) -> p t n", t=TT)
        h1 = big[:, 0:TT * NE1 * HID1].rearrange("p (t n) -> p t n", t=TT)
        m16 = big[:, 2304:2304 + TT * NE1 * HID1].bitcast(F16).rearrange("p (s t e n) -> p s t e n", s=2, t=TT, e=NE1)
        outb = x4
        stats = sb("stats", [P, TT, 6])
        mv = sb("mv", [P, TT, 2])
        var = sb("var", [P, 2, TT])
        rstd = sb("rstd", [P, 2, TT])
        ss = sb("ss", [P, TT])
        spare = sb("spare", [P, 1])
        lg = sb("lg", [P, TT, EXPERTS])
        lgx = sb("lgx", [P, TT, EXPERTS])
        lge = sb("lge", [P, TT, EXPERTS])
        top = sb("top", [P, TT, 8])
        topi = sb("topi", [P, TT, 8], U32)
        topf = sb("topf", [P, TT, 8])
        sel = sb("sel", [P, 2, TT, EXPERTS])
        den = sb("den", [P, TT])
        rden = sb("rden", [P, TT])
        cw = sb("cw", [P, TT, EXPERTS])
        s12 = sb("s12", [P, TT, EXPERTS])
        sm = sb("sm", [P, TT, EXPERTS])
        wln = sb("wln", [P, 4])

        ident = const[:, C_ID:C_ID + P]

        def col(k, n=1):
            return const[:, C_COL + k:C_COL + k + n]

        def ring(name):
            return [es.enter_context(nc.psum_tensor(f"{name}{i}", [P, 512], F32)) for i in range(2)]

        turn_b, act_b, dve_b, sum_b = ring("turn_b"), ring("act_b"), ring("dve_b"), ring("sum_b")

        fr_turn = att_turns(0) + ["xn1"] + att_turns(1) + ["hT", "xn2", "lg"]
        bk_turn = ["kT", "yT", "x4", "gl"] + [f"m{t}{c}" for t in range(TT) for c in range(3)]
        fr_act = att_acts(0) + ["v0", "v1"] + att_acts(1) + [f"g{k}" for k in range(2 * EXPERTS)]
        bk_act = [f"mg{t}{c}" for t in range(TT) for c in range(3)]
        fr_dve = att_dves(0) + att_dves(1) + ["wo0", "wo1"] + [f"u{k}" for k in range(2 * EXPERTS)]
        bk_dve = [f"mu{t}{c}" for t in range(TT) for c in range(3)]
        fr_sum = ["a0o0", "a0o1", "a1o0", "a1o1"] + [f"d{e}" for e in range(EXPERTS)]
        bk_sum = [f"md{t}" for t in range(TT)]

        def pair(name, front, back):
            return Signal(sem(name + "_filled"), front, back), Signal(sem(name + "_used"), front, back, start=2)

        turn_filled, turn_used = pair("turn", fr_turn, bk_turn)
        act_filled, act_used = pair("act", fr_act, bk_act)
        dve_filled, dve_used = pair("dve", fr_dve, bk_dve)
        sum_filled, sum_used = pair("sum", fr_sum, bk_sum)
        x_loaded = Signal(sem("x_loaded"), ["x"])
        ctx_loaded = Signal(sem("ctx_loaded"), ["c"])
        v_loaded = Signal(sem("v_loaded"), [], ["v"])
        ctx_used = Signal(sem("ctx_used"), ["c"])
        v_used = Signal(sem("v_used"), [], ["v"])
        highs = Signal(sem("highs"), ["a0q", "a0k", "xn1", "a1q", "a1k", "hT", "xn2"] + [f"h{k}" for k in range(2 * EXPERTS)],
                       ["x4"] + [f"m{t}{c}" for t in range(TT) for c in range(3)])
        hid_ready = Signal(sem("hid_ready"), [f"h{k}" for k in range(2 * EXPERTS)])
        pv_done = Signal(sem("pv_done"), ["a0g0", "a1g0"])
        rows_ready = Signal(sem("rows_ready"), ["a0q", "xn1", "xn2"], ["kT", "y", "x4"])
        var_ready = Signal(sem("var_ready"), ["ln1", "ln2", "rms2"], ["ln3", "ln4"])
        rstd_ready = Signal(sem("rstd_ready"), ["ln1", "ln2", "rms2"], ["ln3", "ln4"])
        squares = Signal(sem("squares"), ["r2"])
        base_ready = Signal(sem("base_ready"), ["x"])
        rt_in = Signal(sem("rt_in"), ["lg"])
        rt_exp = Signal(sem("rt_exp"), ["lg"], ["gl"])
        scores_ready = Signal(sem("scores_ready"), [], ["s"])
        wkv_exp = Signal(sem("wkv_exp"), [], ["w"])
        out_stored = sem("out_stored")
        out_free = Signal(sem("out_free"), [], ["o"])
        s_dve = sem("dve_steps")
        s_pool = sem("pool_steps")
        const_loaded = sem("const_loaded")
        sel_loaded = sem("sel_loaded")
        const_ready = sem("const_ready")
        cleared = sem("cleared")
        staged = [sem(f"staged{s}") for s in range(STAGES)]
        w_ready = sem("w_ready")

        FILL = {}
        for order in (fr_turn + bk_turn, fr_act + bk_act, fr_dve + bk_dve, fr_sum + bk_sum):
            assert len(order) % 2 == 0
            for i, n in enumerate(order):
                FILL[n] = i % 2
        for order in (fr_turn, fr_act, fr_dve, fr_sum):
            assert len(order) % 2 == 0
        T_ = lambda n: turn_b[FILL[n]]
        A_ = lambda n: act_b[FILL[n]]
        D_ = lambda n: dve_b[FILL[n]]
        S_ = lambda n: sum_b[FILL[n]]

        def unit_of(col_):
            return max(k for k, (c, _) in enumerate(UNITS) if c <= col_)

        block = es.enter_context(nc.Block())

        @block.sync
        def _(sp):
            def load(b):
                sp.dma_start(xin[:], x_d[bass.ds(b, 1)].rearrange("o (t p) d -> p (o t) d", p=P)).then_inc(x_loaded.sem, 16)
                sp.dma_start(ctx[:], ctx_d[bass.ds(b, 1)].rearrange("o (t p) d -> p (o t) d", p=P)).then_inc(ctx_loaded.sem, 16)

            def load_v(b):
                sp.dma_start(vT[:], ctxT_d[bass.ds(b, 1)].rearrange("o (c p) t -> p (o c) t", p=P)).then_inc(v_loaded.sem, 16)

            sp.dma_start(const[:], c_d[:, 0:C_SEL]).then_inc(const_loaded, 16)
            sp.dma_start(work[:, 0:N_SEL * P], c_d[:, C_SEL:C_COLS]).then_inc(sel_loaded, 16)
            load(0)
            load_v(0)
            for k, (c, n) in enumerate(UNITS):
                if k >= STAGES:
                    sp.wait_ge(w_ready, k - STAGES + 1)
                sp.dma_start(stage[k % STAGES][:, 0:n], w_d[:, c:c + n]).then_inc(staged[k % STAGES], 16)
            sp.sem_inc(out_free.sem, 1)
            sp.wait_ge(sum_used.sem, sum_used.at(Turn("first"), "d7"))
            load(1)

            def store(turn, b):
                sp.wait_ge(sum_used.sem, sum_used.at(turn, "md1"))
                sp.dma_start(out_d[bass.ds(b, 1)].rearrange("o (t p) d -> p (o t) d", p=P), outb[:]).then_inc(out_stored, 16)

            def mid(j, more):
                turn = Turn("mid", j)
                sp.wait_ge(v_used.sem, j + 1)
                load_v(j + 1)
                if more:
                    sp.wait_ge(sum_used.sem, sum_used.at(turn, "d7"))
                    load(j + 2)
                store(turn, j)
                sp.wait_ge(out_stored, j * 16 + 16)
                sp.sem_inc(out_free.sem, 1)

            with sp.Fori(0, BATCH - 2) as j:
                mid(j, True)
            mid(BATCH - 2, False)
            store(Turn("last"), BATCH - 1)
            sp.wait_ge(out_stored, 16 * BATCH)

        @block.gpsimd
        def _(pool):
            steps = [0]

            def step(ins):
                steps[0] += 1
                ins.then_inc(s_pool, 1)

            def split(k):
                c, n = UNITS[k]
                s = stage[k % STAGES][:, 0:n]
                pool.wait_ge(staged[k % STAGES], 16 * (k // STAGES + 1))
                step(pool.tensor_scalar(wh[:, c:c + n], s, W_UP, 0.0, ALU.mult, ALU.add))
                step(pool.tensor_scalar(s, s, W_UP, 0.0, ALU.mult, ALU.add))
                pool.wait_ge(s_pool, steps[0])
                pool.tensor_tensor(wl[:, c:c + n], s, wh[:, c:c + n], ALU.subtract).then_inc(w_ready, 1)

            def root(turn, name, k=1):
                pool.wait_ge(var_ready.sem, var_ready.at(turn, name))
                pool.tensor_tensor(rstd[:, 0:k, :], var[:, 0:k, :],
                                   col(COL_HALF, 4).rearrange("p (k t) -> p k t", k=2)[:, 0:k, :],
                                   ALU.pow).then_inc(rstd_ready.sem, 1)

            def base(turn):
                pool.wait_ge(dve_used.sem, dve_used.at(turn, "wo1"))
                pool.tensor_tensor(x1[:], x1[:], r2[:], ALU.add).then_inc(base_ready.sem, 1)

            pool.memset(qbd[:], 0.0).then_inc(cleared, 1)
            pool.memset(vcols[:], 0.0).then_inc(s_pool, 1)
            steps[0] += 1
            pool.memset(nmx[:], 0.0).then_inc(cleared, 1)
            pool.wait_ge(s_pool, 1)
            pool.memset(vaug[:, :, :, HD:HD + 1], 1.0).then_inc(cleared, 1)
            first = Turn("first")
            pool.wait_ge(const_loaded, 16)
            root(first, "ln1")
            for k in range(3):
                split(k)
            for k in range(3, 6):
                split(k)
            root(first, "ln2", 2)
            for k in range(6, 9):
                split(k)
            base(first)
            root(first, "rms2")
            for k in range(9, len(UNITS)):
                split(k)
            with pool.Fori(0, BATCH - 1) as j:
                turn = Turn("mid", j)
                root(turn, "ln1")
                root(turn, "ln2", 2)
                base(turn)
                root(turn, "rms2")
                root(turn, "ln3")
                root(turn, "ln4")
            last = Turn("last")
            root(last, "ln3")
            root(last, "ln4")

        @block.scalar
        def _(act):
            def context_values(turn):
                act.wait_ge(ctx_loaded.sem, ctx_loaded.at(turn, "c") * 16)
                if turn.back:
                    act.wait_ge(sum_filled.sem, sum_filled.at(turn, "a0o0") - 1)
                act.activation(vaug[:, :, :, 0:HD], ctx[:].rearrange("p t (h d) -> p t h d", h=HEADS), ACT.Copy).then_inc(ctx_used.sem, 1)

            def attention(turn, a):
                rows_high(turn, f"a{a}q", QK_SCALE[a])
                rows_high(turn, f"a{a}k", QK_SCALE[a], kT)
                for n in range(4):
                    name = f"a{a}k{n}"
                    act.wait_ge(act_filled.sem, act_filled.at(turn, name))
                    act.activation(kst[:, 2 * n:2 * n + 2, :], A_(name)[:].rearrange("p (h n) -> p h n", h=2), ACT.Copy).then_inc(act_used.sem, 1)
                for k in range(12):
                    name = f"a{a}p{k}"
                    act.wait_ge(act_filled.sem, act_filled.at(turn, name))
                    if k == 6:
                        act.wait_ge(pv_done.sem, pv_done.at(turn, f"a{a}g0"))
                    if k == 9:
                        act.wait_ge(sum_filled.sem, sum_filled.at(turn, f"a{a}o0"))
                    act.activation(probs[:, k % 6, :], A_(name)[:], ACT.Exp, scale=SCORE_DOWN).then_inc(act_used.sem, 1)

            def rows_high(turn, name, scale, dst=xT):
                act.wait_ge(turn_filled.sem, turn_filled.at(turn, name))
                if isinstance(scale, float):
                    act.activation(dst[:, 0, :, :], T_(name)[:].rearrange("p (c n) -> p c n", c=DC), ACT.Copy, scale=scale).then_inc(highs.sem, 1)
                    return
                for c in range(DC):
                    ins = act.activation(xT[:, 0, c, :], T_(name)[:, c * TOK:(c + 1) * TOK], ACT.Copy, scale=wln[:, scale + c:scale + c + 1])
                ins.then_inc(highs.sem, 1)

            def second_values(turn):
                for t in range(TT):
                    act.wait_ge(act_filled.sem, act_filled.at(turn, f"v{t}"))
                    act.activation(vaug[:, t, :, 0:HD], A_(f"v{t}")[:, 0:DIM].rearrange("p (h d) -> p h d", h=HEADS), ACT.Copy,
                                   scale=PROD_DOWN).then_inc(act_used.sem, 1)

            def square(turn):
                act.wait_ge(dve_used.sem, dve_used.at(turn, "wo1"))
                for t in range(TT):
                    ins = act.activation(xn[:, t, :], r2[:, t, :], ACT.Square, accum_out=ss[:, t:t + 1])
                ins.then_inc(squares.sem, 1)

            def router_exp(turn, name, scale):
                if name == "lg":
                    act.wait_ge(rt_in.sem, rt_in.at(turn, name))
                else:
                    act.wait_ge(turn_used.sem, turn_used.at(turn, name))
                act.activation(lge[:], lgx[:], ACT.Exp, scale=scale).then_inc(rt_exp.sem, 1)

            def silu(turn, k):
                act.wait_ge(act_filled.sem, act_filled.at(turn, f"g{k}"))
                act.wait_ge(dve_used.sem, dve_used.at(turn, f"u{k}") - 2)
                act.activation(sg[:, k % 2, :], A_(f"g{k}")[:], ACT.Silu, scale=PROD_DOWN).then_inc(act_used.sem, 1)

            def hidden_high(turn, k):
                act.wait_ge(dve_used.sem, dve_used.at(turn, f"u{k}"))
                act.activation(hT[:, 0, (k // 2) % 2, 2 * (k % 2):2 * (k % 2) + 2, :], h32[:, k % 2, :].rearrange("p (i n) -> p i n", i=2),
                               ACT.Copy).then_inc(highs.sem, 1)

            def experts(turn):
                for k in range(2 * EXPERTS):
                    silu(turn, k)
                    if k:
                        hidden_high(turn, k - 1)
                    if turn.back and k == 8:
                        act.wait_ge(turn_used.sem, turn_used.at(turn, "kT"))
                        act.activation(ex[:], ex[:], ACT.Exp).then_inc(wkv_exp.sem, 1)
                hidden_high(turn, 2 * EXPERTS - 1)

            def experts1(turn):
                rows_high(turn, "x4", A_UP)
                router_exp(turn, "gl", -1.0)
                act.wait_ge(scores_ready.sem, scores_ready.at(turn, "s"))
                for t in range(TT):
                    for c, (e0, n) in enumerate(CHUNKS1):
                        name = f"mg{t}{c}"
                        act.wait_ge(act_filled.sem, act_filled.at(turn, name))
                        act.wait_ge(dve_used.sem, dve_used.at(turn, f"mu{t}{c}") - 2)
                        for e in range(e0, e0 + n):
                            s = s12[:, t, e:e + 1] if e < EXPERTS else PROD_DOWN
                            ins = act.activation(sg[:, FILL[name], (e - e0) * P:(e - e0 + 1) * P], A_(name)[:, (e - e0) * P:(e - e0 + 1) * P],
                                                 ACT.Silu, scale=s)
                        ins.then_inc(act_used.sem, 1)
                for t in range(TT):
                    for c, (e0, n) in enumerate(CHUNKS1):
                        name = f"m{t}{c}"
                        act.wait_ge(turn_filled.sem, turn_filled.at(turn, name))
                        act.activation(m16[:, 0, t, e0:e0 + n, :], T_(name)[:, 0:n * P].rearrange("p (e n) -> p e n", e=n), ACT.Copy).then_inc(highs.sem, 1)

            def front(turn):
                context_values(turn)
                attention(turn, 0)
                rows_high(turn, "xn1", 0)
                second_values(turn)
                attention(turn, 1)
                rows_high(turn, "hT", A_UP)
                square(turn)
                rows_high(turn, "xn2", 2)
                router_exp(turn, "lg", 1.0)
                experts(turn)

            act.sem_inc(act_used.sem, act_used.start)
            act.wait_ge(sel_loaded, 16)
            act.activation(sel_rows[:], work[:, 0:N_SEL * P].rearrange("p (s n) -> p s n", s=N_SEL), ACT.Copy)
            act.wait_ge(const_loaded, 16)
            act.activation(identb[:], ident, ACT.Copy)
            act.activation(mask_id[:], ident, ACT.Copy, scale=-MASK)
            act.activation(mask_q[:], const[:, C_TRIQ:C_TRIQ + P], ACT.Copy, scale=MASK)
            act.activation(wln[:], col(COL_LN1, 4), ACT.Copy, scale=A_UP).then_inc(const_ready, 1)
            act.activation(mask_k[:], const[:, C_TRIK:C_TRIK + P], ACT.Copy, scale=MASK).then_inc(const_ready, 1)
            act.wait_ge(const_ready, 2)
            act.wait_ge(cleared, 3)
            front(Turn("first"))
            with act.Fori(0, BATCH - 1) as j:
                turn = Turn("mid", j)
                front(turn)
                experts1(turn)
            last = Turn("last")
            act.wait_ge(turn_used.sem, turn_used.at(last, "kT"))
            act.activation(ex[:], ex[:], ACT.Exp).then_inc(wkv_exp.sem, 1)
            experts1(last)

        @block.vector
        def _(dve):
            st = Steps(dve, s_dve, DVE_FIRST, DVE_MID)

            def stand_alone():
                dve.memset(spare[:], 0.0)

            def row_stats(src):
                for t in range(TT):
                    st.done(dve.bn_stats(stats[:, t, :], src[:, t, :]))
                st.wait()
                stand_alone()
                for t in range(TT):
                    st.done(dve.bn_aggr(mv[:, t, :], stats[:, t, :]))
                st.wait()

            def normed(dst, src, k=0):
                for t in range(TT):
                    ins = dve.tensor_scalar(dst[:, t, :], src[:, t, :], mv[:, t, 0:1], rstd[:, k, t:t + 1], ALU.subtract, ALU.mult)
                return ins

            def ln1(turn):
                dve.wait_ge(x_loaded.sem, x_loaded.at(turn, "x") * 16)
                row_stats(xin)
                dve.tensor_scalar(var[:, 0, :], mv[:, :, 1], EPS, None, ALU.add).then_inc(var_ready.sem, 1)
                dve.wait_ge(rstd_ready.sem, rstd_ready.at(turn, "ln1"))
                normed(lnq, xin).then_inc(rows_ready.sem, 1)

            def place_queries(turn, a, n):
                name = f"a{a}q{n}"
                dve.wait_ge(dve_filled.sem, dve_filled.at(turn, name))
                for ab in range(2):
                    r = slice(64 * ab, 64 * ab + 64)
                    ins = dve.tensor_copy(qbd[r, 2 * n:2 * n + 2, ab, :], D_(name)[r, :].rearrange("p (h n) -> p h n", h=2))
                ins.then_inc(dve_used.sem, 1)

            def score_max(turn, a, k):
                name = f"a{a}s{k}"
                half, k = divmod(k, 6)
                t, h, n = (0, 4 * k, 4) if k < 2 else (1, 2 * (k - 2), 2)
                dve.wait_ge(dve_filled.sem, dve_filled.at(turn, name))
                dve.tensor_reduce(nmx[:, half, t, h:h + n], D_(name)[:].rearrange("p (h n) -> p h n", h=n), X, ALU.max,
                                  negate=True).then_inc(dve_used.sem, 1)

            def attention(turn, a):
                rows_low(turn, f"a{a}q", QK_SCALE[a])
                rows_low(turn, f"a{a}k", QK_SCALE[a], kT)
                for half in range(2):
                    for n in (2 * half, 2 * half + 1):
                        place_queries(turn, a, n)
                    for k in range(6):
                        score_max(turn, a, 6 * half + k)
                for half in range(2):
                    name = f"a{a}n{half}"
                    dve.wait_ge(turn_filled.sem, turn_filled.at(turn, name))
                    dve.tensor_copy(nmT[:, half, :], T_(name)[:].bitcast(BF16)[:, 0:TOK]).then_inc(turn_used.sem, 1)
                for half in range(2):
                    name = f"a{a}o{half}"
                    dve.wait_ge(sum_filled.sem, sum_filled.at(turn, name))
                    dve.tensor_copy(oT[:, 2 * half:2 * half + 2, :], S_(name)[:].rearrange("p (g n) -> p g n", g=2)).then_inc(sum_used.sem, 1)
                for t in range(TT):
                    name = f"a{a}ot{t}"
                    dve.wait_ge(turn_filled.sem, turn_filled.at(turn, name))
                    o = T_(name)[:].rearrange("p (h d) -> p h d", h=HEADS)
                    st.done(dve.reciprocal(rsum[:, t, :], o[:, :, HD]))
                    st.wait()
                    ins = dve.tensor_tensor(att[:, t, :].rearrange("p (h d) -> p h d", h=HEADS), o[:, :, 0:HD],
                                            rsum[:, t, :].unsqueeze(2).broadcast_to([P, HEADS, HD]), ALU.mult)
                    ins.then_inc(turn_used.sem, 1)

            def first_sum(turn):
                dve.wait_ge(turn_used.sem, turn_used.at(turn, "a0ot1"))
                st.done(dve.tensor_tensor(x1[:], xin[:], att[:], ALU.add))
                st.wait()
                row_stats(x1)
                st.done(dve.tensor_scalar(var[:, 0, :], mv[:, :, 1], EPS, None, ALU.add))
                dve.tensor_scalar(var[:, 1, :], mv[:, :, 1], 1 + EPS, EPS * EPS, ALU.mult, ALU.add).then_inc(var_ready.sem, 1)
                dve.wait_ge(rstd_ready.sem, rstd_ready.at(turn, "ln2"))
                normed(xn, x1, 1).then_inc(rows_ready.sem, 1)
                st.done(normed(z, x1, 0))

            def rows_low(turn, name, scale, dst=xT):
                dve.wait_ge(highs.sem, highs.at(turn, name))
                if isinstance(scale, float):
                    dve.scalar_tensor_tensor(dst[:, 1, :, :], T_(name)[:].rearrange("p (c n) -> p c n", c=DC), scale, dst[:, 0, :, :],
                                             ALU.mult, ALU.subtract).then_inc(turn_used.sem, 1)
                    return
                for c in range(DC):
                    ins = dve.scalar_tensor_tensor(xT[:, 1, c, :], T_(name)[:, c * TOK:(c + 1) * TOK], wln[:, scale + c:scale + c + 1], xT[:, 0, c, :],
                                                   ALU.mult, ALU.subtract)
                ins.then_inc(turn_used.sem, 1)

            def second_sum(turn):
                for t in range(TT):
                    dve.wait_ge(dve_filled.sem, dve_filled.at(turn, f"wo{t}"))
                    if t == 0:
                        st.wait()
                    dve.scalar_tensor_tensor(r2[:, t, :], D_(f"wo{t}")[:, 0:DIM], PROD_DOWN, z[:, t, :], ALU.mult,
                                             ALU.add).then_inc(dve_used.sem, 1)
                dve.wait_ge(squares.sem, squares.at(turn, "r2"))
                dve.tensor_scalar(var[:, 0, :], ss[:], 1 / DIM, EPS, ALU.mult, ALU.add).then_inc(var_ready.sem, 1)
                dve.wait_ge(rstd_ready.sem, rstd_ready.at(turn, "rms2"))
                dve.wait_ge(dve_used.sem, dve_used.at(turn, "wo1"))
                for t in range(TT):
                    ins = dve.tensor_scalar(xn[:, t, :], r2[:, t, :], rstd[:, 0, t:t + 1], None, ALU.mult)
                ins.then_inc(rows_ready.sem, 1)

            def top2(src):
                stand_alone()
                for t in range(TT):
                    st.done(dve.max(top[:, t, :], src[:, t, :]))
                st.wait()
                stand_alone()
                for t in range(TT):
                    st.done(dve.max_index(topi[:, t, :], top[:, t, :], src[:, t, :]))
                st.wait()
                st.done(dve.tensor_copy(topf[:], topi[:]))
                st.wait()
                iota = col(COL_IOTA, 8).unsqueeze(1).broadcast_to([P, TT, EXPERTS])
                for k in range(2):
                    st.done(dve.tensor_tensor(sel[:, k], iota, topf[:, :, k:k + 1].broadcast_to([P, TT, EXPERTS]), ALU.is_equal))
                st.wait()
                st.done(dve.tensor_tensor(sel[:, 0], sel[:, 0], sel[:, 1], ALU.add))
                st.wait()

            def router(turn):
                dve.wait_ge(turn_filled.sem, turn_filled.at(turn, "lg"))
                dve.tensor_scalar(lg[:], T_("lg")[:, 0:TT * EXPERTS].rearrange("p (t e) -> p t e", t=TT), PROD_DOWN, None,
                                  ALU.mult).then_inc(turn_used.sem, 1)
                dve.wait_ge(turn_used.sem, turn_used.at(turn, "lg"))
                top2(lg)
                dve.tensor_tensor(lgx[:], lg[:], top[:, :, 0:1].broadcast_to([P, TT, EXPERTS]), ALU.subtract).then_inc(rt_in.sem, 1)
                dve.wait_ge(rt_exp.sem, rt_exp.at(turn, "lg"))
                st.done(dve.tensor_tensor(lge[:], lge[:], sel[:, 0], ALU.mult))
                st.wait()
                st.done(dve.tensor_reduce(den[:], lge[:], X, ALU.add))
                st.wait()
                st.done(dve.reciprocal(rden[:], den[:]))
                st.wait()
                st.done(dve.scalar_tensor_tensor(cw[:], lge[:], 1 / (H_UP * W_UP), rden[:].unsqueeze(2).broadcast_to([P, TT, EXPERTS]),
                                                 ALU.mult, ALU.mult))
                st.wait()

            def hidden(turn, k):
                dve.wait_ge(dve_filled.sem, dve_filled.at(turn, f"u{k}"))
                dve.wait_ge(act_used.sem, act_used.at(turn, f"g{k}"))
                if turn.back or k >= 2:
                    dve.wait_ge(hid_ready.sem, hid_ready.at(turn, f"h{k}") - 2)
                dve.scalar_tensor_tensor(h32[:, k % 2, :], D_(f"u{k}")[:], H_UP * PROD_DOWN, sg[:, k % 2, :], ALU.mult,
                                         ALU.mult).then_inc(dve_used.sem, 1)

            def hidden_low(turn, k):
                dve.wait_ge(highs.sem, highs.at(turn, f"h{k}"))
                dve.tensor_tensor(hT[:, 1, (k // 2) % 2, 2 * (k % 2):2 * (k % 2) + 2, :], h32[:, k % 2, :].rearrange("p (i n) -> p i n", i=2),
                                  hT[:, 0, (k // 2) % 2, 2 * (k % 2):2 * (k % 2) + 2, :], ALU.subtract).then_inc(hid_ready.sem, 1)

            def add_expert(turn, e):
                dve.wait_ge(sum_filled.sem, sum_filled.at(turn, f"d{e}"))
                if e == 0:
                    dve.wait_ge(base_ready.sem, base_ready.at(turn, "x"))
                else:
                    dve.wait_ge(sum_used.sem, sum_used.at(turn, f"d{e - 1}"))
                dst = x3 if e == EXPERTS - 1 else x1
                for t in range(TT):
                    ins = dve.scalar_tensor_tensor(dst[:, t, :], S_(f"d{e}")[:, t * DIM:(t + 1) * DIM], cw[:, t, e:e + 1], x1[:, t, :],
                                                   ALU.mult, ALU.add)
                ins.then_inc(sum_used.sem, 1)

            def wkv_norm(turn, prev):
                row_stats(x3)
                dve.tensor_scalar(var[:, 0, :], mv[:, :, 1], EPS, None, ALU.add).then_inc(var_ready.sem, 1)

            def wkv_rows(turn):
                dve.wait_ge(w_ready, len(UNITS))
                dve.wait_ge(rstd_ready.sem, rstd_ready.at(turn, "ln3"))
                normed(kx, x3).then_inc(rows_ready.sem, 1)

            def wkv_exponents(turn):
                dve.wait_ge(turn_filled.sem, turn_filled.at(turn, "kT"))
                k = T_("kT")[:].rearrange("p (c n) -> p c n", c=DC)
                exv = ex.rearrange("p k (c n) -> p k c n", c=DC)
                st.done(dve.memset(omax[:, :, 0:1], -1e38))
                st.done(dve.memset(pq[:, :, :, 0:1], 0.0))
                for c in range(DC):
                    st.done(dve.tensor_tensor_scan(omax[:, c, 1:TOK + 1], col(COL_W + c).broadcast_to([P, TOK]), k[:, c, :], -1e38,
                                                   ALU.add, ALU.max))
                st.wait()
                for c in range(DC):
                    st.done(dve.scalar_tensor_tensor(onew[:, c, :], k[:, c, :], col(COL_U + c), omax[:, c, 0:TOK], ALU.add, ALU.max))
                st.wait()
                st.done(dve.tensor_tensor(exv[:, 0], omax[:, :, 0:TOK], onew[:], ALU.subtract))
                for c in range(DC):
                    st.done(dve.scalar_tensor_tensor(exv[:, 1, c, :], omax[:, c, 0:TOK], col(COL_W + c), omax[:, c, 1:TOK + 1], ALU.add, ALU.subtract))
                    st.done(dve.scalar_tensor_tensor(exv[:, 2, c, :], k[:, c, :], col(COL_U + c), onew[:, c, :], ALU.add, ALU.subtract))
                dve.tensor_tensor(exv[:, 3], k, omax[:, :, 1:TOK + 1], ALU.subtract).then_inc(turn_used.sem, 1)

            def wkv_scan(turn):
                dve.wait_ge(wkv_exp.sem, wkv_exp.at(turn, "w"))
                dve.wait_ge(v_loaded.sem, v_loaded.at(turn, "v") * 16)
                dve.tensor_tensor(ev, ex[:, 2:4, :], vT[:].rearrange("p c n -> p (c n)").unsqueeze(1).broadcast_to([P, 2, 512]),
                                  ALU.mult).then_inc(v_used.sem, 1)
                dve.wait_ge(v_used.sem, v_used.at(turn, "v"))
                for c in range(DC):
                    r = slice(c * TOK, (c + 1) * TOK)
                    st.done(dve.tensor_tensor_scan(pq[:, 0, c, 1:TOK + 1], ex[:, 1, r], ev[:, 1, r], 0.0, ALU.mult, ALU.add))
                    st.done(dve.tensor_tensor_scan(pq[:, 1, c, 1:TOK + 1], ex[:, 1, r], ex[:, 3, r], 0.0, ALU.mult, ALU.add))
                st.wait()

            def wkv_out(turn):
                a = ex[:, 0, :].rearrange("p (c n) -> p c n", c=DC).unsqueeze(1).broadcast_to([P, 2, DC, TOK])
                st.done(dve.tensor_tensor(nd, a, nd, ALU.mult))
                st.wait()
                st.done(dve.tensor_tensor(nd[:, 1], nd[:, 1], ex[:, 2].rearrange("p (c n) -> p c n", c=DC), ALU.add))
                st.done(dve.tensor_tensor(nd[:, 0], nd[:, 0], ev[:, 0].rearrange("p (c n) -> p c n", c=DC), ALU.add))
                st.wait()
                st.done(dve.reciprocal(nd[:, 1], nd[:, 1]))
                st.wait()
                dve.tensor_tensor(y, nd[:, 0], nd[:, 1], ALU.mult).then_inc(rows_ready.sem, 1)

            def third_sum(turn):
                dve.wait_ge(turn_filled.sem, turn_filled.at(turn, "yT"))
                dve.wait_ge(out_free.sem, out_free.at(turn, "o"))
                dve.tensor_tensor(x4[:], x3[:], T_("yT")[:].rearrange("p (t n) -> p t n", t=TT), ALU.add).then_inc(turn_used.sem, 1)

            def last_norm(turn):
                dve.wait_ge(turn_used.sem, turn_used.at(turn, "yT"))
                row_stats(x4)
                dve.tensor_scalar(var[:, 0, :], mv[:, :, 1], EPS, None, ALU.add).then_inc(var_ready.sem, 1)
                dve.wait_ge(rstd_ready.sem, rstd_ready.at(turn, "ln4"))
                normed(kx, x4).then_inc(rows_ready.sem, 1)

            def experts1(turn):
                rows_low(turn, "x4", A_UP)
                dve.wait_ge(turn_filled.sem, turn_filled.at(turn, "gl"))
                dve.tensor_scalar(lgx[:], T_("gl")[:, 0:TT * EXPERTS].rearrange("p (t e) -> p t e", t=TT), PROD_DOWN, None,
                                  ALU.mult).then_inc(turn_used.sem, 1)
                dve.wait_ge(rt_exp.sem, rt_exp.at(turn, "gl"))
                st.done(dve.tensor_scalar(lge[:], lge[:], 1.0, None, ALU.add))
                st.wait()
                st.done(dve.reciprocal(lg[:], lge[:]))
                st.wait()
                dve.tensor_scalar(s12[:], lg[:], PROD_DOWN, None, ALU.mult).then_inc(scores_ready.sem, 1)
                top2(lg)
                st.done(dve.scalar_tensor_tensor(sm[:], lg[:], H_UP * PROD_DOWN, sel[:, 0], ALU.mult, ALU.mult))
                st.wait()
                for t in range(TT):
                    for c, (e0, n) in enumerate(CHUNKS1):
                        name = f"mu{t}{c}"
                        dve.wait_ge(dve_filled.sem, dve_filled.at(turn, name))
                        dve.wait_ge(act_used.sem, act_used.at(turn, f"mg{t}{c}"))
                        for e in range(e0, e0 + n):
                            s = sm[:, t, e:e + 1] if e < EXPERTS else H_UP * PROD_DOWN
                            r = slice((e - e0) * P, (e - e0 + 1) * P)
                            ins = dve.scalar_tensor_tensor(h1[:, t, e * P:(e + 1) * P], D_(name)[:, r], s, sg[:, FILL[f"mg{t}{c}"], r], ALU.mult, ALU.mult)
                        ins.then_inc(dve_used.sem, 1)
                for t in range(TT):
                    for c, (e0, n) in enumerate(CHUNKS1):
                        name = f"m{t}{c}"
                        dve.wait_ge(highs.sem, highs.at(turn, name))
                        dve.tensor_tensor(m16[:, 1, t, e0:e0 + n, :], T_(name)[:, 0:n * P].rearrange("p (e n) -> p e n", e=n),
                                          m16[:, 0, t, e0:e0 + n, :], ALU.subtract).then_inc(turn_used.sem, 1)
                for t in range(TT):
                    dve.wait_ge(sum_filled.sem, sum_filled.at(turn, f"md{t}"))
                    dve.scalar_tensor_tensor(outb[:, t, :], S_(f"md{t}")[:, 0:DIM], 1 / (H_UP * W_UP), x4[:, t, :], ALU.mult,
                                             ALU.add).then_inc(sum_used.sem, 1)

            def front(turn):
                ln1(turn)
                attention(turn, 0)
                first_sum(turn)
                rows_low(turn, "xn1", 0)
                attention(turn, 1)
                rows_low(turn, "hT", A_UP)
                second_sum(turn)
                rows_low(turn, "xn2", 2)
                router(turn)
                for e in range(EXPERTS):
                    hidden(turn, 2 * e)
                    if e:
                        hidden_low(turn, 2 * e - 1)
                    hidden(turn, 2 * e + 1)
                    hidden_low(turn, 2 * e)
                    if turn.back:
                        if e == 0:
                            wkv_norm(turn, True)
                        if e == 1:
                            wkv_rows(turn)
                        if e == 3:
                            wkv_exponents(turn)
                        if e == 4:
                            wkv_scan(turn)
                        if e == 5:
                            wkv_out(turn)
                        if e == 7:
                            third_sum(turn)
                    if e:
                        add_expert(turn, e - 1)
                hidden_low(turn, 2 * EXPERTS - 1)
                add_expert(turn, EXPERTS - 1)

            for used in (turn_used, dve_used, sum_used):
                dve.sem_inc(used.sem, used.start)
            dve.wait_ge(const_ready, 2)
            dve.wait_ge(cleared, 3)
            first = Turn("first")
            st.turn(first)
            front(first)
            assert st.n == DVE_FIRST, st.n
            with dve.Fori(0, BATCH - 1) as j:
                turn = Turn("mid", j)
                st.turn(turn)
                front(turn)
                last_norm(turn)
                experts1(turn)
                assert st.n == DVE_MID, st.n
            last = Turn("last")
            st.turn(last)
            wkv_norm(last, False)
            wkv_rows(last)
            wkv_exponents(last)
            wkv_scan(last)
            wkv_out(last)
            third_sum(last)
            last_norm(last)
            experts1(last)

        @block.tensor
        def _(pe):
            def split_product(out, terms, low_low=False):
                mm = [(l, r) for lhs, rhs in terms for l, r in ([(lhs[0], rhs[0]), (lhs[0], rhs[1]), (lhs[1], rhs[0])] + [(lhs[1], rhs[1])] * low_low)]
                for i, (l, r) in enumerate(mm):
                    ins = pe.matmul(out, l, r, start=(i == 0), stop=(i == len(mm) - 1))
                return ins

            def w_pair(off, n):
                return wh[:, off:off + n], wl[:, off:off + n]

            def weights(turn, off):
                if turn.mode == "first" or off >= OFF_W1:
                    pe.wait_ge(w_ready, unit_of(off - 1) + 1)

            def stack_rows(turn, a, s, n):
                name = f"a{a}{s}{n}"
                src, k, bank, filled, used = (xT, 0, D_, dve_filled, dve_used) if s == "q" else (kT, 2, A_, act_filled, act_used)
                pe.wait_ge(used.sem, used.at(turn, name) - 2)
                pe.wait_ge(turn_used.sem, turn_used.at(turn, f"a{a}{s}"))
                for i in range(2):
                    for part in range(2):
                        ins = pe.matmul(bank(name)[:, i * TOK:(i + 1) * TOK], sel_rows[:, 4 * (k + part) + (2 * n + i) % 4, :], src[:, part, n // 2, :],
                                        start=(i + part == 0), stop=(i + part == 2), skip_group_check=True)
                ins.then_inc(filled.sem, 1)

            def scores(turn, a, half):
                for k in range(6):
                    name = f"a{a}s{6 * half + k}"
                    pe.wait_ge(dve_used.sem, dve_used.at(turn, name) - 2)
                    t, h0, n, keys = (0, 4 * k, 4, P) if k < 2 else (1, 2 * (k - 2), 2, TOK)
                    if k == 0:
                        pe.wait_ge(dve_used.sem, dve_used.at(turn, f"a{a}q{2 * half + 1}"))
                        pe.wait_ge(act_used.sem, act_used.at(turn, f"a{a}k{2 * half + 1}"))
                    bank = D_(name)[:].rearrange("p (h n) -> p h n", h=n)
                    for i in range(n):
                        hp, ab = divmod(8 * half + h0 + i, 2)
                        pe.matmul(bank[:, i, :], qbd[:, hp, ab, t * P:(t + 1) * P], kst[:, hp, 0:keys], start=(i == 0), stop=False, skip_group_check=True)
                    pe.matmul(bank[:, :, keys - P:keys], mask_id[:], mask_q[:].unsqueeze(1).broadcast_to([P, n, P]), start=False,
                              stop=True, skip_group_check=True).then_inc(dve_filled.sem, 1)

            def turn_max(turn, a, half):
                name = f"a{a}n{half}"
                pe.wait_ge(turn_used.sem, turn_used.at(turn, name) - 2)
                pe.wait_ge(dve_used.sem, dve_used.at(turn, f"a{a}s{6 * half + 5}"))
                for t in range(TT):
                    ins = pe.transpose(T_(name)[:].bitcast(BF16)[:, t * P:(t + 1) * P], nmx[:, half, t, :], identb[:])
                ins.then_inc(turn_filled.sem, 1)

            def exponents(turn, a, g):
                half = g // 2
                if g % 2 == 0:
                    pe.wait_ge(turn_used.sem, turn_used.at(turn, f"a{a}n{half}"))
                for i in range(3):
                    name = f"a{a}p{3 * g + i}"
                    pe.wait_ge(act_used.sem, act_used.at(turn, name) - 2)
                    q0 = 0 if i < 2 else P
                    heads = range(4 * g + 2 * i, 4 * g + 2 * i + 2) if i < 2 else range(4 * g, 4 * g + 4)
                    bank = A_(name)[:].rearrange("p (h n) -> p h n", h=len(heads))
                    for hp in range(heads[0] // 2, heads[-1] // 2 + 1):
                        r = 2 * hp - heads[0]
                        pe.matmul(bank[:, r:r + 2, :], kst[:, hp, q0:q0 + P], qbd[:, hp, :, q0:TOK], start=(r == 0), stop=False, skip_group_check=True)
                    for r, h in enumerate(heads):
                        pe.matmul(bank[:, r, :], identb[:, h - 8 * half:h - 8 * half + 1].broadcast_to([P, P]), nmT[:, half, q0:TOK],
                                  start=False, stop=False, skip_group_check=True)
                    pe.matmul(bank[:, :, 0:P], mask_id[:], mask_k[:].unsqueeze(1).broadcast_to([P, len(heads), P]), start=False, stop=True,
                              skip_group_check=True).then_inc(act_filled.sem, 1)

            def values(turn, a, g):
                o = f"a{a}o{g // 2}"
                if g % 2 == 0:
                    pe.wait_ge(sum_used.sem, sum_used.at(turn, o) - 2)
                pe.wait_ge(act_used.sem, act_used.at(turn, f"a{a}p{3 * g + 2}"))
                for j in range(4):
                    h = 4 * g + j
                    s = 3 * (g % 2)
                    out = S_(o)[STRIP * j:STRIP * (j + 1), (g % 2) * TOK:(g % 2 + 1) * TOK]
                    pe.matmul(out, vcols[:, 0, h * (HD + 1):h * (HD + 1) + STRIP], probs[:, s + j // 2, (j % 2) * TOK:(j % 2 + 1) * TOK], start=True, stop=False, skip_group_check=True)
                    ins = pe.matmul(out[:, P:TOK], vcols[:, 1, h * (HD + 1):h * (HD + 1) + STRIP], probs[:, s + 2, j * P:(j + 1) * P], start=False, stop=True, skip_group_check=True)
                if g == 0:
                    ins.then_inc(pv_done.sem, 1)
                if g % 2:
                    ins.then_inc(sum_filled.sem, 1)

            def attention(turn, a):
                for half in range(2):
                    for n in (2 * half, 2 * half + 1):
                        stack_rows(turn, a, "q", n)
                        stack_rows(turn, a, "k", n)
                    scores(turn, a, half)
                turn_max(turn, a, 0)
                exponents(turn, a, 0)
                exponents(turn, a, 1)
                values(turn, a, 0)
                turn_max(turn, a, 1)
                exponents(turn, a, 2)
                values(turn, a, 1)
                exponents(turn, a, 3)
                values(turn, a, 2)
                values(turn, a, 3)
                for t in range(TT):
                    name = f"a{a}ot{t}"
                    pe.wait_ge(turn_used.sem, turn_used.at(turn, name) - 2)
                    if t == 0:
                        pe.wait_ge(sum_used.sem, sum_used.at(turn, f"a{a}o1"))
                    for g in range(4):
                        ins = pe.transpose(T_(name)[:, g * P:(g + 1) * P], oT[:, g, t * P:(t + 1) * P], ident)
                    ins.then_inc(turn_filled.sem, 1)

            def turn_rows(turn, name, src):
                pe.wait_ge(turn_used.sem, turn_used.at(turn, name) - 2)
                if name == "hT":
                    pe.wait_ge(turn_used.sem, turn_used.at(turn, "a1ot1"))
                elif name == "a0k":
                    pe.wait_ge(ctx_loaded.sem, ctx_loaded.at(turn, "c") * 16)
                else:
                    pe.wait_ge(rows_ready.sem, rows_ready.at(turn, name))
                for c in range(DC):
                    for t in range(TT):
                        ins = pe.transpose(T_(name)[:, c * TOK + t * P:c * TOK + (t + 1) * P], src[:, t, c * P:(c + 1) * P], ident)
                ins.then_inc(turn_filled.sem, 1)

            def rows_pair(c, t):
                return xT[:, 0, c, t * P:(t + 1) * P], xT[:, 1, c, t * P:(t + 1) * P]

            def qkv(turn):
                pe.wait_ge(turn_used.sem, turn_used.at(turn, "xn1"))
                weights(turn, OFF_WO)
                for m, name in enumerate(("a1q", "a1k")):
                    pe.wait_ge(turn_used.sem, turn_used.at(turn, name) - 2)
                    for o in range(DC):
                        ins = split_product(T_(name)[:, o * TOK:(o + 1) * TOK],
                                            [(w_pair(OFF_QKV + c * 3 * DIM + m * DIM + o * P, P), (xT[:, 0, c, :], xT[:, 1, c, :])) for c in range(DC)])
                    ins.then_inc(turn_filled.sem, 1)
                for t in range(TT):
                    pe.wait_ge(act_used.sem, act_used.at(turn, f"v{t}") - 2)
                    split_product(A_(f"v{t}")[:, 0:DIM], [(rows_pair(c, t), w_pair(OFF_QKV + c * 3 * DIM + 2 * DIM, DIM)) for c in range(DC)])\
                        .then_inc(act_filled.sem, 1)

            def out_projection(turn):
                pe.wait_ge(turn_used.sem, turn_used.at(turn, "hT"))
                weights(turn, OFF_WR)
                for t in range(TT):
                    pe.wait_ge(dve_used.sem, dve_used.at(turn, f"wo{t}") - 2)
                    split_product(D_(f"wo{t}")[:, 0:DIM], [(rows_pair(c, t), w_pair(OFF_WO + c * DIM, DIM)) for c in range(DC)])\
                        .then_inc(dve_filled.sem, 1)

            def logits(turn, name, rows, off):
                pe.wait_ge(turn_used.sem, turn_used.at(turn, rows))
                weights(turn, OFF_E)
                pe.wait_ge(turn_used.sem, turn_used.at(turn, name) - 2)
                for t in range(TT):
                    ins = split_product(T_(name)[:, t * EXPERTS:(t + 1) * EXPERTS],
                                        [(rows_pair(c, t), w_pair(off + c * EXPERTS, EXPERTS)) for c in range(DC)], low_low=True)
                ins.then_inc(turn_filled.sem, 1)

            def gate_up(turn, e, half):
                k = 2 * e + half
                for name, bank, used, filled, m in ((f"g{k}", A_, act_used, act_filled, 0), (f"u{k}", D_, dve_used, dve_filled, 1)):
                    off = OFF_E + (3 * e + m) * E0
                    weights(turn, off + E0)
                    pe.wait_ge(used.sem, used.at(turn, name) - 2)
                    for i in range(2):
                        n0 = (2 * half + i) * P
                        ins = split_product(bank(name)[:, i * TOK:(i + 1) * TOK],
                                            [(w_pair(off + c * INTER + n0, P), (xT[:, 0, c, :], xT[:, 1, c, :])) for c in range(DC)])
                    ins.then_inc(filled.sem, 1)

            def down(turn, e):
                off = OFF_E + (3 * e + 2) * E0
                weights(turn, off + E0)
                pe.wait_ge(sum_used.sem, sum_used.at(turn, f"d{e}") - 2)
                pe.wait_ge(hid_ready.sem, hid_ready.at(turn, f"h{2 * e + 1}"))
                for t in range(TT):
                    ins = split_product(S_(f"d{e}")[:, t * DIM:(t + 1) * DIM],
                                        [((hT[:, 0, e % 2, i, t * P:(t + 1) * P], hT[:, 1, e % 2, i, t * P:(t + 1) * P]), w_pair(off + i * DIM, DIM))
                                         for i in range(IC)])
                ins.then_inc(sum_filled.sem, 1)

            def wkv_out_rows(turn):
                pe.wait_ge(turn_used.sem, turn_used.at(turn, "yT") - 2)
                pe.wait_ge(rows_ready.sem, rows_ready.at(turn, "y"))
                for t in range(TT):
                    for c in range(DC):
                        ins = pe.transpose(T_("yT")[:, t * DIM + c * P:t * DIM + (c + 1) * P], y[:, c, t * P:(t + 1) * P], ident)
                ins.then_inc(turn_filled.sem, 1)

            def experts1(turn):
                turn_rows(turn, "x4", kx)
                logits(turn, "gl", "x4", OFF_GW)
                weights(turn, W_COLS)

                def hidden_rows(t):
                    for c, (e0, n) in enumerate(CHUNKS1):
                        name = f"m{t}{c}"
                        pe.wait_ge(turn_used.sem, turn_used.at(turn, name) - 2)
                        pe.wait_ge(dve_used.sem, dve_used.at(turn, f"mu{t}{c}"))
                        for i in range(n):
                            ins = pe.transpose(T_(name)[:, i * P:(i + 1) * P], h1[:, t, (e0 + i) * P:(e0 + i + 1) * P], ident)
                        ins.then_inc(turn_filled.sem, 1)

                for t in range(TT):
                    for c, (e0, n) in enumerate(CHUNKS1):
                        for name, bank, used, filled, off in ((f"mg{t}{c}", A_, act_used, act_filled, OFF_W1), (f"mu{t}{c}", D_, dve_used, dve_filled, OFF_W3)):
                            pe.wait_ge(used.sem, used.at(turn, name) - 2)
                            split_product(bank(name)[:, 0:n * P], [(rows_pair(d, t), w_pair(off + d * NE1 * HID1 + e0 * P, n * P)) for d in range(DC)])\
                                .then_inc(filled.sem, 1)
                for t in range(TT):
                    hidden_rows(t)
                for t in range(TT):
                    pe.wait_ge(sum_used.sem, sum_used.at(turn, f"md{t}") - 2)
                    pe.wait_ge(turn_used.sem, turn_used.at(turn, f"m{t}2"))
                    split_product(S_(f"md{t}")[:, 0:DIM], [((m16[:, 0, t, e, :], m16[:, 1, t, e, :]), w_pair(OFF_W2 + e * DIM, DIM)) for e in range(NE1)])\
                        .then_inc(sum_filled.sem, 1)

            def front(turn):
                turn_rows(turn, "a0q", lnq)
                turn_rows(turn, "a0k", ctx)
                attention(turn, 0)
                turn_rows(turn, "xn1", xn)
                qkv(turn)
                attention(turn, 1)
                turn_rows(turn, "hT", att)
                out_projection(turn)
                turn_rows(turn, "xn2", xn)
                logits(turn, "lg", "xn2", OFF_WR)
                for e in range(EXPERTS):
                    gate_up(turn, e, 0)
                    gate_up(turn, e, 1)
                    if e:
                        down(turn, e - 1)
                    if turn.back and e == 2:
                        turn_rows(turn, "kT", kx)
                    if turn.back and e == 6:
                        wkv_out_rows(turn)
                down(turn, EXPERTS - 1)

            pe.wait_ge(const_ready, 2)
            pe.wait_ge(cleared, 3)
            front(Turn("first"))
            with pe.Fori(0, BATCH - 1) as j:
                turn = Turn("mid", j)
                front(turn)
                experts1(turn)
            last = Turn("last")
            turn_rows(last, "kT", kx)
            wkv_out_rows(last)
            experts1(last)


def _consts():
    import numpy as np
    c = np.zeros((P, C_COLS), np.float32)
    c[:, C_ID:C_ID + P] = np.eye(P)
    c[:, C_TRIQ:C_TRIQ + P] = np.triu(np.ones((P, P)), 1)
    c[:, C_TRIK:C_TRIK + P] = np.tril(np.ones((P, P)), -1)
    m = np.arange(P)
    part = (m // HD) % 4
    for k, takes in enumerate((part % 2 == 0, part % 2 == 1, part < 2, part >= 2)):
        for pair in range(4):
            s = c[:, C_SEL + (4 * k + pair) * P:C_SEL + (4 * k + pair + 1) * P]
            s[(2 * pair + m // 64) * HD + m % HD, m] = takes
    c[:, C_COL + COL_IOTA:C_COL + COL_IOTA + 8] = np.arange(8)
    c[:, C_COL + COL_HALF:C_COL + COL_HALF + 4] = -0.5
    return c


def kernel(**inputs):
    import numpy as np
    import concourse.bacc as bacc
    from concourse.bass_utils import run_bass_kernel_spmd

    v = {k: np.asarray(a) for k, a in inputs.items()}

    def chunked(a):
        return a.reshape(a.shape[0] // P, P, -1).transpose(1, 0, 2).reshape(P, -1)

    parts = [chunked(np.concatenate([v["L0_ffn_" + n].T for n in ("Wq", "Wk", "Wv")], axis=1)),
             chunked(v["L0_ffn_Wo"].T), chunked(v["L0_ffn_Wr"].T), chunked(v["L1_ffn_gate_w"].T)]
    for e in range(EXPERTS):
        parts += [chunked(v["L0_ffn_Wg"][e].T), chunked(v["L0_ffn_Wu"][e].T), chunked(v["L0_ffn_Wd"][e].T)]
    for n, m in (("w1", "ws1"), ("w3", "ws3")):
        a = np.concatenate([v["L1_ffn_" + n], v["L1_ffn_" + m][None]], axis=0)
        parts.append(chunked(a.transpose(2, 0, 1).reshape(DIM, -1)))
    a = np.concatenate([v["L1_ffn_w2"], v["L1_ffn_ws2"][None]], axis=0)
    parts.append(a.transpose(2, 0, 1).reshape(P, -1))
    const = _consts()
    for k, n in ((COL_LN1, "L0_ffn_w_ln1"), (COL_LN2, "L0_ffn_w_ln2"), (COL_W, "L1_xattn_w"), (COL_U, "L1_xattn_u")):
        const[:, C_COL + k:C_COL + k + DC] = v[n].reshape(DC, P).T
    arrays = {
        "x": v["x"], "ctx": v["ctx_2048"], "ctx_t": np.ascontiguousarray(v["ctx_2048"].transpose(0, 2, 1)),
        "weights": np.ascontiguousarray(np.concatenate(parts, axis=1)), "const": const,
    }
    nc = bacc.Bacc("TRN2", target_bir_lowering=False, num_devices=1)
    args = [nc.dram_tensor("in_" + k, a.shape, mybir.dt.from_np(a.dtype), kind="ExternalInput").ap() for k, a in arrays.items()]
    out = nc.dram_tensor("out", (BATCH, TOK, DIM), F32, kind="ExternalOutput").ap()
    kernel_body(nc, *args, out)
    r = run_bass_kernel_spmd(nc, [{"in_" + k: a for k, a in arrays.items()}], core_ids=[0])
    return r.results[0]["out"]
```

```python
from contextlib import ExitStack

import concourse.bass as bass
from concourse import mybir

F32 = mybir.dt.float32
F16 = mybir.dt.float16
BF16 = mybir.dt.bfloat16
U32 = mybir.dt.uint32
ACT = mybir.ActivationFunctionType
ALU = mybir.AluOpType
X = mybir.AxisListType.X

P = 128
BATCH, TOK, DIM = 4, 256, 256
TT = TOK // P
DC = DIM // P
HEADS, HD = 16, 16
PAIRS = HEADS // 2
STRIP = 32
EXPERTS = 8
INTER = 512
IC = INTER // P
HID1 = 128
NE1 = EXPERTS + 1
CHUNKS1 = [(0, 4), (4, 4), (8, 1)]
EPS = 1e-5

W_UP = 64.0
A_UP = 64.0
QK_UP = 16.0
H_UP = 16.0
SCORE_DOWN = 1.0 / (QK_UP * QK_UP * HD ** 0.5)
PROD_DOWN = 1.0 / (W_UP * A_UP)
QK_SCALE = (QK_UP, QK_UP * PROD_DOWN)
MASK = 2.0 ** 15

E0 = DC * INTER
OFF_QKV = 0
OFF_WO = OFF_QKV + DC * 3 * DIM
OFF_WR = OFF_WO + DC * DIM
OFF_GW = OFF_WR + DC * EXPERTS
OFF_E = OFF_GW + DC * EXPERTS
OFF_W1 = OFF_E + EXPERTS * 3 * E0
OFF_W3 = OFF_W1 + DC * NE1 * HID1
OFF_W2 = OFF_W3 + DC * NE1 * HID1
W_COLS = OFF_W2 + NE1 * DIM
UNIT = 1024
UNITS = [(OFF_QKV, 768), (OFF_QKV + 768, 768), (OFF_WO, OFF_E - OFF_WO)]
UNITS += [(OFF_E + E0 * k, E0) for k in range(3 * EXPERTS)]
UNITS += [(OFF_W1 + 768 * k, 768) for k in range(9)]
STAGES = 2

C_ID, C_TRIQ, C_TRIK, C_COL = 0, P, 2 * P, 3 * P
COL_LN1, COL_LN2, COL_W, COL_U, COL_IOTA, COL_HALF = 2, 4, 6, 8, 10, 18
C_SEL = 3 * P + 22
N_SEL = 16
C_COLS = C_SEL + N_SEL * P


DVE_LOOP = 72

POOL_LN2, POOL_BASE, POOL_LN1 = 8, 17, 19

STAGES_OF = {
    "first": ("att",), "second": ("att", "moe"), "loop": ("att", "moe", "back"),
    "fifth": ("moe", "back"), "last": ("back",),
}
LOOPS = BATCH - 2

PIECES = []
for _e in range(EXPERTS):
    PIECES += [("g", 2 * _e), ("g", 2 * _e + 1)] + [("d", _e - 1)] * (_e > 0)
PIECES.append(("d", EXPERTS - 1))
PLACES = {"start": 1, "rows": 1, "00": 4, "01": 4, "sum": 3, "qkv": 1, "stack": 1, "10": 4, "11": 4, "tail": 1}
assert sum(PLACES.values()) == len(PIECES)


def pieces(place):
    before = 0
    for name, n in PLACES.items():
        if name == place:
            return PIECES[before:before + n]
        before += n


class Turn:

    def __init__(self, mode, j=0):
        self.mode, self.j = mode, j
        self.att, self.moe, self.back = (s in STAGES_OF[mode] for s in ("att", "moe", "back"))


class Signal:

    def __init__(self, sem, events, start=0):
        self.sem, self.start = sem, start
        self.order = {mode: [n for s, n in events if s in stages] for mode, stages in STAGES_OF.items()}

    def before(self, turn):
        n = self.start
        for mode in STAGES_OF:
            if mode == turn.mode:
                break
            n += len(self.order[mode]) * (LOOPS if mode == "loop" else 1)
        if turn.mode == "loop":
            return n + turn.j * len(self.order["loop"])
        return n

    def at(self, turn, name):
        return self.before(turn) + (self.order[turn.mode].index(name) + 1)


class Ring:

    def __init__(self, banks, filled, used, events):
        self.banks = banks
        self.filled, self.used = Signal(filled, events), Signal(used, events, start=2)
        assert len(self.filled.order["loop"]) % 2 == 0

    def __call__(self, turn, name):
        first = self.filled.before(Turn(turn.mode))
        return self.banks[(first + self.filled.order[turn.mode].index(name)) % 2]


class Steps:

    def __init__(self, eng, sem, loop):
        self.eng, self.sem, self.loop = eng, sem, loop
        self.n, self.base = 0, 0

    def turn(self, turn, before=0):
        self.base = before + turn.j * self.loop if turn.mode == "loop" else before
        self.n = 0

    def done(self, ins):
        self.n += 1
        ins.then_inc(self.sem, 1)

    def wait(self):
        self.eng.wait_ge(self.sem, self.base + self.n)


def ring_events():
    turn_b, act_b, dve_b, sum_b = [], [], [], []

    def fill(place):
        for kind, k in pieces(place):
            if kind == "g":
                act_b.append(("moe", f"g{k}"))
                dve_b.append(("moe", f"u{k}"))
            else:
                sum_b.append(("moe", f"d{k}"))

    fill("start")
    turn_b.extend(("att", n) for n in ("a0q", "a0k"))
    fill("rows")
    for a in range(2):
        if a == 1:
            fill("sum")
            turn_b.append(("att", "xn1"))
            fill("qkv")
            turn_b.extend(("att", n) for n in ("a1q", "a1k"))
            act_b.extend(("att", n) for n in ("v0", "v1"))
            fill("stack")
        for half in range(2):
            dve_b.extend(("att", f"a{a}q{n}") for n in (2 * half, 2 * half + 1))
            act_b.extend(("att", f"a{a}k{n}") for n in (2 * half, 2 * half + 1))
            for i, (kind, k) in enumerate(pieces(f"{a}{half}")):
                if kind == "g":
                    act_b.append(("moe", f"g{k}"))
                    dve_b.append(("moe", f"u{k}"))
                else:
                    sum_b.append(("moe", f"d{k}"))
                if i < 3:
                    dve_b.extend(("att", f"a{a}s{6 * half + n}") for n in (2 * i, 2 * i + 1))
            turn_b.append(("att", f"a{a}n{half}"))
            if half == 0:
                turn_b.extend([[("back", "kT0")], [("back", "yT0"), ("back", "kT1")]][a])
            act_b.extend(("att", f"a{a}p{6 * half + n}") for n in range(6))
            act_b.append(("att", f"a{a}o{half}"))
        turn_b.extend(("att", n) for n in (f"a{a}ot0", f"a{a}ot1"))
    turn_b.append(("back", "yT1"))
    fill("tail")
    turn_b.extend([("att", "hT"), ("back", "x4"), ("back", "gl"), ("att", "xn2"), ("att", "lg")])
    dve_b.extend(("att", n) for n in ("wo0", "wo1"))
    act_b.extend(("back", f"mg{t}{c}") for t in range(TT) for c in range(3))
    dve_b.extend(("back", f"mu{t}{c}") for t in range(TT) for c in range(3))
    turn_b.extend(("back", f"m{t}{c}") for t in range(TT) for c in range(3))
    sum_b.extend(("back", f"md{t}") for t in range(TT))
    return turn_b, act_b, dve_b, sum_b


def kernel_body(nc, x_d, ctx_d, ctxT_d, w_d, c_d, out_d):
    es = ExitStack()
    with es:
        def sb(name, shape, dt=F32):
            return es.enter_context(nc.sbuf_tensor(name, shape, dt))

        def sem(name):
            return es.enter_context(nc.semaphore(name))

        wh = sb("wh", [P, W_COLS], F16)
        wl = sb("wl", [P, W_COLS], F16)
        const = sb("const", [P, C_SEL])
        identb = sb("identb", [P, P], BF16)
        mask_id = sb("mask_id", [P, P], BF16)
        mask_q = sb("mask_q", [P, P], BF16)
        mask_k = sb("mask_k", [P, P], BF16)
        wln = sb("wln", [P, 4])
        spare = sb("spare", [P, 1])
        xin = sb("xin", [P, TT, DIM])
        ctx = sb("ctx", [P, TT, DIM])
        sel_rows = sb("sel_rows", [P, N_SEL, P], F16)
        qbd = sb("qbd", [P, PAIRS // 2, 2, TOK], F16)
        kst = sb("kst", [P, PAIRS // 2, TOK], F16)
        nmx = sb("nmx", [P, TT, P], BF16)
        nmT = sb("nmT", [P, TOK], BF16)
        probs = sb("probs", [P, 6, 512])
        vcols = sb("vcols", [P, TT, HEADS * (HD + 1) + STRIP])
        vaug = vcols[:, :, 0:HEADS * (HD + 1)].rearrange("p t (h d) -> p t h d", h=HEADS)
        att = sb("att", [P, TT, DIM])
        rsum = sb("rsum", [P, TT, HEADS])
        x1 = xin
        z = sb("z", [P, TT, DIM])
        xn = lnq = att
        r2 = z
        xkT = sb("xkT", [P, DC, 4, TOK], F16)
        xT = xkT[:, :, 0:2, :].rearrange("p c s n -> p s c n")
        kT = xkT[:, :, 2:4, :].rearrange("p c s n -> p s c n")
        oT = xkT[:].bitcast(F32).rearrange("p c s n -> p (c s n)").rearrange("p (g n) -> p g n", g=4)
        x0T = sb("x0T", [P, 2, DC, TOK], F16)
        acc = sb("acc", [P, TT, DIM])
        sg = sb("sg", [P, 2, 512])
        hid = sb("hid", [P, 4096], F16)
        hT = hid[:].rearrange("p (s e i n) -> p s e i n", s=2, e=2, i=IC)
        x3 = sb("x3", [P, TT, DIM])
        x4 = sb("x4", [P, TT, DIM])
        kx = x4
        outb = x4
        vT = sb("vT", [P, DC, TOK])
        big = sb("big", [P, 2307])
        stage = [big[:, UNIT * s:UNIT * (s + 1)] for s in range(STAGES)]
        ex = big[:, 0:1024].rearrange("p (k n) -> p k n", k=4)
        ev = big[:, 1024:1536].rearrange("p (k n) -> p k n", k=2)
        omax = big[:, 1536:1793]
        pq = big[:, 1793:2307].rearrange("p (k n) -> p k n", k=2)
        nd = pq[:, :, 0:TOK]
        onew = ev[:, 0, :]
        y = nd[:, 0]
        x4n = big[:, 0:512].rearrange("p (t n) -> p t n", t=TT)
        h1 = big[:, 0:TT * NE1 * HID1].rearrange("p (t n) -> p t n", t=TT)
        x4T = hid[:, 0:1024].rearrange("p (s c n) -> p s c n", s=2, c=DC)
        m16 = hid[:, 1024:1024 + 2 * NE1 * HID1].rearrange("p (s e n) -> p s e n", s=2, e=NE1)

        class Small:

            def __init__(self, name):
                self.stats = sb(name + "_stats", [P, TT, 6])
                self.mv = sb(name + "_mv", [P, TT, 2])
                self.var = sb(name + "_var", [P, 2, TT])
                self.rstd = sb(name + "_rstd", [P, 2, TT])
                self.lg = sb(name + "_lg", [P, TT, EXPERTS])
                self.lgx = sb(name + "_lgx", [P, TT, EXPERTS])
                self.lge = sb(name + "_lge", [P, TT, EXPERTS])
                self.top = sb(name + "_top", [P, TT, 8])
                self.topi = sb(name + "_topi", [P, TT, 8], U32)
                self.topf = sb(name + "_topf", [P, TT, 8])
                self.sel = sb(name + "_sel", [P, 2, TT, EXPERTS])

        sa, sk = Small("att"), Small("back")
        ss = sb("ss", [P, TT])
        den = sb("den", [P, TT])
        rden = sb("rden", [P, TT])
        cw = sb("cw", [P, TT, EXPERTS])
        s12 = sb("s12", [P, TT, EXPERTS])
        sm = sb("sm", [P, TT, EXPERTS])

        ident = const[:, C_ID:C_ID + P]

        def col(k, n=1):
            return const[:, C_COL + k:C_COL + k + n]

        def ring(name, events):
            banks = [es.enter_context(nc.psum_tensor(f"{name}{i}", [P, 512], F32)) for i in range(2)]
            return Ring(banks, sem(name + "_filled"), sem(name + "_used"), events)

        turn_b, act_b, dve_b, sum_b = (ring(n, ev_) for n, ev_ in zip(("turn_b", "act_b", "dve_b", "sum_b"), ring_events()))
        turn_filled, turn_used = turn_b.filled, turn_b.used
        act_filled, act_used = act_b.filled, act_b.used
        dve_filled, dve_used = dve_b.filled, dve_b.used
        sum_filled, sum_used = sum_b.filled, sum_b.used

        def signal(name, stage_, *events):
            return Signal(sem(name), [(stage_, n) for n in events])

        x_loaded = signal("x_loaded", "att", "x")
        ctx_loaded = signal("ctx_loaded", "att", "c")
        v_loaded = signal("v_loaded", "back", "v")
        v_used = signal("v_used", "back", "v0", "v1")
        highs = signal("highs", "att", "a0q", "a0k", "xn1", "a1q", "a1k", "hT", "xn2")
        hid_highs = signal("hid_highs", "moe", *(f"h{k}" for k in range(2 * EXPERTS)))
        back_highs = signal("back_highs", "back", "x4", *(f"m{t}{c}" for t in range(TT) for c in range(3)))
        hid_ready = Signal(sem("hid_ready"), [("moe", f"h{k}") for k in range(2 * EXPERTS)], start=2)
        rows_ready = signal("rows_ready", "att", "a0q", "xn1", "xn2")
        back_rows = signal("back_rows", "back", "kT", "y0", "y1", "x4")
        var_ready = signal("var_ready", "att", "ln1", "ln2", "rms2")
        rstd_ready = signal("rstd_ready", "att", "ln1", "ln2", "rms2")
        back_var = signal("back_var", "back", "ln3", "ln4")
        back_rstd = signal("back_rstd", "back", "ln3", "ln4")
        squares = signal("squares", "att", "r2")
        base_ready = signal("base_ready", "att", "x")
        rt_in = signal("rt_in", "att", "lg")
        rt_exp = signal("rt_exp", "att", "lg")
        back_exp = signal("back_exp", "back", "gl")
        scores_ready = signal("scores_ready", "back", "s")
        wkv_in = signal("wkv_in", "back", "w0", "w1")
        wkv_exp = signal("wkv_exp", "back", "w0", "w1")
        out_free = signal("out_free", "back", "o")
        out_stored = sem("out_stored")
        s_dve = sem("dve_steps")
        s_pool = sem("pool_steps")
        const_loaded = sem("const_loaded")
        sel_loaded = sem("sel_loaded")
        const_ready = sem("const_ready")
        cleared = sem("cleared")
        staged = [sem(f"staged{s}") for s in range(STAGES)]
        w_ready = sem("w_ready")

        def unit_of(col_):
            return max(k for k, (c, _) in enumerate(UNITS) if c <= col_)

        block = es.enter_context(nc.Block())

        @block.sync
        def _(sp):
            def load(b):
                sp.dma_start(xin[:], x_d[b:b + 1].rearrange("o (t p) d -> p (o t) d", p=P)).then_inc(x_loaded.sem, 16)
                sp.dma_start(ctx[:], ctx_d[b:b + 1].rearrange("o (t p) d -> p (o t) d", p=P)).then_inc(ctx_loaded.sem, 16)

            def load_v(b):
                sp.dma_start(vT[:], ctxT_d[b:b + 1].rearrange("o (c p) t -> p (o c) t", p=P)).then_inc(v_loaded.sem, 16)

            def store(turn, b):
                sp.wait_ge(sum_used.sem, sum_used.at(turn, "md1"))
                sp.dma_start(out_d[b:b + 1].rearrange("o (t p) d -> p (o t) d", p=P), outb[:]).then_inc(out_stored, 16)

            sp.dma_start(const[:], c_d[:, 0:C_SEL]).then_inc(const_loaded, 16)
            load(0)
            sp.dma_start(probs[:].rearrange("p k n -> p (k n)")[:, 0:N_SEL * P], c_d[:, C_SEL:C_COLS]).then_inc(sel_loaded, 16)
            load_v(0)
            for k, (c, n) in enumerate(UNITS):
                if k >= STAGES:
                    sp.wait_ge(w_ready, k - STAGES + 1)
                sp.dma_start(stage[k % STAGES][:, 0:n], w_d[:, c:c + n]).then_inc(staged[k % STAGES], 16)
                if k == POOL_BASE:
                    sp.wait_ge(base_ready.sem, base_ready.at(Turn("first"), "x"))
                    load(1)
            sp.sem_inc(out_free.sem, 1)
            sp.wait_ge(base_ready.sem, base_ready.at(Turn("second"), "x"))
            load(2)
            for turn, b in [(Turn("loop", j), j) for j in range(LOOPS)] + [(Turn("fifth"), BATCH - 2)]:
                sp.wait_ge(v_used.sem, v_used.at(turn, "v1"))
                load_v(b + 1)
                if b + 3 < BATCH:
                    sp.wait_ge(base_ready.sem, base_ready.at(turn, "x"))
                    load(b + 3)
                store(turn, b)
                sp.wait_ge(out_stored, b * 16 + 16)
                sp.sem_inc(out_free.sem, 1)
            store(Turn("last"), BATCH - 1)
            sp.wait_ge(out_stored, 16 * BATCH)

        @block.gpsimd
        def _(pool):
            steps = [0]

            def step(ins):
                steps[0] += 1
                ins.then_inc(s_pool, 1)

            def split(k):
                c, n = UNITS[k]
                s = stage[k % STAGES][:, 0:n]
                pool.wait_ge(staged[k % STAGES], 16 * (k // STAGES + 1))
                step(pool.tensor_scalar(wh[:, c:c + n], s, W_UP, 0.0, ALU.mult, ALU.add))
                step(pool.tensor_scalar(s, s, W_UP, 0.0, ALU.mult, ALU.add))
                pool.wait_ge(s_pool, steps[0])
                pool.tensor_tensor(wl[:, c:c + n], s, wh[:, c:c + n], ALU.subtract).then_inc(w_ready, 1)

            half_cols = col(COL_HALF, 4).rearrange("p (k t) -> p k t", k=2)

            def root(turn, name, k=1):
                pool.wait_ge(var_ready.sem, var_ready.at(turn, name))
                pool.tensor_tensor(sa.rstd[:, 0:k, :], sa.var[:, 0:k, :], half_cols[:, 0:k, :], ALU.pow).then_inc(rstd_ready.sem, 1)

            def back_root(turn, name):
                pool.wait_ge(back_var.sem, back_var.at(turn, name))
                pool.tensor_tensor(sk.rstd[:, 0:1, :], sk.var[:, 0:1, :], half_cols[:, 0:1, :], ALU.pow).then_inc(back_rstd.sem, 1)

            def base(turn):
                pool.wait_ge(dve_used.sem, dve_used.at(turn, "wo1"))
                if turn.moe:
                    pool.wait_ge(sum_used.sem, sum_used.at(turn, "d7"))
                pool.tensor_tensor(acc[:], x1[:], r2[:], ALU.add).then_inc(base_ready.sem, 1)

            def roots(turn):
                if turn.att:
                    root(turn, "ln1")
                if turn.back:
                    back_root(turn, "ln3")
                if turn.att:
                    root(turn, "ln2", 2)
                if turn.back:
                    back_root(turn, "ln4")
                if turn.att:
                    root(turn, "rms2")
                    base(turn)

            pool.memset(qbd[:], 0.0).then_inc(cleared, 1)
            pool.memset(vcols[:], 0.0).then_inc(s_pool, 1)
            steps[0] += 1
            pool.memset(nmx[:], 0.0).then_inc(cleared, 1)
            pool.wait_ge(s_pool, 1)
            pool.memset(vaug[:, :, :, HD:HD + 1], 1.0).then_inc(cleared, 1)
            pool.wait_ge(const_loaded, 16)
            first, second = Turn("first"), Turn("second")
            root(first, "ln1")
            for k in range(len(UNITS)):
                if k == POOL_LN2:
                    root(first, "ln2", 2)
                if k == POOL_BASE:
                    root(first, "rms2")
                    base(first)
                if k == POOL_LN1:
                    root(second, "ln1")
                split(k)
            root(second, "ln2", 2)
            root(second, "rms2")
            base(second)
            with pool.Fori(0, LOOPS) as j:
                roots(Turn("loop", j))
            roots(Turn("fifth"))
            roots(Turn("last"))

        @block.scalar
        def _(act):
            def context_values(turn):
                act.wait_ge(ctx_loaded.sem, ctx_loaded.at(turn, "c") * 16)
                act.activation(vaug[:, :, :, 0:HD], ctx[:].rearrange("p t (h d) -> p t h d", h=HEADS), ACT.Copy)

            def rows_high(turn, name, scale, dst, sig):
                act.wait_ge(turn_filled.sem, turn_filled.at(turn, name))
                if isinstance(scale, float):
                    act.activation(dst[:, 0, :, :], turn_b(turn, name)[:].rearrange("p (c n) -> p c n", c=DC), ACT.Copy, scale=scale).then_inc(sig.sem, 1)
                    return
                for c in range(DC):
                    ins = act.activation(dst[:, 0, c, :], turn_b(turn, name)[:, c * TOK:(c + 1) * TOK], ACT.Copy, scale=wln[:, scale + c:scale + c + 1])
                ins.then_inc(sig.sem, 1)

            def stacked_keys(turn, a, half):
                for n in range(2):
                    name = f"a{a}k{2 * half + n}"
                    act.wait_ge(act_filled.sem, act_filled.at(turn, name))
                    act.activation(kst[:, 2 * n:2 * n + 2, :], act_b(turn, name)[:].rearrange("p (h n) -> p h n", h=2), ACT.Copy).then_inc(act_used.sem, 1)

            def probabilities(turn, a, half):
                for k in range(6):
                    name = f"a{a}p{6 * half + k}"
                    act.wait_ge(act_filled.sem, act_filled.at(turn, name))
                    act.activation(probs[:, k, :], act_b(turn, name)[:], ACT.Exp, scale=SCORE_DOWN).then_inc(act_used.sem, 1)
                name = f"a{a}o{half}"
                act.wait_ge(act_filled.sem, act_filled.at(turn, name))
                act.activation(oT[:, 2 * half:2 * half + 2, :], act_b(turn, name)[:].rearrange("p (g n) -> p g n", g=2), ACT.Copy).then_inc(act_used.sem, 1)

            def second_values(turn):
                for t in range(TT):
                    act.wait_ge(act_filled.sem, act_filled.at(turn, f"v{t}"))
                    act.activation(vaug[:, t, :, 0:HD], act_b(turn, f"v{t}")[:, 0:DIM].rearrange("p (h d) -> p h d", h=HEADS), ACT.Copy,
                                   scale=PROD_DOWN).then_inc(act_used.sem, 1)

            def square(turn):
                act.wait_ge(dve_used.sem, dve_used.at(turn, "wo1"))
                for t in range(TT):
                    ins = act.activation(xn[:, t, :], r2[:, t, :], ACT.Square, accum_out=ss[:, t:t + 1])
                ins.then_inc(squares.sem, 1)

            def silu(turn, k):
                act.wait_ge(act_filled.sem, act_filled.at(turn, f"g{k}"))
                act.wait_ge(hid_ready.sem, hid_ready.at(turn, f"h{k}") - 2)
                act.activation(sg[:, k % 2, :], act_b(turn, f"g{k}")[:], ACT.Silu, scale=PROD_DOWN).then_inc(act_used.sem, 1)

            def hidden_high(turn, k):
                act.wait_ge(dve_used.sem, dve_used.at(turn, f"u{k}"))
                act.activation(hT[:, 0, (k // 2) % 2, 2 * (k % 2):2 * (k % 2) + 2, :], sg[:, k % 2, :].rearrange("p (i n) -> p i n", i=2),
                               ACT.Copy).then_inc(hid_highs.sem, 1)

            def experts(turn, kind, k):
                if not turn.moe:
                    return
                if kind == "g":
                    silu(turn, k)
                    if k:
                        hidden_high(turn, k - 1)
                elif k == EXPERTS - 2:
                    hidden_high(turn, 2 * EXPERTS - 1)

            def fill(turn, place):
                for kind, k in pieces(place):
                    experts(turn, kind, k)

            def half_attention(turn, a, half):
                if turn.att:
                    stacked_keys(turn, a, half)
                fill(turn, f"{a}{half}")
                if turn.att:
                    probabilities(turn, a, half)
                if turn.back and half == 0:
                    act.wait_ge(wkv_in.sem, wkv_in.at(turn, f"w{a}"))
                    act.activation(ex[:], ex[:], ACT.Exp).then_inc(wkv_exp.sem, 1)

            def back_gate(turn, t, c):
                e0, n = CHUNKS1[c]
                name = f"mg{t}{c}"
                i = 3 * t + c
                act.wait_ge(act_filled.sem, act_filled.at(turn, name))
                if i >= 2:
                    act.wait_ge(dve_used.sem, dve_used.at(turn, f"mu{(i - 2) // 3}{(i - 2) % 3}"))
                if i == 0:
                    act.wait_ge(scores_ready.sem, scores_ready.at(turn, "s"))
                    if turn.moe:
                        act.wait_ge(hid_ready.sem, hid_ready.at(turn, f"h{2 * EXPERTS - 1}"))
                for e in range(e0, e0 + n):
                    s = s12[:, t, e:e + 1] if e < EXPERTS else PROD_DOWN
                    ins = act.activation(sg[:, i % 2, (e - e0) * P:(e - e0 + 1) * P], act_b(turn, name)[:, (e - e0) * P:(e - e0 + 1) * P],
                                         ACT.Silu, scale=s)
                ins.then_inc(act_used.sem, 1)

            def back_hidden(turn, t):
                for c, (e0, n) in enumerate(CHUNKS1):
                    name = f"m{t}{c}"
                    act.wait_ge(turn_filled.sem, turn_filled.at(turn, name))
                    if t == 1 and c == 0:
                        act.wait_ge(sum_filled.sem, sum_filled.at(turn, "md0"))
                    act.activation(m16[:, 0, e0:e0 + n, :], turn_b(turn, name)[:, 0:n * P].rearrange("p (e n) -> p e n", e=n), ACT.Copy).then_inc(back_highs.sem, 1)

            def turn_program(turn):
                if turn.att:
                    context_values(turn)
                fill(turn, "start")
                if turn.att:
                    rows_high(turn, "a0q", QK_SCALE[0], xT, highs)
                    rows_high(turn, "a0k", QK_SCALE[0], kT, highs)
                fill(turn, "rows")
                half_attention(turn, 0, 0)
                half_attention(turn, 0, 1)
                fill(turn, "sum")
                if turn.att:
                    rows_high(turn, "xn1", 0, xT, highs)
                fill(turn, "qkv")
                if turn.att:
                    second_values(turn)
                    act.wait_ge(turn_filled.sem, turn_filled.at(turn, "a1k"))
                    rows_high(turn, "a1q", QK_SCALE[1], xT, highs)
                    rows_high(turn, "a1k", QK_SCALE[1], kT, highs)
                fill(turn, "stack")
                half_attention(turn, 1, 0)
                half_attention(turn, 1, 1)
                fill(turn, "tail")
                if turn.att:
                    rows_high(turn, "hT", A_UP, xT, highs)
                if turn.back:
                    rows_high(turn, "x4", A_UP, x4T, back_highs)
                if turn.att:
                    square(turn)
                if turn.back:
                    act.wait_ge(turn_used.sem, turn_used.at(turn, "gl"))
                    act.activation(sk.lge[:], sk.lgx[:], ACT.Exp, scale=-1.0).then_inc(back_exp.sem, 1)
                    for c in range(3):
                        back_gate(turn, 0, c)
                if turn.att:
                    rows_high(turn, "xn2", 2, x0T, highs)
                if turn.back:
                    back_gate(turn, 1, 0)
                if turn.att:
                    act.wait_ge(rt_in.sem, rt_in.at(turn, "lg"))
                    act.activation(sa.lge[:], sa.lgx[:], ACT.Exp).then_inc(rt_exp.sem, 1)
                if turn.back:
                    back_gate(turn, 1, 1)
                    back_gate(turn, 1, 2)
                    back_hidden(turn, 0)
                    back_hidden(turn, 1)

            act.sem_inc(act_used.sem, act_used.start)
            act.wait_ge(const_loaded, 16)
            act.activation(identb[:], ident, ACT.Copy)
            act.activation(mask_id[:], ident, ACT.Copy, scale=-MASK)
            act.activation(mask_q[:], const[:, C_TRIQ:C_TRIQ + P], ACT.Copy, scale=MASK)
            act.activation(wln[:], col(COL_LN1, 4), ACT.Copy, scale=A_UP)
            act.activation(mask_k[:], const[:, C_TRIK:C_TRIK + P], ACT.Copy, scale=MASK).then_inc(const_ready, 1)
            act.wait_ge(sel_loaded, 16)
            act.activation(sel_rows[:], probs[:].rearrange("p k n -> p (k n)")[:, 0:N_SEL * P].rearrange("p (s n) -> p s n", s=N_SEL), ACT.Copy).then_inc(const_ready, 1)
            act.wait_ge(const_ready, 2)
            act.wait_ge(cleared, 3)
            turn_program(Turn("first"))
            turn_program(Turn("second"))
            with act.Fori(0, LOOPS) as j:
                turn_program(Turn("loop", j))
            turn_program(Turn("fifth"))
            turn_program(Turn("last"))

        @block.vector
        def _(dve):
            st = Steps(dve, s_dve, DVE_LOOP)

            def stand_alone():
                dve.memset(spare[:], 0.0)

            def row_stats(b, src):
                for t in range(TT):
                    st.done(dve.bn_stats(b.stats[:, t, :], src[:, t, :]))
                st.wait()
                stand_alone()
                for t in range(TT):
                    st.done(dve.bn_aggr(b.mv[:, t, :], b.stats[:, t, :]))
                st.wait()

            def normed(b, dst, src, k=0):
                for t in range(TT):
                    ins = dve.tensor_scalar(dst[:, t, :], src[:, t, :], b.mv[:, t, 0:1], b.rstd[:, k, t:t + 1], ALU.subtract, ALU.mult)
                return ins

            def ln1_stats(turn):
                dve.wait_ge(x_loaded.sem, x_loaded.at(turn, "x") * 16)
                row_stats(sa, xin)
                dve.tensor_scalar(sa.var[:, 0, :], sa.mv[:, :, 1], EPS, None, ALU.add).then_inc(var_ready.sem, 1)

            def ln1_rows(turn):
                dve.wait_ge(rstd_ready.sem, rstd_ready.at(turn, "ln1"))
                normed(sa, lnq, xin).then_inc(rows_ready.sem, 1)

            def place_queries(turn, a, half):
                for n in range(2):
                    name = f"a{a}q{2 * half + n}"
                    dve.wait_ge(dve_filled.sem, dve_filled.at(turn, name))
                    for ab in range(2):
                        r = slice(64 * ab, 64 * ab + 64)
                        ins = dve.tensor_copy(qbd[r, 2 * n:2 * n + 2, ab, :], dve_b(turn, name)[r, :].rearrange("p (h n) -> p h n", h=2))
                    ins.then_inc(dve_used.sem, 1)

            def score_max(turn, a, half, k):
                name = f"a{a}s{6 * half + k}"
                t, h, n = (0, 4 * k, 4) if k < 2 else (1, 2 * (k - 2), 2)
                dve.wait_ge(dve_filled.sem, dve_filled.at(turn, name))
                dve.tensor_reduce(nmx[:, t, h:h + n], dve_b(turn, name)[:].rearrange("p (h n) -> p h n", h=n), X, ALU.max,
                                  negate=True).then_inc(dve_used.sem, 1)

            def outputs(turn, a):
                for t in range(TT):
                    name = f"a{a}ot{t}"
                    dve.wait_ge(turn_filled.sem, turn_filled.at(turn, name))
                    o = turn_b(turn, name)[:].rearrange("p (h d) -> p h d", h=HEADS)
                    st.done(dve.reciprocal(rsum[:, t, :], o[:, :, HD]))
                    st.wait()
                    dve.tensor_tensor(att[:, t, :].rearrange("p (h d) -> p h d", h=HEADS), o[:, :, 0:HD],
                                      rsum[:, t, :].unsqueeze(2).broadcast_to([P, HEADS, HD]), ALU.mult).then_inc(turn_used.sem, 1)

            def first_sum(turn):
                dve.wait_ge(turn_used.sem, turn_used.at(turn, "a0ot1"))
                st.done(dve.tensor_tensor(x1[:], xin[:], att[:], ALU.add))
                st.wait()
                row_stats(sa, x1)
                st.done(dve.tensor_scalar(sa.var[:, 0, :], sa.mv[:, :, 1], EPS, None, ALU.add))
                dve.tensor_scalar(sa.var[:, 1, :], sa.mv[:, :, 1], 1 + EPS, EPS * EPS, ALU.mult, ALU.add).then_inc(var_ready.sem, 1)
                dve.wait_ge(rstd_ready.sem, rstd_ready.at(turn, "ln2"))
                normed(sa, xn, x1, 1).then_inc(rows_ready.sem, 1)
                st.done(normed(sa, z, x1, 0))

            def rows_low(turn, name, scale, dst, sig):
                dve.wait_ge(sig.sem, sig.at(turn, name))
                if isinstance(scale, float):
                    dve.scalar_tensor_tensor(dst[:, 1, :, :], turn_b(turn, name)[:].rearrange("p (c n) -> p c n", c=DC), scale, dst[:, 0, :, :],
                                             ALU.mult, ALU.subtract).then_inc(turn_used.sem, 1)
                    return
                for c in range(DC):
                    ins = dve.scalar_tensor_tensor(dst[:, 1, c, :], turn_b(turn, name)[:, c * TOK:(c + 1) * TOK], wln[:, scale + c:scale + c + 1],
                                                   dst[:, 0, c, :], ALU.mult, ALU.subtract)
                ins.then_inc(turn_used.sem, 1)

            def second_sum(turn):
                for t in range(TT):
                    dve.wait_ge(dve_filled.sem, dve_filled.at(turn, f"wo{t}"))
                    if t == 0:
                        st.wait()
                    dve.scalar_tensor_tensor(r2[:, t, :], dve_b(turn, f"wo{t}")[:, 0:DIM], PROD_DOWN, z[:, t, :], ALU.mult,
                                             ALU.add).then_inc(dve_used.sem, 1)

            def mean_squares(turn):
                dve.wait_ge(squares.sem, squares.at(turn, "r2"))
                dve.tensor_scalar(sa.var[:, 0, :], ss[:], 1 / DIM, EPS, ALU.mult, ALU.add).then_inc(var_ready.sem, 1)

            def rms_rows(turn):
                dve.wait_ge(rstd_ready.sem, rstd_ready.at(turn, "rms2"))
                dve.wait_ge(dve_used.sem, dve_used.at(turn, "wo1"))
                for t in range(TT):
                    ins = dve.tensor_scalar(xn[:, t, :], r2[:, t, :], sa.rstd[:, 0, t:t + 1], None, ALU.mult)
                ins.then_inc(rows_ready.sem, 1)

            def top2(b):
                stand_alone()
                for t in range(TT):
                    st.done(dve.max(b.top[:, t, :], b.lg[:, t, :]))
                st.wait()
                stand_alone()
                for t in range(TT):
                    st.done(dve.max_index(b.topi[:, t, :], b.top[:, t, :], b.lg[:, t, :]))
                st.wait()
                st.done(dve.tensor_copy(b.topf[:], b.topi[:]))
                st.wait()
                iota = col(COL_IOTA, 8).unsqueeze(1).broadcast_to([P, TT, EXPERTS])
                for k in range(2):
                    st.done(dve.tensor_tensor(b.sel[:, k], iota, b.topf[:, :, k:k + 1].broadcast_to([P, TT, EXPERTS]), ALU.is_equal))
                st.wait()
                st.done(dve.tensor_tensor(b.sel[:, 0], b.sel[:, 0], b.sel[:, 1], ALU.add))
                st.wait()

            def router(turn):
                b = sa
                dve.wait_ge(turn_filled.sem, turn_filled.at(turn, "lg"))
                dve.tensor_scalar(b.lg[:], turn_b(turn, "lg")[:, 0:TT * EXPERTS].rearrange("p (t e) -> p t e", t=TT), PROD_DOWN, None,
                                  ALU.mult).then_inc(turn_used.sem, 1)
                dve.wait_ge(turn_used.sem, turn_used.at(turn, "lg"))
                top2(b)
                dve.tensor_tensor(b.lgx[:], b.lg[:], b.top[:, :, 0:1].broadcast_to([P, TT, EXPERTS]), ALU.subtract).then_inc(rt_in.sem, 1)
                dve.wait_ge(rt_exp.sem, rt_exp.at(turn, "lg"))
                st.done(dve.tensor_tensor(b.lge[:], b.lge[:], b.sel[:, 0], ALU.mult))
                st.wait()
                st.done(dve.tensor_reduce(den[:], b.lge[:], X, ALU.add))
                st.wait()
                st.done(dve.reciprocal(rden[:], den[:]))
                st.wait()
                if turn.moe:
                    dve.wait_ge(sum_used.sem, sum_used.at(turn, f"d{EXPERTS - 1}"))
                st.done(dve.scalar_tensor_tensor(cw[:], b.lge[:], 1 / (H_UP * W_UP), rden[:].unsqueeze(2).broadcast_to([P, TT, EXPERTS]),
                                                 ALU.mult, ALU.mult))
                st.wait()

            def hidden(turn, k):
                dve.wait_ge(dve_filled.sem, dve_filled.at(turn, f"u{k}"))
                dve.wait_ge(act_used.sem, act_used.at(turn, f"g{k}"))
                dve.scalar_tensor_tensor(sg[:, k % 2, :], dve_b(turn, f"u{k}")[:], H_UP * PROD_DOWN, sg[:, k % 2, :], ALU.mult,
                                         ALU.mult).then_inc(dve_used.sem, 1)

            def hidden_low(turn, k):
                dve.wait_ge(hid_highs.sem, hid_highs.at(turn, f"h{k}"))
                dve.tensor_tensor(hT[:, 1, (k // 2) % 2, 2 * (k % 2):2 * (k % 2) + 2, :], sg[:, k % 2, :].rearrange("p (i n) -> p i n", i=2),
                                  hT[:, 0, (k // 2) % 2, 2 * (k % 2):2 * (k % 2) + 2, :], ALU.subtract).then_inc(hid_ready.sem, 1)

            def add_expert(turn, e):
                dve.wait_ge(sum_filled.sem, sum_filled.at(turn, f"d{e}"))
                if e == 0:
                    dve.wait_ge(base_ready.sem, base_ready.before(turn))
                else:
                    dve.wait_ge(sum_used.sem, sum_used.at(turn, f"d{e - 1}"))
                dst = x3 if e == EXPERTS - 1 else acc
                for t in range(TT):
                    ins = dve.scalar_tensor_tensor(dst[:, t, :], sum_b(turn, f"d{e}")[:, t * DIM:(t + 1) * DIM], cw[:, t, e:e + 1], acc[:, t, :],
                                                   ALU.mult, ALU.add)
                ins.then_inc(sum_used.sem, 1)

            def experts(turn, kind, k):
                if not turn.moe:
                    return
                if kind == "g":
                    hidden(turn, k)
                    if k:
                        hidden_low(turn, k - 1)
                else:
                    if k == EXPERTS - 2:
                        hidden_low(turn, 2 * EXPERTS - 1)
                    add_expert(turn, k)

            def fill(turn, place):
                for kind, k in pieces(place):
                    experts(turn, kind, k)

            def wkv_norm(turn):
                dve.wait_ge(sum_used.sem, sum_used.before(turn))
                row_stats(sk, x3)
                dve.tensor_scalar(sk.var[:, 0, :], sk.mv[:, :, 1], EPS, None, ALU.add).then_inc(back_var.sem, 1)

            def wkv_rows(turn):
                dve.wait_ge(out_free.sem, out_free.at(turn, "o"))
                dve.wait_ge(back_rstd.sem, back_rstd.at(turn, "ln3"))
                normed(sk, kx, x3).then_inc(back_rows.sem, 1)

            def wkv_exponents(turn, c):
                dve.wait_ge(w_ready, len(UNITS))
                dve.wait_ge(turn_filled.sem, turn_filled.at(turn, f"kT{c}"))
                k = turn_b(turn, f"kT{c}")[:, 0:TOK]
                w, u = col(COL_W + c), col(COL_U + c)
                st.done(dve.memset(omax[:, 0:1], -1e38))
                st.done(dve.memset(pq[:, :, 0:1], 0.0))
                st.done(dve.tensor_tensor_scan(omax[:, 1:TOK + 1], w.broadcast_to([P, TOK]), k, -1e38, ALU.add, ALU.max))
                st.wait()
                st.done(dve.scalar_tensor_tensor(onew, k, u, omax[:, 0:TOK], ALU.add, ALU.max))
                st.done(dve.scalar_tensor_tensor(ex[:, 1], omax[:, 0:TOK], w, omax[:, 1:TOK + 1], ALU.add, ALU.subtract))
                st.wait()
                st.done(dve.tensor_tensor(ex[:, 0], omax[:, 0:TOK], onew, ALU.subtract))
                st.done(dve.scalar_tensor_tensor(ex[:, 2], k, u, onew, ALU.add, ALU.subtract))
                dve.tensor_tensor(ex[:, 3], k, omax[:, 1:TOK + 1], ALU.subtract).then_inc(turn_used.sem, 1)
                dve.wait_ge(turn_used.sem, turn_used.at(turn, f"kT{c}"))
                dve.sem_inc(wkv_in.sem, 1)

            def wkv_scan(turn, c):
                dve.wait_ge(wkv_exp.sem, wkv_exp.at(turn, f"w{c}"))
                dve.wait_ge(v_loaded.sem, v_loaded.at(turn, "v") * 16)
                dve.tensor_tensor(ev, ex[:, 2:4, :], vT[:, c, :].unsqueeze(1).broadcast_to([P, 2, TOK]), ALU.mult).then_inc(v_used.sem, 1)
                dve.wait_ge(v_used.sem, v_used.at(turn, f"v{c}"))
                st.done(dve.tensor_tensor_scan(pq[:, 0, 1:TOK + 1], ex[:, 1], ev[:, 1], 0.0, ALU.mult, ALU.add))
                st.done(dve.tensor_tensor_scan(pq[:, 1, 1:TOK + 1], ex[:, 1], ex[:, 3], 0.0, ALU.mult, ALU.add))
                st.wait()

            def wkv_out(turn, c):
                st.done(dve.tensor_tensor(nd, ex[:, 0].unsqueeze(1).broadcast_to([P, 2, TOK]), nd, ALU.mult))
                st.wait()
                st.done(dve.tensor_tensor(nd[:, 1], nd[:, 1], ex[:, 2], ALU.add))
                st.done(dve.tensor_tensor(nd[:, 0], nd[:, 0], ev[:, 0], ALU.add))
                st.wait()
                st.done(dve.reciprocal(nd[:, 1], nd[:, 1]))
                st.wait()
                dve.tensor_tensor(y, nd[:, 0], nd[:, 1], ALU.mult).then_inc(back_rows.sem, 1)

            def third_sum(turn, c):
                dve.wait_ge(turn_filled.sem, turn_filled.at(turn, f"yT{c}"))
                dve.tensor_tensor(x4[:, :, c * P:(c + 1) * P], x3[:, :, c * P:(c + 1) * P],
                                  turn_b(turn, f"yT{c}")[:, 0:TOK].rearrange("p (t n) -> p t n", t=TT), ALU.add).then_inc(turn_used.sem, 1)

            def last_stats(turn):
                dve.wait_ge(turn_used.sem, turn_used.at(turn, "yT1"))
                row_stats(sk, x4)
                dve.tensor_scalar(sk.var[:, 0, :], sk.mv[:, :, 1], EPS, None, ALU.add).then_inc(back_var.sem, 1)

            def last_rows(turn):
                dve.wait_ge(back_rstd.sem, back_rstd.at(turn, "ln4"))
                normed(sk, x4n, x4).then_inc(back_rows.sem, 1)

            def back_scores(turn):
                b = sk
                dve.wait_ge(back_exp.sem, back_exp.at(turn, "gl"))
                st.done(dve.tensor_scalar(b.lge[:], b.lge[:], 1.0, None, ALU.add))
                st.wait()
                st.done(dve.reciprocal(b.lg[:], b.lge[:]))
                st.wait()
                dve.tensor_scalar(s12[:], b.lg[:], PROD_DOWN, None, ALU.mult).then_inc(scores_ready.sem, 1)
                top2(b)
                st.done(dve.scalar_tensor_tensor(sm[:], b.lg[:], H_UP * PROD_DOWN, b.sel[:, 0], ALU.mult, ALU.mult))
                st.wait()

            def back_up(turn, t, c):
                e0, n = CHUNKS1[c]
                name = f"mu{t}{c}"
                dve.wait_ge(dve_filled.sem, dve_filled.at(turn, name))
                dve.wait_ge(act_used.sem, act_used.at(turn, f"mg{t}{c}"))
                for e in range(e0, e0 + n):
                    s = sm[:, t, e:e + 1] if e < EXPERTS else H_UP * PROD_DOWN
                    r = slice((e - e0) * P, (e - e0 + 1) * P)
                    ins = dve.scalar_tensor_tensor(h1[:, t, e * P:(e + 1) * P], dve_b(turn, name)[:, r], s, sg[:, (3 * t + c) % 2, r], ALU.mult, ALU.mult)
                ins.then_inc(dve_used.sem, 1)

            def back_down(turn, t):
                for c, (e0, n) in enumerate(CHUNKS1):
                    name = f"m{t}{c}"
                    dve.wait_ge(back_highs.sem, back_highs.at(turn, name))
                    dve.tensor_tensor(m16[:, 1, e0:e0 + n, :], turn_b(turn, name)[:, 0:n * P].rearrange("p (e n) -> p e n", e=n),
                                      m16[:, 0, e0:e0 + n, :], ALU.subtract).then_inc(turn_used.sem, 1)

            def last_sum(turn, t):
                dve.wait_ge(sum_filled.sem, sum_filled.at(turn, f"md{t}"))
                dve.scalar_tensor_tensor(outb[:, t, :], sum_b(turn, f"md{t}")[:, 0:DIM], 1 / (H_UP * W_UP), x4[:, t, :], ALU.mult,
                                         ALU.add).then_inc(sum_used.sem, 1)

            def half_attention(turn, a, half):
                if turn.att:
                    place_queries(turn, a, half)
                for i, (kind, k) in enumerate(pieces(f"{a}{half}")):
                    experts(turn, kind, k)
                    if turn.att and i < 3:
                        score_max(turn, a, half, 2 * i)
                        score_max(turn, a, half, 2 * i + 1)
                if turn.att:
                    name = f"a{a}n{half}"
                    dve.wait_ge(turn_filled.sem, turn_filled.at(turn, name))
                    dve.tensor_copy(nmT[:], turn_b(turn, name)[:].bitcast(BF16)[:, 0:TOK]).then_inc(turn_used.sem, 1)
                if turn.back:
                    if half == 0:
                        if a == 1:
                            third_sum(turn, 0)
                        wkv_exponents(turn, a)
                    else:
                        wkv_scan(turn, a)
                        wkv_out(turn, a)

            def turn_program(turn):
                if turn.att:
                    ln1_stats(turn)
                if turn.back:
                    wkv_norm(turn)
                if turn.att:
                    ln1_rows(turn)
                if turn.back:
                    wkv_rows(turn)
                fill(turn, "start")
                if turn.att:
                    rows_low(turn, "a0q", QK_SCALE[0], xT, highs)
                    rows_low(turn, "a0k", QK_SCALE[0], kT, highs)
                fill(turn, "rows")
                half_attention(turn, 0, 0)
                half_attention(turn, 0, 1)
                if turn.att:
                    outputs(turn, 0)
                    first_sum(turn)
                fill(turn, "sum")
                if turn.att:
                    rows_low(turn, "xn1", 0, xT, highs)
                fill(turn, "qkv")
                if turn.att:
                    rows_low(turn, "a1q", QK_SCALE[1], xT, highs)
                    rows_low(turn, "a1k", QK_SCALE[1], kT, highs)
                fill(turn, "stack")
                half_attention(turn, 1, 0)
                half_attention(turn, 1, 1)
                if turn.att:
                    outputs(turn, 1)
                if turn.back:
                    third_sum(turn, 1)
                    last_stats(turn)
                fill(turn, "tail")
                if turn.att:
                    rows_low(turn, "hT", A_UP, xT, highs)
                if turn.back:
                    last_rows(turn)
                    rows_low(turn, "x4", A_UP, x4T, back_highs)
                if turn.att:
                    second_sum(turn)
                    mean_squares(turn)
                if turn.back:
                    dve.wait_ge(turn_filled.sem, turn_filled.at(turn, "gl"))
                    dve.tensor_scalar(sk.lgx[:], turn_b(turn, "gl")[:, 0:TT * EXPERTS].rearrange("p (t e) -> p t e", t=TT), PROD_DOWN, None,
                                      ALU.mult).then_inc(turn_used.sem, 1)
                if turn.att:
                    rms_rows(turn)
                if turn.back:
                    back_scores(turn)
                    for c in range(3):
                        back_up(turn, 0, c)
                if turn.att:
                    rows_low(turn, "xn2", 2, x0T, highs)
                if turn.back:
                    back_up(turn, 1, 0)
                if turn.att:
                    router(turn)
                if turn.back:
                    back_up(turn, 1, 1)
                    back_up(turn, 1, 2)
                    back_down(turn, 0)
                    back_down(turn, 1)
                    last_sum(turn, 0)
                    last_sum(turn, 1)

            for used in (turn_used, dve_used, sum_used):
                dve.sem_inc(used.sem, used.start)
            dve.sem_inc(hid_ready.sem, hid_ready.start)
            dve.wait_ge(const_ready, 2)
            dve.wait_ge(cleared, 3)
            before = 0
            for mode in ("first", "second"):
                st.turn(Turn(mode), before)
                turn_program(Turn(mode))
                before += st.n
            with dve.Fori(0, LOOPS) as j:
                st.turn(Turn("loop", j), before)
                turn_program(Turn("loop", j))
                assert st.n == DVE_LOOP, st.n
            before += LOOPS * DVE_LOOP
            for mode in ("fifth", "last"):
                st.turn(Turn(mode), before)
                turn_program(Turn(mode))
                before += st.n

        @block.tensor
        def _(pe):
            def split_product(out, terms, low_low=False):
                mm = [(l, r) for lhs, rhs in terms for l, r in ([(lhs[0], rhs[0]), (lhs[0], rhs[1]), (lhs[1], rhs[0])] + [(lhs[1], rhs[1])] * low_low)]
                for i, (l, r) in enumerate(mm):
                    ins = pe.matmul(out, l, r, start=(i == 0), stop=(i == len(mm) - 1))
                return ins

            def w_pair(off, n):
                return wh[:, off:off + n], wl[:, off:off + n]

            def weights(turn, off):
                if turn.mode in ("first", "second") or off >= OFF_W1:
                    pe.wait_ge(w_ready, unit_of(off - 1) + 1)

            def stack_rows(turn, a, s, n):
                name = f"a{a}{s}{n}"
                src, k, bank, filled, used = (xT, 0, dve_b, dve_filled, dve_used) if s == "q" else (kT, 2, act_b, act_filled, act_used)
                pe.wait_ge(used.sem, used.at(turn, name) - 2)
                pe.wait_ge(turn_used.sem, turn_used.at(turn, f"a{a}{s}"))
                for i in range(2):
                    for part in range(2):
                        ins = pe.matmul(bank(turn, name)[:, i * TOK:(i + 1) * TOK], sel_rows[:, 4 * (k + part) + (2 * n + i) % 4, :], src[:, part, n // 2, :],
                                        start=(i + part == 0), stop=(i + part == 2), skip_group_check=True)
                ins.then_inc(filled.sem, 1)

            def scores(turn, a, half, k):
                name = f"a{a}s{6 * half + k}"
                pe.wait_ge(dve_used.sem, dve_used.at(turn, name) - 2)
                t, h0, n, keys = (0, 4 * k, 4, P) if k < 2 else (1, 2 * (k - 2), 2, TOK)
                if k == 0:
                    pe.wait_ge(dve_used.sem, dve_used.at(turn, f"a{a}q{2 * half + 1}"))
                    pe.wait_ge(act_used.sem, act_used.at(turn, f"a{a}k{2 * half + 1}"))
                bank = dve_b(turn, name)[:].rearrange("p (h n) -> p h n", h=n)
                for i in range(n):
                    hp, ab = divmod(h0 + i, 2)
                    pe.matmul(bank[:, i, :], qbd[:, hp, ab, t * P:(t + 1) * P], kst[:, hp, 0:keys], start=(i == 0), stop=False, skip_group_check=True)
                pe.matmul(bank[:, :, keys - P:keys], mask_id[:], mask_q[:].unsqueeze(1).broadcast_to([P, n, P]), start=False,
                          stop=True, skip_group_check=True).then_inc(dve_filled.sem, 1)

            def turn_max(turn, a, half):
                name = f"a{a}n{half}"
                pe.wait_ge(turn_used.sem, turn_used.at(turn, name) - 2)
                pe.wait_ge(dve_used.sem, dve_used.at(turn, f"a{a}s{6 * half + 5}"))
                for t in range(TT):
                    ins = pe.transpose(turn_b(turn, name)[:].bitcast(BF16)[:, t * P:(t + 1) * P], nmx[:, t, :], identb[:])
                ins.then_inc(turn_filled.sem, 1)

            def exponents(turn, a, g):
                half = g // 2
                if g % 2 == 0:
                    pe.wait_ge(turn_used.sem, turn_used.at(turn, f"a{a}n{half}"))
                for i in range(3):
                    name = f"a{a}p{3 * g + i}"
                    pe.wait_ge(act_used.sem, act_used.at(turn, name) - 2)
                    q0 = 0 if i < 2 else P
                    h0 = 4 * (g % 2) + (2 * i if i < 2 else 0)
                    heads = range(h0, h0 + (2 if i < 2 else 4))
                    bank = act_b(turn, name)[:].rearrange("p (h n) -> p h n", h=len(heads))
                    for hp in range(heads[0] // 2, heads[-1] // 2 + 1):
                        r = 2 * hp - heads[0]
                        pe.matmul(bank[:, r:r + 2, :], kst[:, hp, q0:q0 + P], qbd[:, hp, :, q0:TOK], start=(r == 0), stop=False, skip_group_check=True)
                    for r, h in enumerate(heads):
                        pe.matmul(bank[:, r, :], identb[:, h:h + 1].broadcast_to([P, P]), nmT[:, q0:TOK],
                                  start=False, stop=False, skip_group_check=True)
                    pe.matmul(bank[:, :, 0:P], mask_id[:], mask_k[:].unsqueeze(1).broadcast_to([P, len(heads), P]), start=False, stop=True,
                              skip_group_check=True).then_inc(act_filled.sem, 1)

            def values(turn, a, g):
                o = f"a{a}o{g // 2}"
                if g % 2 == 0:
                    pe.wait_ge(act_used.sem, act_used.at(turn, o) - 2)
                pe.wait_ge(act_used.sem, act_used.at(turn, f"a{a}p{3 * g + 2}"))
                for j in range(4):
                    h = 4 * g + j
                    s = 3 * (g % 2)
                    out = act_b(turn, o)[STRIP * j:STRIP * (j + 1), (g % 2) * TOK:(g % 2 + 1) * TOK]
                    pe.matmul(out, vcols[:, 0, h * (HD + 1):h * (HD + 1) + STRIP], probs[:, s + j // 2, (j % 2) * TOK:(j % 2 + 1) * TOK], start=True, stop=False, skip_group_check=True)
                    ins = pe.matmul(out[:, P:TOK], vcols[:, 1, h * (HD + 1):h * (HD + 1) + STRIP], probs[:, s + 2, j * P:(j + 1) * P], start=False, stop=True, skip_group_check=True)
                if g % 2:
                    ins.then_inc(act_filled.sem, 1)

            def outputs(turn, a):
                for t in range(TT):
                    name = f"a{a}ot{t}"
                    pe.wait_ge(turn_used.sem, turn_used.at(turn, name) - 2)
                    if t == 0:
                        pe.wait_ge(act_used.sem, act_used.at(turn, f"a{a}o1"))
                    for g in range(4):
                        ins = pe.transpose(turn_b(turn, name)[:, g * P:(g + 1) * P], oT[:, g, t * P:(t + 1) * P], ident)
                    ins.then_inc(turn_filled.sem, 1)

            def turn_rows(turn, name, src):
                pe.wait_ge(turn_used.sem, turn_used.at(turn, name) - 2)
                if name == "hT":
                    pe.wait_ge(turn_used.sem, turn_used.at(turn, "a1ot1"))
                elif name == "a0k":
                    pe.wait_ge(ctx_loaded.sem, ctx_loaded.at(turn, "c") * 16)
                elif name == "x4":
                    pe.wait_ge(back_rows.sem, back_rows.at(turn, name))
                else:
                    pe.wait_ge(rows_ready.sem, rows_ready.at(turn, name))
                for c in range(DC):
                    for t in range(TT):
                        ins = pe.transpose(turn_b(turn, name)[:, c * TOK + t * P:c * TOK + (t + 1) * P], src[:, t, c * P:(c + 1) * P], ident)
                ins.then_inc(turn_filled.sem, 1)

            def rows_pair(xT_, c, t):
                return xT_[:, 0, c, t * P:(t + 1) * P], xT_[:, 1, c, t * P:(t + 1) * P]

            def qkv(turn):
                pe.wait_ge(turn_used.sem, turn_used.at(turn, "xn1"))
                weights(turn, OFF_WO)
                for t in range(TT):
                    pe.wait_ge(act_used.sem, act_used.at(turn, f"v{t}") - 2)
                    split_product(act_b(turn, f"v{t}")[:, 0:DIM], [(rows_pair(xT, c, t), w_pair(OFF_QKV + c * 3 * DIM + 2 * DIM, DIM)) for c in range(DC)])\
                        .then_inc(act_filled.sem, 1)
                for m, name in enumerate(("a1q", "a1k")):
                    pe.wait_ge(turn_used.sem, turn_used.at(turn, name) - 2)
                    for o in range(DC):
                        ins = split_product(turn_b(turn, name)[:, o * TOK:(o + 1) * TOK],
                                            [(w_pair(OFF_QKV + c * 3 * DIM + m * DIM + o * P, P), (xT[:, 0, c, :], xT[:, 1, c, :])) for c in range(DC)])
                    ins.then_inc(turn_filled.sem, 1)

            def out_projection(turn):
                pe.wait_ge(turn_used.sem, turn_used.at(turn, "hT"))
                weights(turn, OFF_WR)
                for t in range(TT):
                    pe.wait_ge(dve_used.sem, dve_used.at(turn, f"wo{t}") - 2)
                    split_product(dve_b(turn, f"wo{t}")[:, 0:DIM], [(rows_pair(xT, c, t), w_pair(OFF_WO + c * DIM, DIM)) for c in range(DC)])\
                        .then_inc(dve_filled.sem, 1)

            def logits(turn, name, rows, xT_, off):
                pe.wait_ge(turn_used.sem, turn_used.at(turn, rows))
                weights(turn, OFF_E)
                pe.wait_ge(turn_used.sem, turn_used.at(turn, name) - 2)
                for t in range(TT):
                    ins = split_product(turn_b(turn, name)[:, t * EXPERTS:(t + 1) * EXPERTS],
                                        [(rows_pair(xT_, c, t), w_pair(off + c * EXPERTS, EXPERTS)) for c in range(DC)], low_low=True)
                ins.then_inc(turn_filled.sem, 1)

            def gate_up(turn, k):
                e, half = divmod(k, 2)
                for name, bank, used, filled, m in ((f"g{k}", act_b, act_used, act_filled, 0), (f"u{k}", dve_b, dve_used, dve_filled, 1)):
                    off = OFF_E + (3 * e + m) * E0
                    weights(turn, off + E0)
                    pe.wait_ge(used.sem, used.at(turn, name) - 2)
                    for i in range(2):
                        n0 = (2 * half + i) * P
                        ins = split_product(bank(turn, name)[:, i * TOK:(i + 1) * TOK],
                                            [(w_pair(off + c * INTER + n0, P), (x0T[:, 0, c, :], x0T[:, 1, c, :])) for c in range(DC)])
                    ins.then_inc(filled.sem, 1)

            def down(turn, e):
                off = OFF_E + (3 * e + 2) * E0
                weights(turn, off + E0)
                pe.wait_ge(sum_used.sem, sum_used.at(turn, f"d{e}") - 2)
                pe.wait_ge(hid_ready.sem, hid_ready.at(turn, f"h{2 * e + 1}"))
                for t in range(TT):
                    ins = split_product(sum_b(turn, f"d{e}")[:, t * DIM:(t + 1) * DIM],
                                        [((hT[:, 0, e % 2, i, t * P:(t + 1) * P], hT[:, 1, e % 2, i, t * P:(t + 1) * P]), w_pair(off + i * DIM, DIM))
                                         for i in range(IC)])
                ins.then_inc(sum_filled.sem, 1)

            def experts(turn, kind, k):
                if turn.moe:
                    (gate_up if kind == "g" else down)(turn, k)

            def fill(turn, place):
                for kind, k in pieces(place):
                    experts(turn, kind, k)

            def wkv_keys(turn, c):
                pe.wait_ge(turn_used.sem, turn_used.at(turn, f"kT{c}") - 2)
                pe.wait_ge(back_rows.sem, back_rows.at(turn, "kT"))
                for t in range(TT):
                    ins = pe.transpose(turn_b(turn, f"kT{c}")[:, t * P:(t + 1) * P], kx[:, t, c * P:(c + 1) * P], ident)
                ins.then_inc(turn_filled.sem, 1)

            def wkv_out_rows(turn, c):
                pe.wait_ge(turn_used.sem, turn_used.at(turn, f"yT{c}") - 2)
                pe.wait_ge(back_rows.sem, back_rows.at(turn, f"y{c}"))
                for t in range(TT):
                    ins = pe.transpose(turn_b(turn, f"yT{c}")[:, t * P:(t + 1) * P], y[:, t * P:(t + 1) * P], ident)
                ins.then_inc(turn_filled.sem, 1)

            def back_gate_up(turn, t, c):
                e0, n = CHUNKS1[c]
                weights(turn, W_COLS)
                for name, bank, used, filled, off in ((f"mg{t}{c}", act_b, act_used, act_filled, OFF_W1), (f"mu{t}{c}", dve_b, dve_used, dve_filled, OFF_W3)):
                    pe.wait_ge(used.sem, used.at(turn, name) - 2)
                    split_product(bank(turn, name)[:, 0:n * P], [(rows_pair(x4T, d, t), w_pair(off + d * NE1 * HID1 + e0 * P, n * P)) for d in range(DC)])\
                        .then_inc(filled.sem, 1)

            def back_hidden(turn, t):
                for c, (e0, n) in enumerate(CHUNKS1):
                    name = f"m{t}{c}"
                    pe.wait_ge(turn_used.sem, turn_used.at(turn, name) - 2)
                    pe.wait_ge(dve_used.sem, dve_used.at(turn, f"mu{t}{c}"))
                    for i in range(n):
                        ins = pe.transpose(turn_b(turn, name)[:, i * P:(i + 1) * P], h1[:, t, (e0 + i) * P:(e0 + i + 1) * P], ident)
                    ins.then_inc(turn_filled.sem, 1)

            def back_down(turn, t):
                pe.wait_ge(sum_used.sem, sum_used.at(turn, f"md{t}") - 2)
                pe.wait_ge(turn_used.sem, turn_used.at(turn, f"m{t}2"))
                split_product(sum_b(turn, f"md{t}")[:, 0:DIM], [((m16[:, 0, e, :], m16[:, 1, e, :]), w_pair(OFF_W2 + e * DIM, DIM)) for e in range(NE1)])\
                    .then_inc(sum_filled.sem, 1)

            def half_attention(turn, a, half):
                if turn.att:
                    for n in (2 * half, 2 * half + 1):
                        stack_rows(turn, a, "q", n)
                        stack_rows(turn, a, "k", n)
                for i, (kind, k) in enumerate(pieces(f"{a}{half}")):
                    experts(turn, kind, k)
                    if turn.att and i < 3:
                        scores(turn, a, half, 2 * i)
                        scores(turn, a, half, 2 * i + 1)
                if turn.att:
                    turn_max(turn, a, half)
                if turn.back and half == 0:
                    if a == 1:
                        wkv_out_rows(turn, 0)
                    wkv_keys(turn, a)
                if turn.att:
                    exponents(turn, a, 2 * half)
                    exponents(turn, a, 2 * half + 1)
                    values(turn, a, 2 * half)
                    values(turn, a, 2 * half + 1)

            def turn_program(turn):
                fill(turn, "start")
                if turn.att:
                    turn_rows(turn, "a0q", lnq)
                    turn_rows(turn, "a0k", ctx)
                fill(turn, "rows")
                half_attention(turn, 0, 0)
                half_attention(turn, 0, 1)
                if turn.att:
                    outputs(turn, 0)
                fill(turn, "sum")
                if turn.att:
                    turn_rows(turn, "xn1", xn)
                fill(turn, "qkv")
                if turn.att:
                    qkv(turn)
                fill(turn, "stack")
                half_attention(turn, 1, 0)
                half_attention(turn, 1, 1)
                if turn.att:
                    outputs(turn, 1)
                if turn.back:
                    wkv_out_rows(turn, 1)
                fill(turn, "tail")
                if turn.att:
                    turn_rows(turn, "hT", att)
                if turn.back:
                    turn_rows(turn, "x4", x4n)
                if turn.att:
                    out_projection(turn)
                if turn.back:
                    logits(turn, "gl", "x4", x4T, OFF_GW)
                    for c in range(3):
                        back_gate_up(turn, 0, c)
                if turn.att:
                    turn_rows(turn, "xn2", xn)
                if turn.back:
                    back_gate_up(turn, 1, 0)
                if turn.att:
                    logits(turn, "lg", "xn2", x0T, OFF_WR)
                if turn.back:
                    back_gate_up(turn, 1, 1)
                    back_gate_up(turn, 1, 2)
                    back_hidden(turn, 0)
                    back_down(turn, 0)
                    back_hidden(turn, 1)
                    back_down(turn, 1)

            pe.wait_ge(const_ready, 2)
            pe.wait_ge(cleared, 3)
            turn_program(Turn("first"))
            turn_program(Turn("second"))
            with pe.Fori(0, LOOPS) as j:
                turn_program(Turn("loop", j))
            turn_program(Turn("fifth"))
            turn_program(Turn("last"))


def _consts():
    import numpy as np
    c = np.zeros((P, C_COLS), np.float32)
    c[:, C_ID:C_ID + P] = np.eye(P)
    c[:, C_TRIQ:C_TRIQ + P] = np.triu(np.ones((P, P)), 1)
    c[:, C_TRIK:C_TRIK + P] = np.tril(np.ones((P, P)), -1)
    m = np.arange(P)
    part = (m // HD) % 4
    for k, takes in enumerate((part % 2 == 0, part % 2 == 1, part < 2, part >= 2)):
        for pair in range(4):
            s = c[:, C_SEL + (4 * k + pair) * P:C_SEL + (4 * k + pair + 1) * P]
            s[(2 * pair + m // 64) * HD + m % HD, m] = takes
    c[:, C_COL + COL_IOTA:C_COL + COL_IOTA + 8] = np.arange(8)
    c[:, C_COL + COL_HALF:C_COL + COL_HALF + 4] = -0.5
    return c


def kernel(**inputs):
    import numpy as np
    import concourse.bacc as bacc
    from concourse.bass_utils import run_bass_kernel_spmd

    v = {k: np.asarray(a) for k, a in inputs.items()}

    def chunked(a):
        return a.reshape(a.shape[0] // P, P, -1).transpose(1, 0, 2).reshape(P, -1)

    parts = [chunked(np.concatenate([v["L0_ffn_" + n].T for n in ("Wq", "Wk", "Wv")], axis=1)),
             chunked(v["L0_ffn_Wo"].T), chunked(v["L0_ffn_Wr"].T), chunked(v["L1_ffn_gate_w"].T)]
    for e in range(EXPERTS):
        parts += [chunked(v["L0_ffn_Wg"][e].T), chunked(v["L0_ffn_Wu"][e].T), chunked(v["L0_ffn_Wd"][e].T)]
    for n, m in (("w1", "ws1"), ("w3", "ws3")):
        a = np.concatenate([v["L1_ffn_" + n], v["L1_ffn_" + m][None]], axis=0)
        parts.append(chunked(a.transpose(2, 0, 1).reshape(DIM, -1)))
    a = np.concatenate([v["L1_ffn_w2"], v["L1_ffn_ws2"][None]], axis=0)
    parts.append(a.transpose(2, 0, 1).reshape(P, -1))
    const = _consts()
    for k, n in ((COL_LN1, "L0_ffn_w_ln1"), (COL_LN2, "L0_ffn_w_ln2"), (COL_W, "L1_xattn_w"), (COL_U, "L1_xattn_u")):
        const[:, C_COL + k:C_COL + k + DC] = v[n].reshape(DC, P).T
    arrays = {
        "x": v["x"], "ctx": v["ctx_2048"], "ctx_t": np.ascontiguousarray(v["ctx_2048"].transpose(0, 2, 1)),
        "weights": np.ascontiguousarray(np.concatenate(parts, axis=1)), "const": const,
    }
    nc = bacc.Bacc("TRN2", target_bir_lowering=False, num_devices=1)
    args = [nc.dram_tensor("in_" + k, a.shape, mybir.dt.from_np(a.dtype), kind="ExternalInput").ap() for k, a in arrays.items()]
    out = nc.dram_tensor("out", (BATCH, TOK, DIM), F32, kind="ExternalOutput").ap()
    kernel_body(nc, *args, out)
    r = run_bass_kernel_spmd(nc, [{"in_" + k: a for k, a in arrays.items()}], core_ids=[0])
    return r.results[0]["out"]
```

```python
from contextlib import ExitStack

import concourse.bass as bass
from concourse import mybir

F32 = mybir.dt.float32
F16 = mybir.dt.float16
BF16 = mybir.dt.bfloat16
U32 = mybir.dt.uint32
ACT = mybir.ActivationFunctionType
ALU = mybir.AluOpType
X = mybir.AxisListType.X

P = 128
BATCH, TOK, DIM = 4, 256, 256
TT = TOK // P
DC = DIM // P
HEADS, HD = 16, 16
PAIRS = HEADS // 2
STRIP = 32
EXPERTS = 8
INTER = 512
IC = INTER // P
HID1 = 128
NE1 = EXPERTS + 1
CHUNKS1 = [(0, 4), (4, 4), (8, 1)]
EPS = 1e-5

W_UP = 64.0
A_UP = 64.0
QK_UP = 16.0
H_UP = 16.0
SCORE_DOWN = 1.0 / (QK_UP * QK_UP * HD ** 0.5)
PROD_DOWN = 1.0 / (W_UP * A_UP)
QK_SCALE = (QK_UP, QK_UP * PROD_DOWN)
MASK = 2.0 ** 15

E0 = DC * INTER
OFF_QKV = 0
OFF_WO = OFF_QKV + DC * 3 * DIM
OFF_WR = OFF_WO + DC * DIM
OFF_GW = OFF_WR + DC * EXPERTS
OFF_E = OFF_GW + DC * EXPERTS
OFF_W1 = OFF_E + EXPERTS * 3 * E0
OFF_W3 = OFF_W1 + DC * NE1 * HID1
OFF_W2 = OFF_W3 + DC * NE1 * HID1
W_COLS = OFF_W2 + NE1 * DIM
UNIT = 1024
UNITS = [(OFF_QKV, 768), (OFF_QKV + 768, 768), (OFF_WO, OFF_E - OFF_WO)]
UNITS += [(OFF_E + E0 * k, E0) for k in range(3 * EXPERTS)]
UNITS += [(OFF_W1 + 768 * k, 768) for k in range((W_COLS - OFF_W1) // 768)]
STAGES = 2

C_ID, C_TRIQ, C_TRIK, C_COL = 0, P, 2 * P, 3 * P
COL_LN1, COL_LN2, COL_W, COL_U, COL_IOTA, COL_HALF, COL_REST = 2, 4, 6, 8, 10, 18, 22
C_SEL = 3 * P + 23
N_SEL = 16
C_COLS = C_SEL + N_SEL * P


DVE_LOOP = 72

POOL_LN2, POOL_BASE, POOL_LN1, POOL_LN2_SECOND = 7, 17, 19, 31

STAGES_OF = {
    "first": ("att",), "second": ("att", "moe"), "loop": ("att", "moe", "back"),
    "end": ("moe", "back"),
}
LOOPS = BATCH - 2

PIECES = []
for _e in range(EXPERTS + 1):
    if _e < EXPERTS:
        PIECES += [("g", 2 * _e), ("u", 2 * _e), ("g", 2 * _e + 1), ("u", 2 * _e + 1)]
    if _e:
        PIECES += [("d0", _e - 1), ("d1", _e - 1)]
HALF_PLACES = (("stacked", 2), ("scores0", 2), ("scores1", 1), ("scores2", 1), ("maxima", 1), ("exponents", 1))
PLACES = {"start": 4, "rows": 2}
for _a in range(2):
    if _a:
        PLACES.update({"outputs": 1, "sum": 3, "qkv": 2, "stack": 2})
    for _half in range(2):
        PLACES.update({(_a, _half, name): n for name, n in HALF_PLACES})
PLACES.update({"tail": 1, "projection": 1})
assert sum(PLACES.values()) == len(PIECES)


def pieces(place):
    before = 0
    for name, n in PLACES.items():
        if name == place:
            return PIECES[before:before + n]
        before += n


class Turn:

    def __init__(self, mode, j=0, last=False):
        self.mode, self.j, self.last = mode, j, last
        self.att, self.moe, self.back = (s in STAGES_OF[mode] and (s == "back" or not last) for s in ("att", "moe", "back"))


class Signal:

    def __init__(self, sem, events, start=0, first=None, end=None):
        self.sem, self.start = sem, start
        self.order = {mode: [n for s, n in events if s in stages] for mode, stages in STAGES_OF.items()}
        self.order["first"] = first or self.order["first"]
        self.order["end"] = end or self.order["end"] + [n + "+" for s, n in events if s == "back"]

    def before(self, turn):
        n = self.start
        for mode in STAGES_OF:
            if mode == turn.mode:
                break
            n += len(self.order[mode]) * (LOOPS if mode == "loop" else 1)
        if turn.mode == "loop":
            return n + turn.j * len(self.order["loop"])
        return n

    def at(self, turn, name):
        return self.before(turn) + (self.order[turn.mode].index(name + "+" * turn.last) + 1)


class Ring:

    def __init__(self, banks, filled, used, events, first, end):
        self.banks, self.depth = banks, len(banks)
        self.filled, self.used = Signal(filled, events, 0, first, end), Signal(used, events, self.depth, first, end)
        assert len(self.filled.order["loop"]) % self.depth == 0

    def __call__(self, turn, name):
        first = self.filled.before(Turn(turn.mode))
        return self.banks[(first + self.filled.order[turn.mode].index(name + "+" * turn.last)) % self.depth]


class Steps:

    def __init__(self, eng, sem, loop):
        self.eng, self.sem, self.loop = eng, sem, loop
        self.n, self.base = 0, 0

    def turn(self, turn, before=0):
        self.base = before + turn.j * self.loop if turn.mode == "loop" else before
        self.n = 0

    def done(self, ins):
        self.n += 1
        ins.then_inc(self.sem, 1)

    def wait(self):
        self.eng.wait_ge(self.sem, self.base + self.n)


def ring_events():
    turn_b, act_b, dve_b, sum_b = [], [], [], []

    def fill(place):
        for kind, k in pieces(place):
            if kind == "g":
                act_b.append(("moe", f"g{k}"))
            elif kind == "u":
                dve_b.append(("moe", f"u{k}"))
            elif kind == "d1":
                sum_b.append(("moe", f"d{k}"))

    fill("start")
    turn_b.extend(("att", n) for n in ("a0k", "a0q"))
    fill("rows")
    for a in range(2):
        if a == 1:
            fill("outputs")
            fill("sum")
            turn_b.append(("att", "xn1"))
            fill("qkv")
            turn_b.extend(("att", n) for n in ("a1q", "a1k"))
            act_b.extend(("att", n) for n in ("v0", "v1"))
            fill("stack")
        for half in range(2):
            dve_b.extend(("att", f"a{a}q{n}") for n in (2 * half, 2 * half + 1))
            act_b.extend(("att", f"a{a}k{n}") for n in (2 * half, 2 * half + 1))
            fill((a, half, "stacked"))
            for i in range(3):
                dve_b.extend(("att", f"a{a}s{6 * half + n}") for n in (2 * i, 2 * i + 1))
                fill((a, half, f"scores{i}"))
            turn_b.append(("att", f"a{a}n{half}"))
            fill((a, half, "maxima"))
            if half == 0:
                if a == 1:
                    dve_b.append(("back", "yT0"))
                turn_b.append(("back", f"kT{a}"))
            act_b.extend(("att", f"a{a}p{6 * half + n}") for n in range(3))
            fill((a, half, "exponents"))
            act_b.extend(("att", f"a{a}p{6 * half + n}") for n in range(3, 6))
            act_b.append(("att", f"a{a}o{half}"))
        turn_b.extend(("att", n) for n in (f"a{a}ot0", f"a{a}ot1"))
    dve_b.append(("back", "yT1"))
    fill("tail")
    turn_b.append(("att", "hT"))
    fill("projection")
    turn_b.extend([("back", "x4"), ("att", "xn2")])
    act_b.extend(("back", f"mg{t}{c}") for t in range(TT) for c in range(3))
    dve_b.extend([("att", "wo0"), ("att", "wo1"), ("back", "gl")])
    dve_b.extend(("back", n) for n in ("mu00", "mu01", "mu02", "mu10"))
    dve_b.append(("att", "lg"))
    dve_b.extend(("back", n) for n in ("mu11", "mu12"))
    turn_b.extend(("back", f"m{t}{c}") for t in range(TT) for c in range(3))
    sum_b.append(("back", "md"))

    def end(events, start, with_last):
        order = [n for s, n in events if s in STAGES_OF["end"]]
        rest = [n + "+" for s, n in events if s == "back" and n + "+" not in with_last]
        return order[:order.index(start)] + with_last + rest

    turn_end = end(turn_b, "m00", ["kT0+", "m00", "m01", "kT1+", "m02", "m10", "m11", "m12"])
    dve_end = end(dve_b, "mu00", ["mu00", "mu01", "mu02", "mu10", "mu11", "yT0+", "mu12", "yT1+"])
    act_first = [n for s, n in act_b if s == "att"]
    for a in range(2):
        for n in (f"a{a}k2", f"a{a}k3"):
            act_first.remove(n)
            act_first.insert(act_first.index(f"a{a}p0"), n)
    return (turn_b, None, turn_end), (act_b, act_first, None), (dve_b, None, dve_end), (sum_b, None, None)


def kernel_body(nc, x_d, ctx_d, ctxT_d, w_d, c_d, out_d):
    es = ExitStack()
    with es:
        def sb(name, shape, dt=F32):
            return es.enter_context(nc.sbuf_tensor(name, shape, dt))

        def sem(name):
            return es.enter_context(nc.semaphore(name))

        wh = sb("wh", [P, W_COLS], F16)
        wl = sb("wl", [P, W_COLS], F16)
        const = sb("const", [P, C_SEL])
        identb = sb("identb", [P, P], BF16)
        mask_id = sb("mask_id", [P, P], BF16)
        mask_q = sb("mask_q", [P, P], BF16)
        mask_k = sb("mask_k", [P, P], BF16)
        wln = sb("wln", [P, 4])
        spare = sb("spare", [P, 1])
        spare_act = sb("spare_act", [P, 2])
        xin = sb("xin", [P, TT, DIM])
        ctx = sb("ctx", [P, TT, DIM])
        sel_rows = sb("sel_rows", [P, N_SEL, P], F16)
        qbd = sb("qbd", [P, PAIRS // 2, 2, TOK], F16)
        kst = sb("kst", [P, PAIRS // 2, TOK], F16)
        nmx = sb("nmx", [P, TT, P], BF16)
        nmR = sb("nmR", [P, TOK + P], BF16)
        pick = sb("pick", [P, PAIRS, P], BF16)
        probs = sb("probs", [P, 6, 512])
        vcols = sb("vcols", [P, TT, HEADS * (HD + 1) + STRIP])
        vaug = vcols[:, :, 0:HEADS * (HD + 1)].rearrange("p t (h d) -> p t h d", h=HEADS)
        att = sb("att", [P, TT, DIM])
        rsum = sb("rsum", [P, TT, HEADS])
        x1 = xin
        z = sb("z", [P, TT, DIM])
        xn = lnq = att
        r2 = z
        xkT = sb("xkT", [P, DC, 4, TOK], F16)
        xT = xkT[:, :, 0:2, :].rearrange("p c s n -> p s c n")
        kT = xkT[:, :, 2:4, :].rearrange("p c s n -> p s c n")
        oT = xkT[:].bitcast(F32).rearrange("p c s n -> p (c s n)").rearrange("p (g n) -> p g n", g=4)
        x0T = sb("x0T", [P, 2, DC, TOK], F16)
        acc = sb("acc", [P, TT, DIM])
        sg = sb("sg", [P, 2, 512])
        hid = sb("hid", [P, 4096], F16)
        hT = hid[:].rearrange("p (s e i n) -> p s e i n", s=2, e=2, i=IC)


        def stacks(turn, half):
            if turn.mode == "first" and half == 1:
                return (hid[:, 0:2048].rearrange("p (h a n) -> p h a n", h=PAIRS // 2, a=2),
                        hid[:, 2048:3072].rearrange("p (h n) -> p h n", h=PAIRS // 2))
            return qbd, kst

        x3 = sb("x3", [P, TT, DIM])
        x4 = sb("x4", [P, TT, DIM])
        vT = sb("vT", [P, DC, TOK])
        big = sb("big", [P, 2307])
        stage = [big[:, UNIT * s:UNIT * (s + 1)] for s in range(STAGES)]

        class Wkv:

            def __init__(self, area, keys, sums):
                self.kx, self.x4 = keys, sums
                self.ex = area[:, 0:1024].rearrange("p (k n) -> p k n", k=4)
                self.ev = area[:, 1024:1536].rearrange("p (k n) -> p k n", k=2)
                self.omax = area[:, 1536:1793]
                self.pq = area[:, 1793:2307].rearrange("p (k n) -> p k n", k=2)
                self.nd = self.pq[:, :, 0:TOK]
                self.onew = self.ev[:, 0, :]
                self.y = self.nd[:, 0]

        wkvs = {False: Wkv(big, x4, x4), True: Wkv(probs[:].rearrange("p k n -> p (k n)"), xin, z)}
        x4n = big[:, 0:512].rearrange("p (t n) -> p t n", t=TT)
        h1 = big[:, 0:TT * NE1 * HID1].rearrange("p (t n) -> p t n", t=TT)
        x4T = hid[:, 0:1024].rearrange("p (s c n) -> p s c n", s=2, c=DC)
        m16_at = [[hid[:, 1024:2048], hid[:, 2048:3072], hid[:, 3072:3328]],
                  [hid[:, 0:1024], xkT[:].rearrange("p c s n -> p (c s n)")[:, 0:1024], hid[:, 3328:3584]]]
        m16 = [[m16_at[t][c].rearrange("p (s e n) -> p s e n", s=2, e=n) for c, (_, n) in enumerate(CHUNKS1)] for t in range(TT)]

        class Small:

            def __init__(self, name):
                self.stats = sb(name + "_stats", [P, TT, 6])
                self.mv = sb(name + "_mv", [P, TT, 2])
                self.var = sb(name + "_var", [P, 2, TT])
                self.rstd = sb(name + "_rstd", [P, 2, TT])
                self.lg = sb(name + "_lg", [P, TT, EXPERTS])
                self.lgx = sb(name + "_lgx", [P, TT, EXPERTS])
                self.lge = sb(name + "_lge", [P, TT, EXPERTS])
                self.top = sb(name + "_top", [P, TT, 8])
                self.topi = sb(name + "_topi", [P, TT, 8], U32)
                self.topf = sb(name + "_topf", [P, TT, 8])
                self.sel = sb(name + "_sel", [P, 2, TT, EXPERTS])

        sa, sk = Small("att"), Small("back")
        ss = sb("ss", [P, TT])
        den = sb("den", [P, TT])
        rden = sb("rden", [P, TT])
        cw = sb("cw", [P, TT, EXPERTS])
        s12 = sb("s12", [P, TT, EXPERTS])
        sm = sb("sm", [P, TT, EXPERTS])

        ident = const[:, C_ID:C_ID + P]

        def col(k, n=1):
            return const[:, C_COL + k:C_COL + k + n]

        def ring(name, depth, events, first, end):
            banks = [es.enter_context(nc.psum_tensor(f"{name}{i}", [P, 512], F32)) for i in range(depth)]
            return Ring(banks, sem(name + "_filled"), sem(name + "_used"), events, first, end)

        turn_b, act_b, dve_b, sum_b = (
            ring(n, depth, *events) for (n, depth), events in zip((("turn_b", 2), ("act_b", 2), ("dve_b", 3), ("sum_b", 1)), ring_events()))
        turn_filled, turn_used = turn_b.filled, turn_b.used
        act_filled, act_used = act_b.filled, act_b.used
        dve_filled, dve_used = dve_b.filled, dve_b.used
        sum_filled, sum_used = sum_b.filled, sum_b.used

        def signal(name, stage_, *events):
            return Signal(sem(name), [(stage_, n) for n in events])

        x_loaded = signal("x_loaded", "att", "x")
        ctx_loaded = signal("ctx_loaded", "att", "c")
        v_loaded = signal("v_loaded", "back", "v")
        v_used = signal("v_used", "back", "v0", "v1")
        highs = signal("highs", "att", "a0k", "a0q", "xn1", "a1q", "a1k", "hT", "xn2")
        hid_highs = signal("hid_highs", "moe", *(f"h{k}" for k in range(2 * EXPERTS)))
        back_highs = signal("back_highs", "back", "x4", *(f"m{t}{c}" for t in range(TT) for c in range(3)))
        hid_ready = Signal(sem("hid_ready"), [("moe", f"h{k}") for k in range(2 * EXPERTS)], start=2)
        rows_ready = signal("rows_ready", "att", "a0q", "xn1", "xn2")
        back_rows = signal("back_rows", "back", "kT", "y0", "y1", "x4")
        var_ready = signal("var_ready", "att", "ln1", "ln2", "rms2")
        rstd_ready = signal("rstd_ready", "att", "ln1", "ln2", "rms2")
        back_var = signal("back_var", "back", "ln3", "ln4")
        back_rstd = signal("back_rstd", "back", "ln3", "ln4")
        squares = signal("squares", "att", "r2")
        base_ready = signal("base_ready", "att", "x")
        rt_in = signal("rt_in", "att", "lg")
        rt_exp = signal("rt_exp", "att", "lg")
        back_exp = signal("back_exp", "back", "gl")
        scores_ready = signal("scores_ready", "back", "s")
        wkv_in = signal("wkv_in", "back", "w0", "w1")
        wkv_exp = signal("wkv_exp", "back", "w0", "w1")
        out_free = signal("out_free", "back", "o")
        out_stored = sem("out_stored")
        s_dve = sem("dve_steps")
        s_pool = sem("pool_steps")
        const_loaded = sem("const_loaded")
        sel_loaded = sem("sel_loaded")
        const_ready = sem("const_ready")
        pick_ready = sem("pick_ready")
        cleared = sem("cleared")
        staged = [sem(f"staged{s}") for s in range(STAGES)]
        w_ready = sem("w_ready")

        def unit_of(col_):
            return max(k for k, (c, _) in enumerate(UNITS) if c <= col_)

        block = es.enter_context(nc.Block())

        @block.sync
        def _(sp):
            def load(b):
                sp.dma_start(xin[:], x_d[b:b + 1].rearrange("o (t p) d -> p (o t) d", p=P)).then_inc(x_loaded.sem, 16)
                sp.dma_start(ctx[:], ctx_d[b:b + 1].rearrange("o (t p) d -> p (o t) d", p=P)).then_inc(ctx_loaded.sem, 16)

            def load_v(b):
                sp.dma_start(vT[:], ctxT_d[b:b + 1].rearrange("o (c p) t -> p (o c) t", p=P)).then_inc(v_loaded.sem, 16)

            def store(turn, b):
                sp.wait_ge(sum_used.sem, sum_used.at(turn, "md"))
                sp.dma_start(out_d[b:b + 1].rearrange("o (t p) d -> p (o t) d", p=P), wkvs[turn.last].x4[:]).then_inc(out_stored, 16)

            sp.dma_start(xin[:], x_d[0:1].rearrange("o (t p) d -> p (o t) d", p=P)).then_inc(x_loaded.sem, 16)
            sp.dma_start(const[:], c_d[:, 0:C_SEL]).then_inc(const_loaded, 16)
            sp.dma_start(ctx[:], ctx_d[0:1].rearrange("o (t p) d -> p (o t) d", p=P)).then_inc(ctx_loaded.sem, 16)
            sp.dma_start(probs[:].rearrange("p k n -> p (k n)")[:, 0:N_SEL * P], c_d[:, C_SEL:C_COLS]).then_inc(sel_loaded, 16)
            load_v(0)
            for k, (c, n) in enumerate(UNITS):
                if k >= STAGES:
                    sp.wait_ge(w_ready, k - STAGES + 1)
                sp.dma_start(stage[k % STAGES][:, 0:n], w_d[:, c:c + n]).then_inc(staged[k % STAGES], 16)
                if k == POOL_BASE:
                    sp.wait_ge(base_ready.sem, base_ready.at(Turn("first"), "x"))
                    load(1)
            sp.sem_inc(out_free.sem, 1)
            sp.wait_ge(base_ready.sem, base_ready.at(Turn("second"), "x"))
            load(2)
            for turn, b in [(Turn("loop", j), j) for j in range(LOOPS)] + [(Turn("end"), BATCH - 2)]:
                sp.wait_ge(v_used.sem, v_used.at(turn, "v1"))
                load_v(b + 1)
                if b + 3 < BATCH:
                    sp.wait_ge(base_ready.sem, base_ready.at(turn, "x"))
                    load(b + 3)
                store(turn, b)
                if b < BATCH - 2:
                    sp.wait_ge(out_stored, b * 16 + 16)
                    sp.sem_inc(out_free.sem, 1)
            store(Turn("end", last=True), BATCH - 1)
            sp.wait_ge(out_stored, 16 * BATCH)

        @block.gpsimd
        def _(pool):
            steps = [0]

            def step(ins):
                steps[0] += 1
                ins.then_inc(s_pool, 1)

            def split(k):
                c, n = UNITS[k]
                s = stage[k % STAGES][:, 0:n]
                pool.wait_ge(staged[k % STAGES], 16 * (k // STAGES + 1))
                step(pool.tensor_scalar(wh[:, c:c + n], s, W_UP, 0.0, ALU.mult, ALU.add))
                step(pool.tensor_scalar(s, s, W_UP, 0.0, ALU.mult, ALU.add))
                pool.wait_ge(s_pool, steps[0])
                pool.tensor_tensor(wl[:, c:c + n], s, wh[:, c:c + n], ALU.subtract).then_inc(w_ready, 1)

            half_cols = col(COL_HALF, 4).rearrange("p (k t) -> p k t", k=2)

            def root(turn, name, k=1):
                pool.wait_ge(var_ready.sem, var_ready.at(turn, name))
                pool.tensor_tensor(sa.rstd[:, 0:k, :], sa.var[:, 0:k, :], half_cols[:, 0:k, :], ALU.pow).then_inc(rstd_ready.sem, 1)

            def back_root(turn, name):
                pool.wait_ge(back_var.sem, back_var.at(turn, name))
                pool.tensor_tensor(sk.rstd[:, 0:1, :], sk.var[:, 0:1, :], half_cols[:, 0:1, :], ALU.pow).then_inc(back_rstd.sem, 1)

            def base(turn):
                pool.wait_ge(dve_used.sem, dve_used.at(turn, "wo1"))
                if turn.moe:
                    pool.wait_ge(sum_used.sem, sum_used.at(turn, "d7"))
                pool.tensor_tensor(acc[:], x1[:], r2[:], ALU.add).then_inc(base_ready.sem, 1)

            def roots(turn):
                if turn.att:
                    root(turn, "ln1")
                if turn.back:
                    back_root(turn, "ln3")
                if turn.att:
                    root(turn, "ln2", 2)
                if turn.back:
                    back_root(turn, "ln4")
                if turn.att:
                    root(turn, "rms2")
                    base(turn)

            pool.memset(qbd[:], 0.0).then_inc(cleared, 1)
            pool.memset(vcols[:], 0.0).then_inc(s_pool, 1)
            steps[0] += 1
            pool.memset(nmx[:], 0.0).then_inc(cleared, 1)
            pool.wait_ge(s_pool, 1)
            pool.memset(vaug[:, :, :, HD:HD + 1], 1.0).then_inc(cleared, 1)
            pool.memset(hid[:, 0:2048], 0.0).then_inc(cleared, 1)
            pool.wait_ge(const_loaded, 16)
            first, second = Turn("first"), Turn("second")
            root(first, "ln1")
            for k in range(len(UNITS)):
                if k == POOL_LN2:
                    root(first, "ln2", 2)
                if k == POOL_BASE:
                    root(first, "rms2")
                    base(first)
                if k == POOL_LN1:
                    root(second, "ln1")
                if k == POOL_LN2_SECOND:
                    root(second, "ln2", 2)
                split(k)
            root(second, "rms2")
            base(second)
            with pool.Fori(0, LOOPS) as j:
                roots(Turn("loop", j))
            roots(Turn("end"))
            roots(Turn("end", last=True))

        @block.scalar
        def _(act):
            def table(func):
                k = int(func == ACT.Silu)
                act.activation(spare_act[:, k:k + 1], ident[:, 0:1], func)

            def context_values(turn):
                act.wait_ge(ctx_loaded.sem, ctx_loaded.at(turn, "c") * 16)
                act.activation(vaug[:, :, :, 0:HD], ctx[:].rearrange("p t (h d) -> p t h d", h=HEADS), ACT.Copy)

            def rows_high(turn, name, scale, dst, sig):
                act.wait_ge(turn_filled.sem, turn_filled.at(turn, name))
                if isinstance(scale, float):
                    act.activation(dst[:, 0, :, :], turn_b(turn, name)[:].rearrange("p (c n) -> p c n", c=DC), ACT.Copy, scale=scale).then_inc(sig.sem, 1)
                    return
                for c in range(DC):
                    ins = act.activation(dst[:, 0, c, :], turn_b(turn, name)[:, c * TOK:(c + 1) * TOK], ACT.Copy, scale=wln[:, scale + c:scale + c + 1])
                ins.then_inc(sig.sem, 1)

            def stacked_keys(turn, a, half):
                kst_ = stacks(turn, half)[1]
                for n in range(2):
                    name = f"a{a}k{2 * half + n}"
                    act.wait_ge(act_filled.sem, act_filled.at(turn, name))
                    act.activation(kst_[:, 2 * n:2 * n + 2, :], act_b(turn, name)[:].rearrange("p (h n) -> p h n", h=2), ACT.Copy).then_inc(act_used.sem, 1)

            def probabilities(turn, a, half, g):
                for k in range(3 * g, 3 * g + 3):
                    name = f"a{a}p{6 * half + k}"
                    act.wait_ge(act_filled.sem, act_filled.at(turn, name))
                    act.activation(probs[:, k, :], act_b(turn, name)[:], ACT.Exp, scale=SCORE_DOWN).then_inc(act_used.sem, 1)

            def unnormalised(turn, a, half):
                name = f"a{a}o{half}"
                act.wait_ge(act_filled.sem, act_filled.at(turn, name))
                act.activation(oT[:, 2 * half:2 * half + 2, :], act_b(turn, name)[:].rearrange("p (g n) -> p g n", g=2), ACT.Copy).then_inc(act_used.sem, 1)

            def second_values(turn):
                for t in range(TT):
                    act.wait_ge(act_filled.sem, act_filled.at(turn, f"v{t}"))
                    act.activation(vaug[:, t, :, 0:HD], act_b(turn, f"v{t}")[:, 0:DIM].rearrange("p (h d) -> p h d", h=HEADS), ACT.Copy,
                                   scale=PROD_DOWN).then_inc(act_used.sem, 1)

            def square(turn):
                act.wait_ge(dve_used.sem, dve_used.at(turn, "wo1"))
                for t in range(TT):
                    ins = act.activation(xn[:, t, :], r2[:, t, :], ACT.Square, accum_out=ss[:, t:t + 1])
                ins.then_inc(squares.sem, 1)

            def silu(turn, k):
                act.wait_ge(act_filled.sem, act_filled.at(turn, f"g{k}"))
                act.wait_ge(hid_ready.sem, hid_ready.at(turn, f"h{k}") - 2)
                act.activation(sg[:, k % 2, :], act_b(turn, f"g{k}")[:], ACT.Silu, scale=PROD_DOWN).then_inc(act_used.sem, 1)

            def hidden_high(turn, k):
                act.wait_ge(dve_used.sem, dve_used.at(turn, f"u{k}"))
                act.activation(hT[:, 0, (k // 2) % 2, 2 * (k % 2):2 * (k % 2) + 2, :], sg[:, k % 2, :].rearrange("p (i n) -> p i n", i=2),
                               ACT.Copy).then_inc(hid_highs.sem, 1)

            def experts(turn, kind, k):
                if not turn.moe:
                    return
                if kind == "g":
                    silu(turn, k)
                    if k:
                        hidden_high(turn, k - 1)
                elif kind == "d0" and k == EXPERTS - 2:
                    hidden_high(turn, 2 * EXPERTS - 1)

            def fill(turn, place):
                for kind, k in pieces(place):
                    experts(turn, kind, k)

            def wkv_exponentials(turn, c):
                ex = wkvs[turn.last].ex
                if not turn.att:
                    table(ACT.Exp)
                act.wait_ge(wkv_in.sem, wkv_in.at(turn, f"w{c}"))
                act.activation(ex[:], ex[:], ACT.Exp).then_inc(wkv_exp.sem, 1)

            def back_router(turn):
                act.wait_ge(dve_used.sem, dve_used.at(turn, "gl"))
                act.activation(sk.lge[:], sk.lgx[:], ACT.Exp, scale=-1.0).then_inc(back_exp.sem, 1)

            def half_attention(turn, a, half):
                if turn.att:
                    stacked_keys(turn, a, half)
                for name, _ in HALF_PLACES[:-1]:
                    fill(turn, (a, half, name))
                if turn.att:
                    if turn.moe:
                        table(ACT.Exp)
                    probabilities(turn, a, half, 0)
                fill(turn, (a, half, "exponents"))
                if turn.att:
                    probabilities(turn, a, half, 1)
                    unnormalised(turn, a, half)
                if turn.back and half == 0:
                    wkv_exponentials(turn, a)
                if turn.moe:
                    table(ACT.Silu)

            def back_gate(turn, t, c):
                e0, n = CHUNKS1[c]
                name = f"mg{t}{c}"
                i = 3 * t + c
                act.wait_ge(act_filled.sem, act_filled.at(turn, name))
                if i >= 2:
                    act.wait_ge(dve_used.sem, dve_used.at(turn, f"mu{(i - 2) // 3}{(i - 2) % 3}"))
                if i == 0:
                    act.wait_ge(scores_ready.sem, scores_ready.at(turn, "s"))
                    if turn.moe:
                        act.wait_ge(hid_ready.sem, hid_ready.at(turn, f"h{2 * EXPERTS - 1}"))
                for e in range(e0, e0 + n):
                    s = s12[:, t, e:e + 1] if e < EXPERTS else PROD_DOWN
                    ins = act.activation(sg[:, i % 2, (e - e0) * P:(e - e0 + 1) * P], act_b(turn, name)[:, (e - e0) * P:(e - e0 + 1) * P],
                                         ACT.Silu, scale=s)
                ins.then_inc(act_used.sem, 1)

            def back_hidden(turn, t, c):
                name = f"m{t}{c}"
                act.wait_ge(turn_filled.sem, turn_filled.at(turn, name))
                act.activation(m16[t][c][:, 0], turn_b(turn, name)[:, 0:CHUNKS1[c][1] * P].rearrange("p (e n) -> p e n", e=CHUNKS1[c][1]), ACT.Copy)\
                    .then_inc(back_highs.sem, 1)

            def first_attention(turn, a):
                for half in range(2):
                    stacked_keys(turn, a, half)
                for half in range(2):
                    probabilities(turn, a, half, 0)
                    probabilities(turn, a, half, 1)
                    unnormalised(turn, a, half)

            def attention(turn, a):
                if turn.mode == "first":
                    first_attention(turn, a)
                else:
                    half_attention(turn, a, 0)
                    half_attention(turn, a, 1)

            def first_part(turn):
                if turn.att:
                    context_values(turn)
                fill(turn, "start")
                if turn.att:
                    rows_high(turn, "a0k", QK_SCALE[0], kT, highs)
                    rows_high(turn, "a0q", QK_SCALE[0], xT, highs)
                if turn.mode == "first":
                    act.wait_ge(sel_loaded, 16)
                    act.activation(sel_rows[:], probs[:].rearrange("p k n -> p (k n)")[:, 0:N_SEL * P].rearrange("p (s n) -> p s n", s=N_SEL), ACT.Copy)\
                        .then_inc(const_ready, 1)
                fill(turn, "rows")
                attention(turn, 0)
                fill(turn, "outputs")
                fill(turn, "sum")
                if turn.att:
                    rows_high(turn, "xn1", 0, xT, highs)
                fill(turn, "qkv")
                if turn.att:
                    second_values(turn)
                    act.wait_ge(turn_filled.sem, turn_filled.at(turn, "a1k"))
                    rows_high(turn, "a1q", QK_SCALE[1], xT, highs)
                    rows_high(turn, "a1k", QK_SCALE[1], kT, highs)
                fill(turn, "stack")
                attention(turn, 1)
                if turn.back and not turn.att:
                    rows_high(turn, "x4", A_UP, x4T, back_highs)
                fill(turn, "tail")

            def second_part(turn):
                if turn.att:
                    rows_high(turn, "hT", A_UP, xT, highs)
                if turn.back:
                    rows_high(turn, "x4", A_UP, x4T, back_highs)
                if turn.att:
                    square(turn)
                if turn.back:
                    back_router(turn)
                    table(ACT.Silu)
                    for c in range(3):
                        back_gate(turn, 0, c)
                if turn.att:
                    rows_high(turn, "xn2", 2, x0T, highs)
                if turn.back:
                    back_gate(turn, 1, 0)
                if turn.back:
                    back_hidden(turn, 0, 0)
                    back_hidden(turn, 0, 1)
                    back_gate(turn, 1, 1)
                    back_hidden(turn, 0, 2)
                    back_gate(turn, 1, 2)
                    for c in range(3):
                        back_hidden(turn, 1, c)
                if turn.att:
                    table(ACT.Exp)
                    act.wait_ge(rt_in.sem, rt_in.at(turn, "lg"))
                    act.activation(sa.lge[:], sa.lgx[:], ACT.Exp).then_inc(rt_exp.sem, 1)

            act.sem_inc(act_used.sem, act_used.start)
            act.wait_ge(const_loaded, 16)
            act.activation(identb[:], ident, ACT.Copy)
            act.activation(mask_id[:], ident, ACT.Copy, scale=-MASK)
            act.activation(mask_q[:], const[:, C_TRIQ:C_TRIQ + P], ACT.Copy, scale=MASK)
            act.activation(wln[:], col(COL_LN1, 4), ACT.Copy, scale=A_UP)
            for c in (0, TOK):
                act.activation(nmR[:, c:c + P], const[:, C_TRIK:C_TRIK + P], ACT.Copy, scale=-MASK * MASK)
            act.activation(nmR[:, P:TOK], ident, ACT.Copy, scale=0.0)
            act.activation(mask_k[:], const[:, C_TRIK:C_TRIK + P], ACT.Copy, scale=MASK).then_inc(const_ready, 1)
            act.wait_ge(const_ready, 1)
            act.wait_ge(cleared, 3)
            for mode in ("first", "second"):
                first_part(Turn(mode))
                second_part(Turn(mode))
            with act.Fori(0, LOOPS) as j:
                first_part(Turn("loop", j))
                second_part(Turn("loop", j))
            end, last = Turn("end"), Turn("end", last=True)
            first_part(end)
            back_router(end)
            back_gate(end, 0, 0)
            back_gate(end, 0, 1)
            wkv_exponentials(last, 0)
            back_gate(end, 0, 2)
            back_gate(end, 1, 0)
            back_hidden(end, 0, 0)
            back_hidden(end, 0, 1)
            back_gate(end, 1, 1)
            wkv_exponentials(last, 1)
            back_hidden(end, 0, 2)
            back_gate(end, 1, 2)
            for c in range(3):
                back_hidden(end, 1, c)
            second_part(last)

        @block.vector
        def _(dve):
            st = Steps(dve, s_dve, DVE_LOOP)

            def stand_alone():
                dve.memset(spare[:], 0.0)

            def row_stats(b, src):
                for t in range(TT):
                    st.done(dve.bn_stats(b.stats[:, t, :], src[:, t, :]))
                st.wait()
                stand_alone()
                for t in range(TT):
                    st.done(dve.bn_aggr(b.mv[:, t, :], b.stats[:, t, :]))
                st.wait()

            def normed(b, dst, src, k=0):
                for t in range(TT):
                    ins = dve.tensor_scalar(dst[:, t, :], src[:, t, :], b.mv[:, t, 0:1], b.rstd[:, k, t:t + 1], ALU.subtract, ALU.mult)
                return ins

            def ln1_stats(turn):
                dve.wait_ge(x_loaded.sem, x_loaded.at(turn, "x") * 16)
                row_stats(sa, xin)
                dve.tensor_scalar(sa.var[:, 0, :], sa.mv[:, :, 1], EPS, None, ALU.add).then_inc(var_ready.sem, 1)

            def ln1_rows(turn):
                dve.wait_ge(rstd_ready.sem, rstd_ready.at(turn, "ln1"))
                normed(sa, lnq, xin).then_inc(rows_ready.sem, 1)

            def place_queries(turn, a, half, pairs=(0, 1)):
                qbd_ = stacks(turn, half)[0]
                for n in pairs:
                    name = f"a{a}q{2 * half + n}"
                    dve.wait_ge(dve_filled.sem, dve_filled.at(turn, name))
                    for ab in range(2):
                        r = slice(64 * ab, 64 * ab + 64)
                        ins = dve.tensor_copy(qbd_[r, 2 * n:2 * n + 2, ab, :], dve_b(turn, name)[r, :].rearrange("p (h n) -> p h n", h=2))
                    ins.then_inc(dve_used.sem, 1)

            def score_max(turn, a, half, k):
                name = f"a{a}s{6 * half + k}"
                t, h, n = (0, 4 * k, 4) if k < 2 else (1, 2 * (k - 2), 2)
                dve.wait_ge(dve_filled.sem, dve_filled.at(turn, name))
                dve.tensor_reduce(nmx[:, t, h:h + n], dve_b(turn, name)[:].rearrange("p (h n) -> p h n", h=n), X, ALU.max,
                                  negate=True).then_inc(dve_used.sem, 1)

            def turned_max(turn, a, half):
                name = f"a{a}n{half}"
                dve.wait_ge(turn_filled.sem, turn_filled.at(turn, name))
                maxima = turn_b(turn, name)[:].bitcast(BF16)
                dve.tensor_copy(nmR[0:PAIRS, 0:TOK], maxima[0:PAIRS, 0:TOK])
                dve.tensor_copy(nmR[0:PAIRS, TOK:TOK + P], maxima[0:PAIRS, P:TOK]).then_inc(turn_used.sem, 1)

            def outputs(turn, a):
                for t in range(TT):
                    name = f"a{a}ot{t}"
                    dve.wait_ge(turn_filled.sem, turn_filled.at(turn, name))
                    o = turn_b(turn, name)[:].rearrange("p (h d) -> p h d", h=HEADS)
                    st.done(dve.reciprocal(rsum[:, t, :], o[:, :, HD]))
                    st.wait()
                    dve.tensor_tensor(att[:, t, :].rearrange("p (h d) -> p h d", h=HEADS), o[:, :, 0:HD],
                                      rsum[:, t, :].unsqueeze(2).broadcast_to([P, HEADS, HD]), ALU.mult).then_inc(turn_used.sem, 1)

            def first_sum(turn):
                dve.wait_ge(turn_used.sem, turn_used.at(turn, "a0ot1"))
                st.done(dve.tensor_tensor(x1[:], xin[:], att[:], ALU.add))
                st.wait()
                row_stats(sa, x1)
                st.done(dve.tensor_scalar(sa.var[:, 0, :], sa.mv[:, :, 1], EPS, None, ALU.add))
                dve.tensor_scalar(sa.var[:, 1, :], sa.mv[:, :, 1], 1 + EPS, EPS * EPS, ALU.mult, ALU.add).then_inc(var_ready.sem, 1)
                dve.wait_ge(rstd_ready.sem, rstd_ready.at(turn, "ln2"))
                normed(sa, xn, x1, 1).then_inc(rows_ready.sem, 1)

            def rows_low(turn, name, scale, dst, sig):
                dve.wait_ge(sig.sem, sig.at(turn, name))
                if isinstance(scale, float):
                    dve.scalar_tensor_tensor(dst[:, 1, :, :], turn_b(turn, name)[:].rearrange("p (c n) -> p c n", c=DC), scale, dst[:, 0, :, :],
                                             ALU.mult, ALU.subtract).then_inc(turn_used.sem, 1)
                    return
                for c in range(DC):
                    ins = dve.scalar_tensor_tensor(dst[:, 1, c, :], turn_b(turn, name)[:, c * TOK:(c + 1) * TOK], wln[:, scale + c:scale + c + 1],
                                                   dst[:, 0, c, :], ALU.mult, ALU.subtract)
                ins.then_inc(turn_used.sem, 1)

            def second_sum(turn):
                for t in range(TT):
                    dve.wait_ge(dve_filled.sem, dve_filled.at(turn, f"wo{t}"))
                    if t == 0:
                        st.wait()
                    dve.scalar_tensor_tensor(r2[:, t, :], dve_b(turn, f"wo{t}")[:, 0:DIM], PROD_DOWN, z[:, t, :], ALU.mult,
                                             ALU.add).then_inc(dve_used.sem, 1)

            def mean_squares(turn):
                dve.wait_ge(squares.sem, squares.at(turn, "r2"))
                dve.tensor_scalar(sa.var[:, 0, :], ss[:], 1 / DIM, EPS, ALU.mult, ALU.add).then_inc(var_ready.sem, 1)

            def rms_rows(turn):
                dve.wait_ge(rstd_ready.sem, rstd_ready.at(turn, "rms2"))
                dve.wait_ge(dve_used.sem, dve_used.at(turn, "wo1"))
                for t in range(TT):
                    ins = dve.tensor_scalar(xn[:, t, :], r2[:, t, :], sa.rstd[:, 0, t:t + 1], None, ALU.mult)
                ins.then_inc(rows_ready.sem, 1)

            def top2(b):
                stand_alone()
                for t in range(TT):
                    st.done(dve.max(b.top[:, t, :], b.lg[:, t, :]))
                st.wait()
                stand_alone()
                for t in range(TT):
                    st.done(dve.max_index(b.topi[:, t, :], b.top[:, t, :], b.lg[:, t, :]))
                st.wait()
                st.done(dve.tensor_copy(b.topf[:], b.topi[:]))
                st.wait()
                iota = col(COL_IOTA, 8).unsqueeze(1).broadcast_to([P, TT, EXPERTS])
                for k in range(2):
                    st.done(dve.tensor_tensor(b.sel[:, k], iota, b.topf[:, :, k:k + 1].broadcast_to([P, TT, EXPERTS]), ALU.is_equal))
                st.wait()
                st.done(dve.tensor_tensor(b.sel[:, 0], b.sel[:, 0], b.sel[:, 1], ALU.add))
                st.wait()

            def router_logits(turn):
                dve.wait_ge(dve_filled.sem, dve_filled.at(turn, "lg"))
                dve.tensor_scalar(sa.lg[:], dve_b(turn, "lg")[:, 0:TT * EXPERTS].rearrange("p (t e) -> p t e", t=TT), PROD_DOWN, None,
                                  ALU.mult).then_inc(dve_used.sem, 1)

            def router(turn):
                b = sa
                dve.wait_ge(dve_used.sem, dve_used.at(turn, "lg"))
                top2(b)
                dve.tensor_tensor(b.lgx[:], b.lg[:], b.top[:, :, 0:1].broadcast_to([P, TT, EXPERTS]), ALU.subtract).then_inc(rt_in.sem, 1)
                dve.wait_ge(rt_exp.sem, rt_exp.at(turn, "lg"))
                st.done(dve.tensor_tensor(b.lge[:], b.lge[:], b.sel[:, 0], ALU.mult))
                st.wait()
                st.done(dve.tensor_reduce(den[:], b.lge[:], X, ALU.add))
                st.wait()
                st.done(dve.reciprocal(rden[:], den[:]))
                st.wait()
                if turn.moe:
                    dve.wait_ge(sum_used.sem, sum_used.at(turn, f"d{EXPERTS - 1}"))
                st.done(dve.scalar_tensor_tensor(cw[:], b.lge[:], 1 / (H_UP * W_UP), rden[:].unsqueeze(2).broadcast_to([P, TT, EXPERTS]),
                                                 ALU.mult, ALU.mult))
                st.wait()

            def hidden(turn, k):
                dve.wait_ge(dve_filled.sem, dve_filled.at(turn, f"u{k}"))
                dve.wait_ge(act_used.sem, act_used.at(turn, f"g{k}"))
                dve.scalar_tensor_tensor(sg[:, k % 2, :], dve_b(turn, f"u{k}")[:], H_UP * PROD_DOWN, sg[:, k % 2, :], ALU.mult,
                                         ALU.mult).then_inc(dve_used.sem, 1)

            def hidden_low(turn, k):
                dve.wait_ge(hid_highs.sem, hid_highs.at(turn, f"h{k}"))
                dve.tensor_tensor(hT[:, 1, (k // 2) % 2, 2 * (k % 2):2 * (k % 2) + 2, :], sg[:, k % 2, :].rearrange("p (i n) -> p i n", i=2),
                                  hT[:, 0, (k // 2) % 2, 2 * (k % 2):2 * (k % 2) + 2, :], ALU.subtract).then_inc(hid_ready.sem, 1)

            def add_expert(turn, e):
                dve.wait_ge(sum_filled.sem, sum_filled.at(turn, f"d{e}"))
                if e == 0:
                    dve.wait_ge(base_ready.sem, base_ready.before(turn))
                else:
                    dve.wait_ge(sum_used.sem, sum_used.at(turn, f"d{e - 1}"))
                dst = x3 if e == EXPERTS - 1 else acc
                for t in range(TT):
                    ins = dve.scalar_tensor_tensor(dst[:, t, :], sum_b(turn, f"d{e}")[:, t * DIM:(t + 1) * DIM], cw[:, t, e:e + 1], acc[:, t, :],
                                                   ALU.mult, ALU.add)
                ins.then_inc(sum_used.sem, 1)

            def experts(turn, kind, k):
                if not turn.moe:
                    return
                if kind == "u":
                    hidden(turn, k)
                    if k:
                        hidden_low(turn, k - 1)
                elif kind == "d0" and k == EXPERTS - 2:
                    hidden_low(turn, 2 * EXPERTS - 1)
                elif kind == "d1":
                    add_expert(turn, k)

            def fill(turn, place):
                for kind, k in pieces(place):
                    experts(turn, kind, k)

            def wkv_norm(turn):
                dve.wait_ge(sum_used.sem, sum_used.at(Turn("end"), f"d{EXPERTS - 1}") if turn.last else sum_used.before(turn))
                row_stats(sk, x3)
                dve.tensor_scalar(sk.var[:, 0, :], sk.mv[:, :, 1], EPS, None, ALU.add).then_inc(back_var.sem, 1)

            def wkv_rows(turn):
                if not turn.last:
                    dve.wait_ge(out_free.sem, out_free.at(turn, "o"))
                dve.wait_ge(back_rstd.sem, back_rstd.at(turn, "ln3"))
                normed(sk, wkvs[turn.last].kx, x3).then_inc(back_rows.sem, 1)

            def wkv_exponents(turn, c):
                dve.wait_ge(w_ready, len(UNITS))
                dve.wait_ge(turn_filled.sem, turn_filled.at(turn, f"kT{c}"))
                k = turn_b(turn, f"kT{c}")[:, 0:TOK]
                b = wkvs[turn.last]
                ex, omax, pq, onew = b.ex, b.omax, b.pq, b.onew
                w, u = col(COL_W + c), col(COL_U + c)
                st.done(dve.memset(omax[:, 0:1], -1e38))
                st.done(dve.memset(pq[:, :, 0:1], 0.0))
                st.done(dve.tensor_tensor_scan(omax[:, 1:TOK + 1], w.broadcast_to([P, TOK]), k, -1e38, ALU.add, ALU.max))
                st.wait()
                st.done(dve.scalar_tensor_tensor(onew, k, u, omax[:, 0:TOK], ALU.add, ALU.max))
                st.done(dve.scalar_tensor_tensor(ex[:, 1], omax[:, 0:TOK], w, omax[:, 1:TOK + 1], ALU.add, ALU.subtract))
                st.wait()
                st.done(dve.tensor_tensor(ex[:, 0], omax[:, 0:TOK], onew, ALU.subtract))
                st.done(dve.scalar_tensor_tensor(ex[:, 2], k, u, onew, ALU.add, ALU.subtract))
                dve.tensor_tensor(ex[:, 3], k, omax[:, 1:TOK + 1], ALU.subtract).then_inc(turn_used.sem, 1)
                dve.wait_ge(turn_used.sem, turn_used.at(turn, f"kT{c}"))
                dve.sem_inc(wkv_in.sem, 1)

            def wkv_scan(turn, c):
                b = wkvs[turn.last]
                ex, ev, pq = b.ex, b.ev, b.pq
                dve.wait_ge(wkv_exp.sem, wkv_exp.at(turn, f"w{c}"))
                dve.wait_ge(v_loaded.sem, v_loaded.at(turn, "v") * 16)
                dve.tensor_tensor(ev, ex[:, 2:4, :], vT[:, c, :].unsqueeze(1).broadcast_to([P, 2, TOK]), ALU.mult).then_inc(v_used.sem, 1)
                dve.wait_ge(v_used.sem, v_used.at(turn, f"v{c}"))
                st.done(dve.tensor_tensor_scan(pq[:, 0, 1:TOK + 1], ex[:, 1], ev[:, 1], 0.0, ALU.mult, ALU.add))
                st.done(dve.tensor_tensor_scan(pq[:, 1, 1:TOK + 1], ex[:, 1], ex[:, 3], 0.0, ALU.mult, ALU.add))
                st.wait()

            def wkv_out(turn, c):
                b = wkvs[turn.last]
                ex, ev, nd = b.ex, b.ev, b.nd
                st.done(dve.tensor_tensor(nd, ex[:, 0].unsqueeze(1).broadcast_to([P, 2, TOK]), nd, ALU.mult))
                st.wait()
                st.done(dve.tensor_tensor(nd[:, 1], nd[:, 1], ex[:, 2], ALU.add))
                st.done(dve.tensor_tensor(nd[:, 0], nd[:, 0], ev[:, 0], ALU.add))

            def wkv_quotient(turn, c):
                nd, y = wkvs[turn.last].nd, wkvs[turn.last].y
                st.wait()
                st.done(dve.reciprocal(nd[:, 1], nd[:, 1]))
                st.wait()
                dve.tensor_tensor(y, nd[:, 0], nd[:, 1], ALU.mult).then_inc(back_rows.sem, 1)

            def third_sum(turn, c):
                dve.wait_ge(dve_filled.sem, dve_filled.at(turn, f"yT{c}"))
                dve.tensor_tensor(wkvs[turn.last].x4[:, :, c * P:(c + 1) * P], x3[:, :, c * P:(c + 1) * P],
                                  dve_b(turn, f"yT{c}")[:, 0:TOK].rearrange("p (t n) -> p t n", t=TT), ALU.add).then_inc(dve_used.sem, 1)

            def last_stats(turn):
                dve.wait_ge(dve_used.sem, dve_used.at(turn, "yT1"))
                row_stats(sk, wkvs[turn.last].x4)
                dve.tensor_scalar(sk.var[:, 0, :], sk.mv[:, :, 1], EPS, None, ALU.add).then_inc(back_var.sem, 1)

            def last_rows(turn):
                dve.wait_ge(back_rstd.sem, back_rstd.at(turn, "ln4"))
                normed(sk, x4n, wkvs[turn.last].x4).then_inc(back_rows.sem, 1)

            def back_logits(turn):
                dve.wait_ge(dve_filled.sem, dve_filled.at(turn, "gl"))
                dve.tensor_scalar(sk.lgx[:], dve_b(turn, "gl")[:, 0:TT * EXPERTS].rearrange("p (t e) -> p t e", t=TT), PROD_DOWN, None,
                                  ALU.mult).then_inc(dve_used.sem, 1)

            def back_scores(turn):
                b = sk
                dve.wait_ge(back_exp.sem, back_exp.at(turn, "gl"))
                st.done(dve.tensor_scalar(b.lge[:], b.lge[:], 1.0, None, ALU.add))
                st.wait()
                st.done(dve.reciprocal(b.lg[:], b.lge[:]))
                st.wait()
                dve.tensor_scalar(s12[:], b.lg[:], PROD_DOWN, None, ALU.mult).then_inc(scores_ready.sem, 1)
                top2(b)
                st.done(dve.scalar_tensor_tensor(sm[:], b.lg[:], H_UP * PROD_DOWN, b.sel[:, 0], ALU.mult, ALU.mult))
                st.wait()

            def back_up(turn, t, c):
                e0, n = CHUNKS1[c]
                name = f"mu{t}{c}"
                dve.wait_ge(dve_filled.sem, dve_filled.at(turn, name))
                dve.wait_ge(act_used.sem, act_used.at(turn, f"mg{t}{c}"))
                for e in range(e0, e0 + n):
                    s = sm[:, t, e:e + 1] if e < EXPERTS else H_UP * PROD_DOWN
                    r = slice((e - e0) * P, (e - e0 + 1) * P)
                    ins = dve.scalar_tensor_tensor(h1[:, t, e * P:(e + 1) * P], dve_b(turn, name)[:, r], s, sg[:, (3 * t + c) % 2, r], ALU.mult, ALU.mult)
                ins.then_inc(dve_used.sem, 1)

            def hidden_halves(turn, t, c):
                e0, n = CHUNKS1[c]
                name = f"m{t}{c}"
                dve.wait_ge(back_highs.sem, back_highs.at(turn, name))
                dve.tensor_tensor(m16[t][c][:, 1], turn_b(turn, name)[:, 0:n * P].rearrange("p (e n) -> p e n", e=n),
                                  m16[t][c][:, 0], ALU.subtract).then_inc(turn_used.sem, 1)

            def last_sum(turn):
                dve.wait_ge(sum_filled.sem, sum_filled.at(turn, "md"))
                x4_ = wkvs[turn.last].x4
                dve.scalar_tensor_tensor(x4_[:], sum_b(turn, "md")[:].rearrange("p (t n) -> p t n", t=TT), 1 / (H_UP * W_UP), x4_[:], ALU.mult,
                                         ALU.add).then_inc(sum_used.sem, 1)

            def half_attention(turn, a, half):
                if turn.att:
                    place_queries(turn, a, half)
                elif half == 1 and turn.back:
                    wkv_scan(turn, a)
                fill(turn, (a, half, "stacked"))
                if not turn.att and turn.back and half == 1:
                    wkv_out(turn, a)
                for i in range(3):
                    if turn.att:
                        score_max(turn, a, half, 2 * i)
                        score_max(turn, a, half, 2 * i + 1)
                    fill(turn, (a, half, f"scores{i}"))
                    if not turn.att and turn.back and (a, half, i) in ((0, 1, 1), (1, 1, 0)):
                        wkv_quotient(turn, a)
                    if not turn.att and turn.back and (a, half, i) == (1, 1, 2):
                        third_sum(turn, 1)
                        last_stats(turn)
                        last_rows(turn)
                if turn.att:
                    turned_max(turn, a, half)
                fill(turn, (a, half, "maxima"))
                if turn.back:
                    if half == 0:
                        if a == 1:
                            third_sum(turn, 0)
                        wkv_exponents(turn, a)
                    elif turn.att:
                        wkv_scan(turn, a)
                        wkv_out(turn, a)
                        wkv_quotient(turn, a)
                fill(turn, (a, half, "exponents"))

            def first_attention(turn, a):
                place_queries(turn, a, 0)
                for k in range(6):
                    score_max(turn, a, 0, k)
                if a == 0:
                    dve.wait_ge(cleared, 4)
                place_queries(turn, a, 1, (0,))
                turned_max(turn, a, 0)
                place_queries(turn, a, 1, (1,))
                for k in range(6):
                    score_max(turn, a, 1, k)
                turned_max(turn, a, 1)

            def attention(turn, a):
                if turn.mode == "first":
                    first_attention(turn, a)
                else:
                    half_attention(turn, a, 0)
                    half_attention(turn, a, 1)

            def first_part(turn):
                if turn.att:
                    ln1_stats(turn)
                if turn.mode == "first":
                    dve.wait_ge(const_ready, 1)
                    for h in range(PAIRS):
                        ins = dve.tensor_scalar(pick[:, h, :], ident, col(COL_REST), ident[:, h:h + 1], ALU.mult, ALU.add)
                    ins.then_inc(pick_ready, 1)
                    dve.wait_ge(cleared, 3)
                if turn.back:
                    wkv_norm(turn)
                if turn.att:
                    ln1_rows(turn)
                if turn.back:
                    wkv_rows(turn)
                fill(turn, "start")
                if turn.att:
                    rows_low(turn, "a0k", QK_SCALE[0], kT, highs)
                    rows_low(turn, "a0q", QK_SCALE[0], xT, highs)
                fill(turn, "rows")
                attention(turn, 0)
                fill(turn, "outputs")
                if turn.att:
                    outputs(turn, 0)
                    first_sum(turn)
                fill(turn, "sum")
                if turn.att:
                    rows_low(turn, "xn1", 0, xT, highs)
                    st.done(normed(sa, z, x1, 0))
                fill(turn, "qkv")
                if turn.att:
                    rows_low(turn, "a1q", QK_SCALE[1], xT, highs)
                    rows_low(turn, "a1k", QK_SCALE[1], kT, highs)
                fill(turn, "stack")
                attention(turn, 1)
                if turn.att:
                    outputs(turn, 1)
                if turn.back and turn.att:
                    third_sum(turn, 1)
                    last_stats(turn)
                if turn.back and not turn.att:
                    rows_low(turn, "x4", A_UP, x4T, back_highs)
                fill(turn, "tail")

            def second_part(turn):
                if turn.att:
                    rows_low(turn, "hT", A_UP, xT, highs)
                fill(turn, "projection")
                if turn.back and not turn.last:
                    last_rows(turn)
                if turn.att:
                    second_sum(turn)
                if turn.back:
                    rows_low(turn, "x4", A_UP, x4T, back_highs)
                if turn.att:
                    mean_squares(turn)
                if turn.back:
                    back_logits(turn)
                if turn.att:
                    rms_rows(turn)
                if turn.back:
                    back_scores(turn)
                    for c in range(3):
                        back_up(turn, 0, c)
                if turn.att:
                    rows_low(turn, "xn2", 2, x0T, highs)
                if turn.back:
                    back_up(turn, 1, 0)
                if turn.att:
                    router_logits(turn)
                if turn.back:
                    hidden_halves(turn, 0, 0)
                    hidden_halves(turn, 0, 1)
                    back_up(turn, 1, 1)
                    hidden_halves(turn, 0, 2)
                    back_up(turn, 1, 2)
                    for c in range(3):
                        hidden_halves(turn, 1, c)
                if turn.att:
                    router(turn)
                if turn.back:
                    last_sum(turn)

            for used in (turn_used, dve_used, sum_used):
                dve.sem_inc(used.sem, used.start)
            dve.sem_inc(hid_ready.sem, hid_ready.start)
            before = 0
            for mode in ("first", "second"):
                st.turn(Turn(mode), before)
                first_part(Turn(mode))
                second_part(Turn(mode))
                before += st.n
            with dve.Fori(0, LOOPS) as j:
                st.turn(Turn("loop", j), before)
                first_part(Turn("loop", j))
                second_part(Turn("loop", j))
                assert st.n == DVE_LOOP, st.n
            end, last = Turn("end"), Turn("end", last=True)
            st.turn(end, before + LOOPS * DVE_LOOP)
            first_part(end)
            fill(end, "projection")
            wkv_norm(last)
            back_logits(end)
            wkv_rows(last)
            back_scores(end)
            back_up(end, 0, 0)
            wkv_exponents(last, 0)
            back_up(end, 0, 1)
            wkv_scan(last, 0)
            back_up(end, 0, 2)
            wkv_out(last, 0)
            wkv_quotient(last, 0)
            back_up(end, 1, 0)
            hidden_halves(end, 0, 0)
            hidden_halves(end, 0, 1)
            back_up(end, 1, 1)
            third_sum(last, 0)
            wkv_exponents(last, 1)
            hidden_halves(end, 0, 2)
            back_up(end, 1, 2)
            wkv_scan(last, 1)
            hidden_halves(end, 1, 0)
            wkv_out(last, 1)
            wkv_quotient(last, 1)
            hidden_halves(end, 1, 1)
            hidden_halves(end, 1, 2)
            third_sum(last, 1)
            last_stats(last)
            last_rows(last)
            last_sum(end)
            second_part(last)

        @block.tensor
        def _(pe):
            def split_product(out, terms, low_low=False):
                mm = [(l, r) for lhs, rhs in terms for l, r in ([(lhs[0], rhs[0]), (lhs[0], rhs[1]), (lhs[1], rhs[0])] + [(lhs[1], rhs[1])] * low_low)]
                for i, (l, r) in enumerate(mm):
                    ins = pe.matmul(out, l, r, start=(i == 0), stop=(i == len(mm) - 1))
                return ins

            def w_pair(off, n):
                return wh[:, off:off + n], wl[:, off:off + n]

            def weights(turn, off):
                if turn.mode in ("first", "second") or off >= OFF_W1:
                    pe.wait_ge(w_ready, unit_of(off - 1) + 1)

            def stack_rows(turn, a, s, n):
                name = f"a{a}{s}{n}"
                src, k, bank = (xT, 0, dve_b) if s == "q" else (kT, 2, act_b)
                pe.wait_ge(bank.used.sem, bank.used.at(turn, name) - bank.depth)
                pe.wait_ge(turn_used.sem, turn_used.at(turn, f"a{a}{s}"))
                for i in range(2):
                    for part in range(2):
                        ins = pe.matmul(bank(turn, name)[:, i * TOK:(i + 1) * TOK], sel_rows[:, 4 * (k + part) + (2 * n + i) % 4, :], src[:, part, n // 2, :],
                                        start=(i + part == 0), stop=(i + part == 2), skip_group_check=True)
                ins.then_inc(bank.filled.sem, 1)

            def scores(turn, a, half, k):
                name = f"a{a}s{6 * half + k}"
                pe.wait_ge(dve_used.sem, dve_used.at(turn, name) - 3)
                t, h0, n, keys = (0, 4 * k, 4, P) if k < 2 else (1, 2 * (k - 2), 2, TOK)
                if k == 0:
                    pe.wait_ge(dve_used.sem, dve_used.at(turn, f"a{a}q{2 * half + 1}"))
                    pe.wait_ge(act_used.sem, act_used.at(turn, f"a{a}k{2 * half + 1}"))
                qbd_, kst_ = stacks(turn, half)
                bank = dve_b(turn, name)[:].rearrange("p (h n) -> p h n", h=n)
                for i in range(n):
                    hp, ab = divmod(h0 + i, 2)
                    pe.matmul(bank[:, i, :], qbd_[:, hp, ab, t * P:(t + 1) * P], kst_[:, hp, 0:keys], start=(i == 0), stop=False, skip_group_check=True)
                pe.matmul(bank[:, :, keys - P:keys], mask_id[:], mask_q[:].unsqueeze(1).broadcast_to([P, n, P]), start=False,
                          stop=True, skip_group_check=True).then_inc(dve_filled.sem, 1)

            def turn_max(turn, a, half):
                name = f"a{a}n{half}"
                pe.wait_ge(turn_used.sem, turn_used.at(turn, name) - 2)
                pe.wait_ge(dve_used.sem, dve_used.at(turn, f"a{a}s{6 * half + 5}"))
                for t in range(TT):
                    ins = pe.transpose(turn_b(turn, name)[:].bitcast(BF16)[:, t * P:(t + 1) * P], nmx[:, t, :], identb[:])
                ins.then_inc(turn_filled.sem, 1)

            def exponents(turn, a, g):
                half = g // 2
                qbd_, kst_ = stacks(turn, half)
                if g % 2 == 0:
                    pe.wait_ge(turn_used.sem, turn_used.at(turn, f"a{a}n{half}"))
                for i in range(3):
                    name = f"a{a}p{3 * g + i}"
                    pe.wait_ge(act_used.sem, act_used.at(turn, name) - 2)
                    q0 = 0 if i < 2 else P
                    h0 = 4 * (g % 2) + (2 * i if i < 2 else 0)
                    heads = range(h0, h0 + (2 if i < 2 else 4))
                    bank = act_b(turn, name)[:].rearrange("p (h n) -> p h n", h=len(heads))
                    for hp in range(heads[0] // 2, heads[-1] // 2 + 1):
                        r = 2 * hp - heads[0]
                        pe.matmul(bank[:, r:r + 2, :], kst_[:, hp, q0:q0 + P], qbd_[:, hp, :, q0:TOK], start=(r == 0), stop=False, skip_group_check=True)
                    for r, h in enumerate(heads):
                        pe.matmul(bank[:, r, :], pick[:, h, :], nmR[:, 0:TOK] if i < 2 else nmR[:, TOK:TOK + P],
                                  start=False, stop=False, skip_group_check=True)
                    pe.matmul(bank[:, :, 0:8], mask_id[:], mask_k[:, 0:8].unsqueeze(1).broadcast_to([P, len(heads), 8]), start=False, stop=True,
                              skip_group_check=True).then_inc(act_filled.sem, 1)

            def values(turn, a, g):
                o = f"a{a}o{g // 2}"
                if g % 2 == 0:
                    pe.wait_ge(act_used.sem, act_used.at(turn, o) - 2)
                pe.wait_ge(act_used.sem, act_used.at(turn, f"a{a}p{3 * g + 2}"))
                for j in range(4):
                    h = 4 * g + j
                    s = 3 * (g % 2)
                    out = act_b(turn, o)[STRIP * j:STRIP * (j + 1), (g % 2) * TOK:(g % 2 + 1) * TOK]
                    pe.matmul(out, vcols[:, 0, h * (HD + 1):h * (HD + 1) + STRIP], probs[:, s + j // 2, (j % 2) * TOK:(j % 2 + 1) * TOK], start=True, stop=False, skip_group_check=True)
                    ins = pe.matmul(out[:, P:TOK], vcols[:, 1, h * (HD + 1):h * (HD + 1) + STRIP], probs[:, s + 2, j * P:(j + 1) * P], start=False, stop=True, skip_group_check=True)
                if g % 2:
                    ins.then_inc(act_filled.sem, 1)

            def outputs(turn, a):
                for t in range(TT):
                    name = f"a{a}ot{t}"
                    pe.wait_ge(turn_used.sem, turn_used.at(turn, name) - 2)
                    if t == 0:
                        pe.wait_ge(act_used.sem, act_used.at(turn, f"a{a}o1"))
                    for g in range(4):
                        ins = pe.transpose(turn_b(turn, name)[:, g * P:(g + 1) * P], oT[:, g, t * P:(t + 1) * P], ident)
                    ins.then_inc(turn_filled.sem, 1)

            def turn_rows(turn, name, src):
                pe.wait_ge(turn_used.sem, turn_used.at(turn, name) - 2)
                if name == "hT":
                    pe.wait_ge(turn_used.sem, turn_used.at(turn, "a1ot1"))
                elif name == "a0k":
                    pe.wait_ge(ctx_loaded.sem, ctx_loaded.at(turn, "c") * 16)
                elif name == "x4":
                    pe.wait_ge(back_rows.sem, back_rows.at(turn, name))
                else:
                    pe.wait_ge(rows_ready.sem, rows_ready.at(turn, name))
                for c in range(DC):
                    for t in range(TT):
                        ins = pe.transpose(turn_b(turn, name)[:, c * TOK + t * P:c * TOK + (t + 1) * P], src[:, t, c * P:(c + 1) * P], ident)
                ins.then_inc(turn_filled.sem, 1)

            def rows_pair(xT_, c, t):
                return xT_[:, 0, c, t * P:(t + 1) * P], xT_[:, 1, c, t * P:(t + 1) * P]

            def qkv(turn):
                pe.wait_ge(turn_used.sem, turn_used.at(turn, "xn1"))
                weights(turn, OFF_WO)
                for t in range(TT):
                    pe.wait_ge(act_used.sem, act_used.at(turn, f"v{t}") - 2)
                    split_product(act_b(turn, f"v{t}")[:, 0:DIM], [(rows_pair(xT, c, t), w_pair(OFF_QKV + c * 3 * DIM + 2 * DIM, DIM)) for c in range(DC)])\
                        .then_inc(act_filled.sem, 1)
                for m, name in enumerate(("a1q", "a1k")):
                    pe.wait_ge(turn_used.sem, turn_used.at(turn, name) - 2)
                    for o in range(DC):
                        ins = split_product(turn_b(turn, name)[:, o * TOK:(o + 1) * TOK],
                                            [(w_pair(OFF_QKV + c * 3 * DIM + m * DIM + o * P, P), (xT[:, 0, c, :], xT[:, 1, c, :])) for c in range(DC)])
                    ins.then_inc(turn_filled.sem, 1)

            def out_projection(turn):
                pe.wait_ge(turn_used.sem, turn_used.at(turn, "hT"))
                weights(turn, OFF_WR)
                for t in range(TT):
                    pe.wait_ge(dve_used.sem, dve_used.at(turn, f"wo{t}") - 3)
                    split_product(dve_b(turn, f"wo{t}")[:, 0:DIM], [(rows_pair(xT, c, t), w_pair(OFF_WO + c * DIM, DIM)) for c in range(DC)])\
                        .then_inc(dve_filled.sem, 1)

            def logits(turn, name, rows, xT_, off):
                pe.wait_ge(turn_used.sem, turn_used.at(turn, rows))
                weights(turn, OFF_E)
                pe.wait_ge(dve_used.sem, dve_used.at(turn, name) - 3)
                for t in range(TT):
                    ins = split_product(dve_b(turn, name)[:, t * EXPERTS:(t + 1) * EXPERTS],
                                        [(rows_pair(xT_, c, t), w_pair(off + c * EXPERTS, EXPERTS)) for c in range(DC)], low_low=True)
                ins.then_inc(dve_filled.sem, 1)

            def experts(turn, kind, k):
                if not turn.moe:
                    return
                if kind in ("g", "u"):
                    e, half = divmod(k, 2)
                    name = f"{kind}{k}"
                    bank, m = (act_b, 0) if kind == "g" else (dve_b, 1)
                    off = OFF_E + (3 * e + m) * E0
                    weights(turn, off + E0)
                    pe.wait_ge(bank.used.sem, bank.used.at(turn, name) - bank.depth)
                    for i in range(2):
                        n0 = (2 * half + i) * P
                        ins = split_product(bank(turn, name)[:, i * TOK:(i + 1) * TOK],
                                            [(w_pair(off + c * INTER + n0, P), (x0T[:, 0, c, :], x0T[:, 1, c, :])) for c in range(DC)])
                    ins.then_inc(bank.filled.sem, 1)
                    return
                t, off = int(kind[1]), OFF_E + (3 * k + 2) * E0
                if t == 0:
                    weights(turn, off + E0)
                    pe.wait_ge(sum_used.sem, sum_used.at(turn, f"d{k}") - 1)
                    pe.wait_ge(hid_ready.sem, hid_ready.at(turn, f"h{2 * k + 1}"))
                ins = split_product(sum_b(turn, f"d{k}")[:, t * DIM:(t + 1) * DIM],
                                    [((hT[:, 0, k % 2, i, t * P:(t + 1) * P], hT[:, 1, k % 2, i, t * P:(t + 1) * P]), w_pair(off + i * DIM, DIM))
                                     for i in range(IC)])
                if t == 1:
                    ins.then_inc(sum_filled.sem, 1)

            def fill(turn, place):
                for kind, k in pieces(place):
                    experts(turn, kind, k)

            def wkv_keys(turn, c):
                pe.wait_ge(turn_used.sem, turn_used.at(turn, f"kT{c}") - 2)
                pe.wait_ge(back_rows.sem, back_rows.at(turn, "kT"))
                for t in range(TT):
                    ins = pe.transpose(turn_b(turn, f"kT{c}")[:, t * P:(t + 1) * P], wkvs[turn.last].kx[:, t, c * P:(c + 1) * P], ident)
                ins.then_inc(turn_filled.sem, 1)

            def wkv_out_rows(turn, c):
                pe.wait_ge(dve_used.sem, dve_used.at(turn, f"yT{c}") - 3)
                pe.wait_ge(back_rows.sem, back_rows.at(turn, f"y{c}"))
                for t in range(TT):
                    ins = pe.transpose(dve_b(turn, f"yT{c}")[:, t * P:(t + 1) * P], wkvs[turn.last].y[:, t * P:(t + 1) * P], ident)
                ins.then_inc(dve_filled.sem, 1)

            def back_gate_up(turn, t, c):
                e0, n = CHUNKS1[c]
                weights(turn, W_COLS)
                for name, bank, off in ((f"mg{t}{c}", act_b, OFF_W1), (f"mu{t}{c}", dve_b, OFF_W3)):
                    pe.wait_ge(bank.used.sem, bank.used.at(turn, name) - bank.depth)
                    split_product(bank(turn, name)[:, 0:n * P], [(rows_pair(x4T, d, t), w_pair(off + d * NE1 * HID1 + e0 * P, n * P)) for d in range(DC)])\
                        .then_inc(bank.filled.sem, 1)

            def back_hidden(turn, t, c):
                e0, n = CHUNKS1[c]
                name = f"m{t}{c}"
                pe.wait_ge(turn_used.sem, turn_used.at(turn, name) - 2)
                pe.wait_ge(dve_used.sem, dve_used.at(turn, f"mu{t}{c}"))
                for i in range(n):
                    ins = pe.transpose(turn_b(turn, name)[:, i * P:(i + 1) * P], h1[:, t, (e0 + i) * P:(e0 + i + 1) * P], ident)
                ins.then_inc(turn_filled.sem, 1)

            def back_down(turn, t):
                if t == 0:
                    pe.wait_ge(sum_used.sem, sum_used.at(turn, "md") - 1)
                out = sum_b(turn, "md")[:, t * DIM:(t + 1) * DIM]
                for c, (e0, n) in enumerate(CHUNKS1):
                    pe.wait_ge(turn_used.sem, turn_used.at(turn, f"m{t}{c}"))
                    for e in range(n):
                        w_high, w_low = w_pair(OFF_W2 + (e0 + e) * DIM, DIM)
                        high, low = m16[t][c][:, 0, e, :], m16[t][c][:, 1, e, :]
                        pe.matmul(out, high, w_high, start=(e0 + e == 0), stop=False)
                        pe.matmul(out, high, w_low, start=False, stop=False)
                        ins = pe.matmul(out, low, w_high, start=False, stop=(e0 + e == NE1 - 1))
                if t == 1:
                    ins.then_inc(sum_filled.sem, 1)

            def half_attention(turn, a, half):
                if turn.att:
                    for n in (2 * half, 2 * half + 1):
                        stack_rows(turn, a, "q", n)
                        stack_rows(turn, a, "k", n)
                fill(turn, (a, half, "stacked"))
                for i in range(3):
                    if turn.att:
                        scores(turn, a, half, 2 * i)
                        scores(turn, a, half, 2 * i + 1)
                    fill(turn, (a, half, f"scores{i}"))
                    if not turn.att and turn.back and (a, half, i) == (1, 1, 2):
                        wkv_out_rows(turn, 1)
                if turn.att:
                    turn_max(turn, a, half)
                fill(turn, (a, half, "maxima"))
                if turn.back and half == 0:
                    if a == 1:
                        wkv_out_rows(turn, 0)
                    wkv_keys(turn, a)
                if turn.att:
                    exponents(turn, a, 2 * half)
                fill(turn, (a, half, "exponents"))
                if turn.att:
                    exponents(turn, a, 2 * half + 1)
                    values(turn, a, 2 * half)
                    values(turn, a, 2 * half + 1)

            def first_attention(turn, a):
                if a == 0:
                    pe.wait_ge(const_ready, 2)
                    pe.wait_ge(pick_ready, 1)
                for n in range(2):
                    stack_rows(turn, a, "q", n)
                    stack_rows(turn, a, "k", n)
                for k in range(6):
                    scores(turn, a, 0, k)
                stack_rows(turn, a, "q", 2)
                stack_rows(turn, a, "k", 2)
                turn_max(turn, a, 0)
                stack_rows(turn, a, "q", 3)
                stack_rows(turn, a, "k", 3)
                exponents(turn, a, 0)
                scores(turn, a, 1, 0)
                scores(turn, a, 1, 1)
                exponents(turn, a, 1)
                scores(turn, a, 1, 2)
                scores(turn, a, 1, 3)
                values(turn, a, 0)
                values(turn, a, 1)
                scores(turn, a, 1, 4)
                scores(turn, a, 1, 5)
                turn_max(turn, a, 1)
                exponents(turn, a, 2)
                exponents(turn, a, 3)
                values(turn, a, 2)
                values(turn, a, 3)

            def attention(turn, a):
                if turn.mode == "first":
                    first_attention(turn, a)
                else:
                    half_attention(turn, a, 0)
                    half_attention(turn, a, 1)

            def first_part(turn):
                fill(turn, "start")
                if turn.att:
                    turn_rows(turn, "a0k", ctx)
                    turn_rows(turn, "a0q", lnq)
                fill(turn, "rows")
                attention(turn, 0)
                fill(turn, "outputs")
                if turn.att:
                    outputs(turn, 0)
                fill(turn, "sum")
                if turn.att:
                    turn_rows(turn, "xn1", xn)
                fill(turn, "qkv")
                if turn.att:
                    qkv(turn)
                fill(turn, "stack")
                attention(turn, 1)
                if turn.att:
                    outputs(turn, 1)
                if turn.back and turn.att:
                    wkv_out_rows(turn, 1)
                if turn.back and not turn.att:
                    turn_rows(turn, "x4", x4n)
                fill(turn, "tail")

            def second_part(turn):
                if turn.att:
                    turn_rows(turn, "hT", att)
                fill(turn, "projection")
                if turn.att:
                    out_projection(turn)
                if turn.back:
                    turn_rows(turn, "x4", x4n)
                    logits(turn, "gl", "x4", x4T, OFF_GW)
                    for c in range(3):
                        back_gate_up(turn, 0, c)
                if turn.att:
                    turn_rows(turn, "xn2", xn)
                if turn.back:
                    back_gate_up(turn, 1, 0)
                if turn.att:
                    logits(turn, "lg", "xn2", x0T, OFF_WR)
                if turn.back:
                    back_hidden(turn, 0, 0)
                    back_hidden(turn, 0, 1)
                    back_gate_up(turn, 1, 1)
                    back_hidden(turn, 0, 2)
                    back_gate_up(turn, 1, 2)
                    back_hidden(turn, 1, 0)
                    back_down(turn, 0)
                    back_hidden(turn, 1, 1)
                    back_hidden(turn, 1, 2)
                    back_down(turn, 1)

            pe.wait_ge(const_ready, 1)
            pe.wait_ge(cleared, 3)
            for mode in ("first", "second"):
                first_part(Turn(mode))
                second_part(Turn(mode))
            with pe.Fori(0, LOOPS) as j:
                first_part(Turn("loop", j))
                second_part(Turn("loop", j))
            end, last = Turn("end"), Turn("end", last=True)
            first_part(end)
            fill(end, "projection")
            logits(end, "gl", "x4", x4T, OFF_GW)
            back_gate_up(end, 0, 0)
            back_gate_up(end, 0, 1)
            wkv_keys(last, 0)
            back_gate_up(end, 0, 2)
            back_gate_up(end, 1, 0)
            back_hidden(end, 0, 0)
            back_hidden(end, 0, 1)
            back_gate_up(end, 1, 1)
            wkv_out_rows(last, 0)
            wkv_keys(last, 1)
            back_hidden(end, 0, 2)
            back_gate_up(end, 1, 2)
            back_hidden(end, 1, 0)
            back_down(end, 0)
            back_hidden(end, 1, 1)
            back_hidden(end, 1, 2)
            wkv_out_rows(last, 1)
            back_down(end, 1)
            second_part(last)


def _consts():
    import numpy as np
    c = np.zeros((P, C_COLS), np.float32)
    c[:, C_ID:C_ID + P] = np.eye(P)
    c[:, C_TRIQ:C_TRIQ + P] = np.triu(np.ones((P, P)), 1)
    c[:, C_TRIK:C_TRIK + P] = np.tril(np.ones((P, P)), -1)
    m = np.arange(P)
    part = (m // HD) % 4
    for k, takes in enumerate((part % 2 == 0, part % 2 == 1, part < 2, part >= 2)):
        for pair in range(4):
            s = c[:, C_SEL + (4 * k + pair) * P:C_SEL + (4 * k + pair + 1) * P]
            s[(2 * pair + m // 64) * HD + m % HD, m] = takes
    c[:, C_COL + COL_IOTA:C_COL + COL_IOTA + 8] = np.arange(8)
    c[:, C_COL + COL_HALF:C_COL + COL_HALF + 4] = -0.5
    c[8:, C_COL + COL_REST] = 1
    return c


def kernel(**inputs):
    import numpy as np
    import concourse.bacc as bacc
    from concourse.bass_utils import run_bass_kernel_spmd

    v = {k: np.asarray(a) for k, a in inputs.items()}

    def chunked(a):
        return a.reshape(a.shape[0] // P, P, -1).transpose(1, 0, 2).reshape(P, -1)

    parts = [chunked(np.concatenate([v["L0_ffn_" + n].T for n in ("Wq", "Wk", "Wv")], axis=1)),
             chunked(v["L0_ffn_Wo"].T), chunked(v["L0_ffn_Wr"].T), chunked(v["L1_ffn_gate_w"].T)]
    for e in range(EXPERTS):
        parts += [chunked(v["L0_ffn_Wg"][e].T), chunked(v["L0_ffn_Wu"][e].T), chunked(v["L0_ffn_Wd"][e].T)]
    for n, m in (("w1", "ws1"), ("w3", "ws3")):
        a = np.concatenate([v["L1_ffn_" + n], v["L1_ffn_" + m][None]], axis=0)
        parts.append(chunked(a.transpose(2, 0, 1).reshape(DIM, -1)))
    a = np.concatenate([v["L1_ffn_w2"], v["L1_ffn_ws2"][None]], axis=0)
    parts.append(a.transpose(2, 0, 1).reshape(P, -1))
    const = _consts()
    for k, n in ((COL_LN1, "L0_ffn_w_ln1"), (COL_LN2, "L0_ffn_w_ln2"), (COL_W, "L1_xattn_w"), (COL_U, "L1_xattn_u")):
        const[:, C_COL + k:C_COL + k + DC] = v[n].reshape(DC, P).T
    arrays = {
        "x": v["x"], "ctx": v["ctx_2048"], "ctx_t": np.ascontiguousarray(v["ctx_2048"].transpose(0, 2, 1)),
        "weights": np.ascontiguousarray(np.concatenate(parts, axis=1)), "const": const,
    }
    nc = bacc.Bacc("TRN2", target_bir_lowering=False, num_devices=1)
    args = [nc.dram_tensor("in_" + k, a.shape, mybir.dt.from_np(a.dtype), kind="ExternalInput").ap() for k, a in arrays.items()]
    out = nc.dram_tensor("out", (BATCH, TOK, DIM), F32, kind="ExternalOutput").ap()
    kernel_body(nc, *args, out)
    r = run_bass_kernel_spmd(nc, [{"in_" + k: a for k, a in arrays.items()}], core_ids=[0])
    return r.results[0]["out"]
```
